# Optimizing a Trainium2 kernel written in Bass

```python
import numpy as np
import jax
import jax.numpy as jnp

def _softmax(x, axis=-1):
    return jax.nn.softmax(x, axis=axis)

def _gelu(x):
    return jax.nn.gelu(x, approximate=True)

def _silu(x):
    return jax.nn.silu(x)

def _sigmoid(x):
    return jax.nn.sigmoid(x)

def _layernorm(x, axis=-1, eps=1e-05):
    m = jnp.mean(x, axis=axis, keepdims=True)
    v = jnp.var(x, axis=axis, keepdims=True)
    return (x - m) / jnp.sqrt(v + eps)

def _scatter_add(tgt, idx, src, axis=0):
    return tgt.at[idx].add(src)

def _segment_sum(src, seg, n):
    return jax.ops.segment_sum(src, seg, n)
kernel_name = 'mk_hybrid_d1_jaxref_r8_1d917c'

def setup_inputs(seed: int=0):
    np.random.seed(seed)
    _w = jnp.asarray

    def _L0_attn_a_setup():
        import jax, jax.numpy as jnp
        import numpy as np
        B, L, H = (2, 256, 128)
        NH, DK, DV = (4, 32, 32)
        CONV_K, FIR_S, FIR_L = (4, 3, 63)
        GATE_IN = H + 4 * 2 * NH
        MLP_H = 2 * H
        CHUNK = 32

        def l2norm(x):
            return x * jax.lax.rsqrt(jnp.sum(x * x, -1, keepdims=True) + 1e-06)

        def causal_dwconv(x, w):
            k = w.shape[-1]
            xc = jnp.pad(jnp.transpose(x, (0, 2, 1)), ((0, 0), (0, 0), (k - 1, 0)))
            y = jax.lax.conv_general_dilated(xc, w[:, None, :], (1,), 'VALID', feature_group_count=w.shape[0], dimension_numbers=('NCH', 'OIH', 'NCH'))
            return jnp.transpose(y, (0, 2, 1))

        def delta_rule_chunkwise(q, k, v, beta, chunk=CHUNK):
            b, h, Lp, dk = q.shape
            dv = v.shape[-1]
            n = Lp // chunk
            q = l2norm(q)
            k = l2norm(k)
            v = v * beta[..., None]
            kb = k * beta[..., None]
            qc, kc, vc, kbc = (t.reshape(b, h, n, chunk, -1) for t in (q, k, v, kb))
            A = jnp.tril(jnp.einsum('bhnid,bhnjd->bhnij', kbc, kc), -1)
            T = jnp.linalg.inv(jnp.eye(chunk, dtype=q.dtype) + A)
            u = T @ vc
            w = T @ kbc

            def step(S, inp):
                qi, ki, ui, wi = inp
                attn = jnp.tril(qi @ jnp.swapaxes(ki, -1, -2))
                u2 = ui - wi @ S
                oi = qi @ S + attn @ u2
                return (S + jnp.swapaxes(ki, -1, -2) @ u2, oi)
            S0 = jnp.zeros((b, h, dk, dv), q.dtype)
            xs = tuple((jnp.moveaxis(t, 2, 0) for t in (qc, kc, u, w)))
            S, o = jax.lax.scan(step, S0, xs)
            o = jnp.moveaxis(o, 0, 2).reshape(b, h, Lp, dv)
            return (o, S)

        def branch_stats(x):
            m = x.mean(-1)
            s = jnp.sqrt(jnp.maximum(x.var(-1), 1e-06))
            return jnp.concatenate([m, s], -1)
        key = jax.random.key(seed)
        ks = jax.random.split(key, 16)
        f32 = jnp.float32

        def dirac(k_, shape):
            f = 0.01 * jax.random.normal(k_, shape, f32)
            return f.at[..., shape[-1] // 2].add(1.0)
        b2 = jnp.zeros((NH * 4,), f32).at[jnp.arange(NH) * 4 + 3].set(2.0)
        return {'hidden_states': jax.random.normal(ks[0], (B, L, H), f32), 'Wq': 0.02 * jax.random.normal(ks[1], (H, NH * DK), f32), 'Wk': 0.02 * jax.random.normal(ks[2], (H, NH * DK), f32), 'Wv': 0.02 * jax.random.normal(ks[3], (H, NH * DV), f32), 'Wb': 0.02 * jax.random.normal(ks[4], (H, NH), f32), 'conv_q_w': 0.2 * jax.random.normal(ks[5], (NH * DK, CONV_K), f32), 'conv_k_w': 0.2 * jax.random.normal(ks[6], (NH * DK, CONV_K), f32), 'conv_v_w': 0.2 * jax.random.normal(ks[7], (NH * DV, CONV_K), f32), 'fir_short_w': dirac(ks[8], (NH, DV, FIR_S)), 'fir_long_w': dirac(ks[9], (NH, DV, FIR_L)), 'mlp_w1': 0.02 * jax.random.normal(ks[10], (GATE_IN, MLP_H), f32), 'mlp_b1': jnp.zeros((MLP_H,), f32), 'mlp_w2': 0.02 * jax.random.normal(ks[11], (MLP_H, NH * 4), f32), 'mlp_b2': b2, 'gate_log_temp': jnp.full((NH,), np.log(1.2), f32), 'o_norm_w': jnp.ones((DV,), f32), 'Wo': 0.02 * jax.random.normal(ks[12], (NH * DV, H), f32)}
    _L0_attn_a_in = _L0_attn_a_setup()

    def _L0_attn_b_setup():
        import jax, jax.numpy as jnp
        import numpy as np
        N_HEADS = 16
        HEAD_DIM = 64
        ROPE_THETA = 10000.0
        EPS = 1e-06

        def _rmsnorm(x, w):
            rms = jnp.sqrt(jnp.mean(jnp.square(x), axis=-1, keepdims=True) + EPS)
            return x / rms * w

        def _rope(x, cos, sin):
            x1, x2 = jnp.split(x, 2, axis=-1)
            return jnp.concatenate([x1 * cos - x2 * sin, x1 * sin + x2 * cos], axis=-1)
        key = jax.random.key(seed)
        ks = jax.random.split(key, 3)
        B, T, C = (2, 256, 128)
        x = jax.random.normal(ks[0], (B, T, C), dtype=jnp.float32)
        wqkv = jax.random.normal(ks[1], (3 * N_HEADS * HEAD_DIM, C), dtype=jnp.float32) * C ** (-0.5)
        wo = jax.random.normal(ks[2], (C, N_HEADS * HEAD_DIM), dtype=jnp.float32) * (N_HEADS * HEAD_DIM) ** (-0.5)
        q_norm_w = jnp.ones((HEAD_DIM,), dtype=jnp.float32)
        k_norm_w = jnp.ones((HEAD_DIM,), dtype=jnp.float32)
        return {'x': x, 'wqkv': wqkv, 'wo': wo, 'q_norm_w': q_norm_w, 'k_norm_w': k_norm_w}
    _L0_attn_b_in = _L0_attn_b_setup()

    def _L0_ffn_setup():
        import jax, jax.numpy as jnp
        import numpy as np
        B, S, K, N = (8, 1024, 128, 128)
        key = jax.random.key(seed)
        k1, k2, k3, k4 = jax.random.split(key, 4)
        x = jax.random.normal(k1, (B, S, K), dtype=jnp.float32)
        CB = jnp.clip(jnp.round(jax.random.normal(k2, (N, K), dtype=jnp.float32) * 42.0), -127.0, 127.0)
        SCB = jax.random.uniform(k3, (N,), dtype=jnp.float32, minval=0.5, maxval=2.0)
        bias = jax.random.normal(k4, (N,), dtype=jnp.float32) * 0.02
        return {'x': x, 'CB': CB, 'SCB': SCB, 'bias': bias}
    _L0_ffn_in = _L0_ffn_setup()
    _d = {'L0_attn_a_hidden_states': _L0_attn_a_in['hidden_states'], 'L0_attn_a_Wq': _L0_attn_a_in['Wq'], 'L0_attn_a_Wk': _L0_attn_a_in['Wk'], 'L0_attn_a_Wv': _L0_attn_a_in['Wv'], 'L0_attn_a_Wb': _L0_attn_a_in['Wb'], 'L0_attn_a_conv_q_w': _L0_attn_a_in['conv_q_w'], 'L0_attn_a_conv_k_w': _L0_attn_a_in['conv_k_w'], 'L0_attn_a_conv_v_w': _L0_attn_a_in['conv_v_w'], 'L0_attn_a_fir_short_w': _L0_attn_a_in['fir_short_w'], 'L0_attn_a_fir_long_w': _L0_attn_a_in['fir_long_w'], 'L0_attn_a_mlp_w1': _L0_attn_a_in['mlp_w1'], 'L0_attn_a_mlp_b1': _L0_attn_a_in['mlp_b1'], 'L0_attn_a_mlp_w2': _L0_attn_a_in['mlp_w2'], 'L0_attn_a_mlp_b2': _L0_attn_a_in['mlp_b2'], 'L0_attn_a_gate_log_temp': _L0_attn_a_in['gate_log_temp'], 'L0_attn_a_o_norm_w': _L0_attn_a_in['o_norm_w'], 'L0_attn_a_Wo': _L0_attn_a_in['Wo'], 'L0_attn_b_wqkv': _L0_attn_b_in['wqkv'], 'L0_attn_b_wo': _L0_attn_b_in['wo'], 'L0_attn_b_q_norm_w': _L0_attn_b_in['q_norm_w'], 'L0_attn_b_k_norm_w': _L0_attn_b_in['k_norm_w'], 'L0_ffn_CB': _L0_ffn_in['CB'], 'L0_ffn_SCB': _L0_ffn_in['SCB'], 'L0_ffn_bias': _L0_ffn_in['bias']}
    _x0 = _d['L0_attn_a_hidden_states']
    _d['L0_attn_a_hidden_states'] = jax.random.normal(jax.random.fold_in(jax.random.key(seed), 1), (8, 512, 128), dtype=_x0.dtype)
    del _x0
    return _d

def reference(L0_attn_a_hidden_states, L0_attn_a_Wq, L0_attn_a_Wk, L0_attn_a_Wv, L0_attn_a_Wb, L0_attn_a_conv_q_w, L0_attn_a_conv_k_w, L0_attn_a_conv_v_w, L0_attn_a_fir_short_w, L0_attn_a_fir_long_w, L0_attn_a_mlp_w1, L0_attn_a_mlp_b1, L0_attn_a_mlp_w2, L0_attn_a_mlp_b2, L0_attn_a_gate_log_temp, L0_attn_a_o_norm_w, L0_attn_a_Wo, L0_attn_b_wqkv, L0_attn_b_wo, L0_attn_b_q_norm_w, L0_attn_b_k_norm_w, L0_ffn_CB, L0_ffn_SCB, L0_ffn_bias):

    def _L0_attn_a_ref(hidden_states, Wq, Wk, Wv, Wb, conv_q_w, conv_k_w, conv_v_w, fir_short_w, fir_long_w, mlp_w1, mlp_b1, mlp_w2, mlp_b2, gate_log_temp, o_norm_w, Wo):
        import jax, jax.numpy as jnp
        import numpy as np
        B, L, H = (2, 256, 128)
        NH, DK, DV = (4, 32, 32)
        CONV_K, FIR_S, FIR_L = (4, 3, 63)
        GATE_IN = H + 4 * 2 * NH
        MLP_H = 2 * H
        CHUNK = 32

        def l2norm(x):
            return x * jax.lax.rsqrt(jnp.sum(x * x, -1, keepdims=True) + 1e-06)

        def causal_dwconv(x, w):
            k = w.shape[-1]
            xc = jnp.pad(jnp.transpose(x, (0, 2, 1)), ((0, 0), (0, 0), (k - 1, 0)))
            y = jax.lax.conv_general_dilated(xc, w[:, None, :], (1,), 'VALID', feature_group_count=w.shape[0], dimension_numbers=('NCH', 'OIH', 'NCH'))
            return jnp.transpose(y, (0, 2, 1))

        def delta_rule_chunkwise(q, k, v, beta, chunk=CHUNK):
            b, h, Lp, dk = q.shape
            dv = v.shape[-1]
            n = Lp // chunk
            q = l2norm(q)
            k = l2norm(k)
            v = v * beta[..., None]
            kb = k * beta[..., None]
            qc, kc, vc, kbc = (t.reshape(b, h, n, chunk, -1) for t in (q, k, v, kb))
            A = jnp.tril(jnp.einsum('bhnid,bhnjd->bhnij', kbc, kc), -1)
            T = jnp.linalg.inv(jnp.eye(chunk, dtype=q.dtype) + A)
            u = T @ vc
            w = T @ kbc

            def step(S, inp):
                qi, ki, ui, wi = inp
                attn = jnp.tril(qi @ jnp.swapaxes(ki, -1, -2))
                u2 = ui - wi @ S
                oi = qi @ S + attn @ u2
                return (S + jnp.swapaxes(ki, -1, -2) @ u2, oi)
            S0 = jnp.zeros((b, h, dk, dv), q.dtype)
            xs = tuple((jnp.moveaxis(t, 2, 0) for t in (qc, kc, u, w)))
            S, o = jax.lax.scan(step, S0, xs)
            o = jnp.moveaxis(o, 0, 2).reshape(b, h, Lp, dv)
            return (o, S)

        def branch_stats(x):
            m = x.mean(-1)
            s = jnp.sqrt(jnp.maximum(x.var(-1), 1e-06))
            return jnp.concatenate([m, s], -1)
        x = hidden_states
        b, l, _ = x.shape
        q = jax.nn.silu(causal_dwconv(x @ Wq, conv_q_w)).reshape(b, l, NH, DK)
        k = jax.nn.silu(causal_dwconv(x @ Wk, conv_k_w)).reshape(b, l, NH, DK)
        v = jax.nn.silu(causal_dwconv(x @ Wv, conv_v_w)).reshape(b, l, NH, DV)
        beta = jax.nn.sigmoid(x @ Wb)
        delta_out, _S = delta_rule_chunkwise(jnp.transpose(q, (0, 2, 1, 3)), jnp.transpose(k, (0, 2, 1, 3)), jnp.transpose(v, (0, 2, 1, 3)), jnp.transpose(beta, (0, 2, 1)))
        delta_out = jnp.transpose(delta_out, (0, 2, 1, 3))
        vf = v.reshape(b, l, NH * DV)
        fir_short = causal_dwconv(vf, fir_short_w.reshape(NH * DV, FIR_S)).reshape(b, l, NH, DV)
        fir_long = causal_dwconv(vf, fir_long_w.reshape(NH * DV, FIR_L)).reshape(b, l, NH, DV)
        gate_in = jnp.concatenate([x, branch_stats(fir_short), branch_stats(fir_long), branch_stats(delta_out), branch_stats(v)], -1)
        logits = jax.nn.gelu(gate_in @ mlp_w1 + mlp_b1, approximate=False) @ mlp_w2 + mlp_b2
        temp = jax.nn.softplus(gate_log_temp) + 0.0001
        logits = logits.reshape(b, l, NH, 4) / temp[None, None, :, None]
        w = jax.nn.softmax(logits, -1)
        o = w[..., 0:1] * fir_short + w[..., 1:2] * fir_long + w[..., 2:3] * delta_out + w[..., 3:4] * v
        o = o * jax.lax.rsqrt(jnp.mean(o * o, -1, keepdims=True) + 1e-05) * o_norm_w
        return o.reshape(b, l, NH * DV) @ Wo

    def _L0_attn_b_ref(x, wqkv, wo, q_norm_w, k_norm_w):
        import jax, jax.numpy as jnp
        import numpy as np
        N_HEADS = 16
        HEAD_DIM = 64
        ROPE_THETA = 10000.0
        EPS = 1e-06

        def _rmsnorm(x, w):
            rms = jnp.sqrt(jnp.mean(jnp.square(x), axis=-1, keepdims=True) + EPS)
            return x / rms * w

        def _rope(x, cos, sin):
            x1, x2 = jnp.split(x, 2, axis=-1)
            return jnp.concatenate([x1 * cos - x2 * sin, x1 * sin + x2 * cos], axis=-1)
        B, T, C = x.shape
        H, D = (N_HEADS, HEAD_DIM)
        qkv = jnp.einsum('btc,oc->bto', x, wqkv)
        q, k, v = jnp.split(qkv, 3, axis=-1)

        def to_heads(t):
            return t.reshape(B, T, H, D).transpose(0, 2, 1, 3)
        q, k, v = (to_heads(q), to_heads(k), to_heads(v))
        q = _rmsnorm(q, q_norm_w)
        k = _rmsnorm(k, k_norm_w)
        inv_freq = 1.0 / ROPE_THETA ** (jnp.arange(0, D, 2, dtype=jnp.float32) / D)
        freqs = jnp.arange(T, dtype=jnp.float32)[:, None] * inv_freq
        cos, sin = (jnp.cos(freqs), jnp.sin(freqs))
        q = _rope(q, cos, sin)
        k = _rope(k, cos, sin)
        scale = D ** (-0.5)
        attn = jnp.einsum('bhtd,bhsd->bhts', q, k) * scale
        causal = jnp.tril(jnp.ones((T, T), dtype=bool))
        attn = jnp.where(causal, attn, -jnp.inf)
        attn = jax.nn.softmax(attn.astype(jnp.float32), axis=-1).astype(q.dtype)
        out = jnp.einsum('bhts,bhsd->bhtd', attn, v)
        out = out.transpose(0, 2, 1, 3).reshape(B, T, H * D)
        return jnp.einsum('bte,ce->btc', out, wo)

    def _L0_ffn_ref(x, CB, SCB, bias):
        import jax, jax.numpy as jnp
        import numpy as np
        B, S, K, N = (8, 1024, 128, 128)
        out = jnp.einsum('bsk,nk->bsn', x, CB)
        out = out * (SCB * (1.0 / 127.0)) + bias
        return out
    x = L0_attn_a_hidden_states
    x = x + _L0_attn_a_ref(_layernorm(x, axis=-1), L0_attn_a_Wq, L0_attn_a_Wk, L0_attn_a_Wv, L0_attn_a_Wb, L0_attn_a_conv_q_w, L0_attn_a_conv_k_w, L0_attn_a_conv_v_w, L0_attn_a_fir_short_w, L0_attn_a_fir_long_w, L0_attn_a_mlp_w1, L0_attn_a_mlp_b1, L0_attn_a_mlp_w2, L0_attn_a_mlp_b2, L0_attn_a_gate_log_temp, L0_attn_a_o_norm_w, L0_attn_a_Wo)
    x = x + _L0_ffn_ref(_layernorm(x, axis=-1), L0_ffn_CB, L0_ffn_SCB, L0_ffn_bias)
    x = x + _L0_attn_b_ref(_layernorm(x, axis=-1), L0_attn_b_wqkv, L0_attn_b_wo, L0_attn_b_q_norm_w, L0_attn_b_k_norm_w)
    x = x + _L0_ffn_ref(_layernorm(x, axis=-1), L0_ffn_CB, L0_ffn_SCB, L0_ffn_bias)
    return x

_drawn_inputs = setup_inputs


def setup_inputs(seed=0):
    import zlib

    import numpy as np

    out = dict(_drawn_inputs(seed))
    spreads = {'L0_attn_a_mlp_b1': (0.0, 0.8),
     'L0_attn_a_gate_log_temp': (0.18232156336307526, 0.6),
     'L0_attn_a_o_norm_w': (1.0, 0.2),
     'L0_attn_b_q_norm_w': (1.0, 0.6),
     'L0_attn_b_k_norm_w': (1.0, 0.6)}
    factors = {'L0_attn_a_Wq': 5.205,
     'L0_attn_a_Wk': 5.196,
     'L0_attn_a_Wb': 8.0,
     'L0_attn_a_conv_q_w': 5.284,
     'L0_attn_a_conv_k_w': 5.124,
     'L0_attn_a_fir_short_w': 8.0,
     'L0_attn_a_fir_long_w': 3.059,
     'L0_attn_a_mlp_w1': 8.0,
     'L0_attn_a_mlp_w2': 8.0,
     'L0_ffn_bias': 8.0}
    for name, (base, spread) in spreads.items():
        noise = np.random.default_rng([zlib.crc32(name.encode()), seed]).standard_normal(out[name].shape)
        drawn = base * np.exp(spread * noise) if base else spread * noise
        out[name] = jnp.asarray(drawn.astype(out[name].dtype))
    for name, factor in factors.items():
        out[name] = (out[name] * factor).astype(out[name].dtype)
    return out
```

```python
from contextlib import ExitStack

import numpy as np

import concourse.bass as bass
from concourse import mybir

F32 = mybir.dt.float32
F16 = mybir.dt.float16
BF16 = mybir.dt.bfloat16
ALU = mybir.AluOpType
ACT = mybir.ActivationFunctionType
AX = mybir.AxisListType

P = 128
B, L, H = 8, 512, 128
TILES = B * L // P
NH, DK = 4, 32
CH = 32
PAIR = 2
PT = PAIR * L // P
PTOK = PAIR * L
PC = PTOK // CH
ROUNDS = B // PAIR
STEPS = L // CH
CONV = 4
FS, FL = 3, 63
EPS_LN = 1e-5


class Signal:

    def __init__(self, sem, per):
        self.sem, self.per = sem, per

    def at(self, it, k=None):
        return it * self.per + (self.per if k is None else k)


class Chain:

    def __init__(self, sem, per):
        self.sem, self.per, self.k = sem, per, 0

    def next(self):
        self.k += 1
        return self.k



def delta_phase(nc, d, keep):
    with ExitStack() as ctx:
        def sb(name, shape, dt=F32):
            return ctx.enter_context(nc.sbuf_tensor(name, shape, dt))

        def signal(name, per):
            return Signal(ctx.enter_context(nc.semaphore(name)), per)

        x_in = sb("x_in", [P, PT, H])
        stats = sb("stats", [P, PT, 6])
        mv = sb("mv", [P, PT, 2])
        rstd = sb("rstd", [P, PT])
        xn = sb("xn", [P, PT, H])
        xT = sb("xT", [H, PTOK])
        pre = [sb(f"pre_{n}", [H, PAIR, CONV - 1 + L]) for n in "qkv"]
        con = [sb(f"con_{n}", [H, PAIR, L]) for n in "qkv"]
        vpad = sb("vpad", [H, PAIR, FS - 1 + L])
        fir = sb("fir", [H, PAIR, L])
        sq = sb("sq", [H, 2, PTOK])
        kT = sb("kT", [H, PTOK])
        beta = sb("beta", [P, PT, NH])
        VK = sb("VK", [P, PT, NH, 2, DK])
        M = sb("M", [P, PT, NH, CH])
        A = sb("A", [P, CH, CH])
        X = sb("X", [P, CH, CH])
        tmp = sb("tmp", [P, CH * CH])
        TT = sb("TT", [P, PT * NH, P])
        UW = sb("UW", [P, PT, 2, NH * DK])
        uT = sb("uT", [H, PTOK])
        WQ = sb("WQ", [H, PC, 2, CH])
        kx = sb("kx", [P, PC, NH * DK])
        Sx = sb("Sx", [P, PAIR, NH * DK])
        u2T = sb("u2T", [H, PTOK])
        qsT = sb("qsT", [H, PTOK])
        u2h = sb("u2h", [P, PAIR, DK])
        u2tok = xn
        AT = sb("AT", [P, 4, NH, P])
        qstok = x_in
        zero = sb("zero", [P, PAIR * DK])
        ps01 = ctx.enter_context(nc.psum_tensor("ps01", [P, 2, 512], F32))
        ps23 = ctx.enter_context(nc.psum_tensor("ps23", [P, 2, 512], F32))
        ps47 = ctx.enter_context(nc.psum_tensor("ps47", [P, 4, 512], F32))
        wqkv, wb, cw, fsw, ident, blk, causal = (keep[n] for n in ("wqkv", "wb", "cw", "fsw", "ident", "blk", "causal"))
        v_tok, d_tok, fs_tok = keep["v_tok"], keep["d_tok"], keep["fs_tok"]

        x_loaded = signal("x_loaded", 16)
        cleared = signal("cleared", 6)
        dv = Chain(ctx.enter_context(nc.semaphore("dve_step")), 98)
        ac = Chain(ctx.enter_context(nc.semaphore("act_step")), 90)
        std_ready = signal("std_ready", 1)
        xn_std = signal("xn_std", 1)
        xn_ready = signal("xn_ready", 1)
        xT_ps = signal("xT_ps", 1)
        xT_ready = signal("xT_ready", 1)
        proj_ps = signal("proj_ps", 3)
        pre_ready = signal("pre_ready", 3)
        beta_ps = signal("beta_ps", 1)
        beta_ready = signal("beta_ready", 1)
        con_ready = signal("con_ready", 3)
        silu_ready = signal("silu_ready", 3)
        sq_ready = signal("sq_ready", 2)
        ss_ps = signal("ss_ps", 2)
        norm_ready = signal("norm_ready", 2)
        qk_ready = signal("qk_ready", 2)
        fir_ready = signal("fir_ready", 1)
        tok_ps = signal("tok_ps", 3)
        tok_out = signal("tok_out", 3)
        kk_ps = signal("kk_ps", 2)
        kk_used = signal("kk_used", 2)
        TT_ready = signal("TT_ready", 1)
        kx_ready = signal("kx_ready", 1)
        UW_ps = signal("UW_ps", 2)
        UW_ready = signal("UW_ready", 4)
        UWT_ps = signal("UWT_ps", 2)
        UWT_ready = signal("UWT_ready", 2)
        WS_ps = signal("WS_ps", STEPS)
        u2_ready = signal("u2_ready", STEPS)
        qs_ready = signal("qs_ready", STEPS)
        S_ps = signal("S_ps", STEPS)
        S_ready = signal("S_ready", STEPS)
        S_zero = signal("S_zero", 1)
        u2t_ps = signal("u2t_ps", 1)
        u2t_ready = signal("u2t_ready", 1)
        qst_ps = signal("qst_ps", 1)
        qst_ready = signal("qst_ready", 1)
        qk_ps = signal("qk_ps", 2)
        AT_ready = signal("AT_ready", 2)
        o_ps = signal("o_ps", 2)
        o_ready = signal("o_ready", 1)
        everything = [x_loaded, std_ready, xn_ready, xT_ready, pre_ready, beta_ready, con_ready, silu_ready,
                      qk_ready, fir_ready, tok_out, kk_used, TT_ready, kx_ready, UW_ready, UWT_ready,
                      u2_ready, qs_ready, S_ready, u2t_ready, qst_ready, AT_ready, o_ready, o_ps]

        block = ctx.enter_context(nc.Block())

        def round_over(eng, it):
            for s in everything:
                eng.wait_ge(s.sem, s.at(it))

        @block.gpsimd
        def _(pool):
            for t in (*pre, vpad):
                nc.gpsimd.memset(t[:, :, 0:CONV - 1 if t is not vpad else FS - 1], 0.0).then_inc(cleared.sem, 1)
            nc.gpsimd.memset(TT[:], 0.0).then_inc(cleared.sem, 1)
            nc.gpsimd.memset(kx[:], 0.0).then_inc(cleared.sem, 1)
            pool.wait_ge(cleared.sem, 6)
            nc.gpsimd.memset(zero[:], 0.0).then_inc(cleared.sem, 1)
            with pool.Fori(0, ROUNDS) as it:
                nc.gpsimd.memset(Sx[:], 0.0).then_inc(S_zero.sem, 1)
                round_over(pool, it)

        @block.scalar
        def _(act):
            act.wait_ge(cleared.sem, 7)

            def chain(ins, it):
                k = ac.next()
                ins.then_inc(ac.sem, 1)
                act.wait_ge(ac.sem, it * ac.per + k)

            with act.Fori(0, ROUNDS) as it:
                act.dma_start(x_in[:], d["x"][:, bass.ds(it * PT, PT), :]).then_inc(x_loaded.sem, 16)
                act.wait_ge(std_ready.sem, std_ready.at(it))
                nc.scalar.activation(rstd[:], rstd[:], ACT.Sqrt).then_inc(xn_std.sem, 1)
                act.wait_ge(xT_ps.sem, xT_ps.at(it))
                nc.scalar.activation(xT[:], ps01[:].rearrange("p a b -> p (a b)"), ACT.Copy).then_inc(xT_ready.sem, 1)
                for i, ps in enumerate((ps23, ps47[:, 0:2], ps47[:, 2:4])):
                    act.wait_ge(proj_ps.sem, proj_ps.at(it, i + 1))
                    nc.scalar.activation(pre[i][:, :, CONV - 1:], ps[:] if i == 0 else ps, ACT.Copy).then_inc(pre_ready.sem, 1)
                act.wait_ge(beta_ps.sem, beta_ps.at(it))
                nc.scalar.activation(beta[:].rearrange("p a b -> p (a b)"), ps01[:, 0, 0:PT * NH], ACT.Sigmoid).then_inc(beta_ready.sem, 1)
                for i in range(3):
                    act.wait_ge(con_ready.sem, con_ready.at(it, i + 1))
                    dst = vpad[:, :, FS - 1:] if i == 2 else con[i][:]
                    nc.scalar.activation(dst, con[i][:], ACT.Silu).then_inc(silu_ready.sem, 1)
                    if i < 2:
                        act.wait_ge(silu_ready.sem, silu_ready.at(it, i + 1))
                        nc.scalar.activation(sq[:, i, :], con[i][:].rearrange("p a b -> p (a b)"), ACT.Square).then_inc(sq_ready.sem, 1)
                for i, ps in enumerate((ps23, ps01)):
                    act.wait_ge(ss_ps.sem, ss_ps.at(it, i + 1))
                    nc.scalar.activation(sq[:, i, :], ps[:].rearrange("p a b -> p (a b)"), ACT.Sqrt, bias=keep["eps6"][:, 0:1]).then_inc(norm_ready.sem, 1)
                act.wait_ge(tok_ps.sem, tok_ps.at(it, 1))
                nc.scalar.activation(v_tok[:, bass.ds(it * PT, PT), :], ps23[:].rearrange("p a (b c) -> p (a b) c", c=H), ACT.Copy).then_inc(tok_out.sem, 1)
                act.wait_ge(tok_ps.sem, tok_ps.at(it, 3))
                nc.scalar.activation(fs_tok[:, bass.ds(it * PT, PT), :], ps23[:].rearrange("p a (b c) -> p (a b) c", c=H), ACT.Copy).then_inc(tok_out.sem, 1)
                for hf in range(2):
                    act.wait_ge(UW_ps.sem, UW_ps.at(it, hf + 1))
                    for w in range(2):
                        nc.scalar.activation(
                            UW[:, 4 * hf:4 * hf + 4, w, :].rearrange("p t (h c) -> p t h c", h=NH),
                            ps47[:, 2 * hf:2 * hf + 2].rearrange("p a (t h w c) -> p (a t) h w c", h=NH, w=2, c=DK)[:, :, :, w, :],
                            ACT.Copy).then_inc(UW_ready.sem, 1)
                act.wait_ge(UWT_ps.sem, UWT_ps.at(it, 1))
                nc.scalar.activation(uT[:], ps01[:].rearrange("p a b -> p (a b)"), ACT.Copy).then_inc(UWT_ready.sem, 1)
                act.wait_ge(UWT_ps.sem, UWT_ps.at(it, 2))
                nc.scalar.activation(WQ[:, :, 0, :], ps23[:].rearrange("p a (x c) -> p (a x) c", c=CH), ACT.Copy).then_inc(UWT_ready.sem, 1)
                for n in range(STEPS):
                    act.wait_ge(u2_ready.sem, u2_ready.at(it, n + 1))
                    nc.scalar.activation(
                        qsT[:].rearrange("p (s x) -> p s x", s=PAIR)[:, :, n * CH:(n + 1) * CH],
                        ps01[:, n % 2, 0:PAIR * 64].rearrange("p (s x) -> p s x", s=PAIR)[:, :, 32:64], ACT.Copy).then_inc(qs_ready.sem, 1)
                act.wait_ge(u2t_ps.sem, u2t_ps.at(it))
                nc.scalar.activation(u2tok[:].rearrange("p a b -> p (a b)"), ps01[:].rearrange("p a b -> p (a b)"), ACT.Copy).then_inc(u2t_ready.sem, 1)
                act.wait_ge(qst_ps.sem, qst_ps.at(it))
                nc.scalar.activation(qstok[:].rearrange("p a b -> p (a b)"), ps23[:].rearrange("p a b -> p (a b)"), ACT.Copy).then_inc(qst_ready.sem, 1)
                round_over(act, it)

        @block.vector
        def _(dve):
            dve.wait_ge(cleared.sem, 7)

            def chain(ins, it):
                k = dv.next()
                ins.then_inc(dv.sem, 1)
                dve.wait_ge(dv.sem, it * dv.per + k)

            with dve.Fori(0, ROUNDS) as it:
                dve.wait_ge(x_loaded.sem, x_loaded.at(it))
                for t in range(PT):
                    last = nc.vector.bn_stats(stats[:, t, :], x_in[:, t, :])
                chain(last, it)
                nc.vector.memset(keep["still"][:], 0.0)
                for t in range(PT):
                    last = nc.vector.bn_aggr(mv[:, t, :], stats[:, t, :])
                chain(last, it)
                nc.vector.tensor_scalar(rstd[:], mv[:, :, 1], EPS_LN, None, ALU.add).then_inc(std_ready.sem, 1)
                dve.wait_ge(xn_std.sem, xn_std.at(it))
                chain(nc.vector.reciprocal(rstd[:], rstd[:]), it)
                for t in range(PT):
                    last = nc.vector.tensor_scalar(xn[:, t, :], x_in[:, t, :], mv[:, t, 0:1], rstd[:, t:t + 1], ALU.subtract, ALU.mult)
                last.then_inc(xn_ready.sem, 1)
                for i in range(3):
                    dve.wait_ge(pre_ready.sem, pre_ready.at(it, i + 1))
                    for j in range(CONV):
                        w = cw[:, i, j:j + 1]
                        if j == 0:
                            chain(nc.vector.tensor_scalar(con[i][:], pre[i][:, :, j:j + L], w, None, ALU.mult), it)
                        else:
                            ins = nc.vector.scalar_tensor_tensor(con[i][:], pre[i][:, :, j:j + L], w, con[i][:], ALU.mult, ALU.add)
                            if j < CONV - 1:
                                chain(ins, it)
                    ins.then_inc(con_ready.sem, 1)
                dve.wait_ge(silu_ready.sem, silu_ready.at(it, 3))
                for j in range(FS):
                    w = fsw[:, j:j + 1]
                    if j == 0:
                        chain(nc.vector.tensor_scalar(fir[:], vpad[:, :, j:j + L], w, None, ALU.mult), it)
                    else:
                        ins = nc.vector.scalar_tensor_tensor(fir[:], vpad[:, :, j:j + L], w, fir[:], ALU.mult, ALU.add)
                        if j < FS - 1:
                            chain(ins, it)
                ins.then_inc(fir_ready.sem, 1)
                for i in range(2):
                    dve.wait_ge(norm_ready.sem, norm_ready.at(it, i + 1))
                    chain(nc.vector.reciprocal(sq[:, i, :], sq[:, i, :]), it)
                    if i == 0:
                        dst, a, b_ = WQ[:, :, 1, :], con[0][:].rearrange("p s (n c) -> p (s n) c", c=CH), sq[:, 0, :].rearrange("p (n c) -> p n c", c=CH)
                    else:
                        dst, a, b_ = kT[:], con[1][:].rearrange("p s n -> p (s n)"), sq[:, 1, :]
                    nc.vector.tensor_tensor(dst, a, b_, ALU.mult).then_inc(qk_ready.sem, 1)
                dve.wait_ge(beta_ready.sem, beta_ready.at(it))
                dve.wait_ge(tok_out.sem, tok_out.at(it, 1))
                bb = beta[:].rearrange("p t h -> p (t h)").unsqueeze(2).broadcast_to([P, PT * NH, DK])
                chain(nc.vector.tensor_tensor(VK[:, :, :, 0, :].rearrange("p t h c -> p (t h) c"),
                                        ps23[:].rearrange("p a (b c) -> p (a b) c", c=DK), bb, ALU.mult), it)
                dve.wait_ge(tok_ps.sem, tok_ps.at(it, 2))
                nc.vector.tensor_tensor(VK[:, :, :, 1, :].rearrange("p t h c -> p (t h) c"),
                                        ps01[:].rearrange("p a (b c) -> p (a b) c", c=DK), bb, ALU.mult).then_inc(tok_out.sem, 1)
                dve.wait_ge(qk_ready.sem, qk_ready.at(it, 2))
                for h in range(NH):
                    last = nc.vector.transpose(kx[DK * h:DK * h + DK, :, DK * h:DK * h + DK],
                                               kT[DK * h:DK * h + DK, :].rearrange("p (n c) -> p n c", c=CH))
                last.then_inc(kx_ready.sem, 1)
                for hf in range(2):
                    dve.wait_ge(kk_ps.sem, kk_ps.at(it, hf + 1))
                    for c in range(4):
                        q = slice(CH * c, CH * c + CH)
                        last = nc.vector.tensor_tensor(
                            M[q, 4 * hf:4 * hf + 4].rearrange("p t h c -> p h t c"),
                            ps47[q, :, :].rearrange("p h (t c) -> p h t c", t=4)[:, :, :, CH * c:CH * c + CH],
                            beta[q, 4 * hf:4 * hf + 4].rearrange("p t h -> p h t").unsqueeze(3).broadcast_to([CH, NH, 4, CH]), ALU.mult)
                    last.then_inc(kk_used.sem, 1)
                dve.wait_ge(kk_used.sem, kk_used.at(it, 2))
                nc.vector.memset(X[:], 0.0).then_inc(dv.sem, 1)
                dv.next()
                nc.vector.transpose(A[:], M[:].rearrange("p t h j -> p j (t h)")).then_inc(dv.sem, 1)
                dv.next()
                dve.wait_ge(dv.sem, it * dv.per + dv.k)
                chain(nc.vector.memset(X[:].rearrange("p a b -> p (a b)")[:, 0:CH * CH:CH + 1], 1.0), it)
                for j in range(CH - 1):
                    r, c = CH - 1 - j, j + 1
                    t3 = tmp[:, 0:r * c].rearrange("p (r c) -> p r c", c=c)
                    chain(nc.vector.tensor_tensor(t3, A[:, j, j + 1:].unsqueeze(2).broadcast_to([P, r, c]),
                                                  X[:, j:j + 1, 0:c].broadcast_to([P, r, c]), ALU.mult), it)
                    chain(nc.vector.tensor_tensor(X[:, j + 1:, 0:c], X[:, j + 1:, 0:c], t3, ALU.subtract), it)
                for c in range(4):
                    q = slice(CH * c, CH * c + CH)
                    last = nc.vector.transpose(TT[q, :, CH * c:CH * c + CH].rearrange("p b i -> p i b"), X[q, :, :])
                last.then_inc(TT_ready.sem, 1)
                dve.wait_ge(UWT_ready.sem, UWT_ready.at(it, 2))
                for n in range(STEPS):
                    dve.wait_ge(WS_ps.sem, WS_ps.at(it, n + 1))
                    u3 = u2T[:].rearrange("p (s x) -> p s x", s=PAIR)[:, :, n * CH:(n + 1) * CH]
                    chain(nc.vector.tensor_tensor(
                        u3, uT[:].rearrange("p (s x) -> p s x", s=PAIR)[:, :, n * CH:(n + 1) * CH],
                        ps01[:, n % 2, 0:PAIR * 64].rearrange("p (s x) -> p s x", s=PAIR)[:, :, 0:32], ALU.subtract), it)
                    if n:
                        dve.wait_ge(S_ps.sem, S_ps.at(it, n))
                    nc.vector.transpose(u2h[:], u3).then_inc(u2_ready.sem, 1)
                    dve.wait_ge(S_ps.sem, S_ps.at(it, n + 1))
                    for h in range(NH):
                        last = nc.vector.tensor_copy(
                            Sx[DK * h:DK * h + DK, :, DK * h:DK * h + DK],
                            ps23[DK * h:DK * h + DK, 0, 0:PAIR * DK].rearrange("p (s x) -> p s x", s=PAIR))
                    last.then_inc(S_ready.sem, 1)
                for hf in range(2):
                    dve.wait_ge(qk_ps.sem, qk_ps.at(it, hf + 1))
                    if hf:
                        dve.wait_ge(o_ps.sem, o_ps.at(it, 1))
                    for h in range(NH):
                        last = nc.vector.tensor_tensor(
                            AT[:, :, h, :], ps47[:, h, :].rearrange("p (t i) -> p t i", t=4),
                            causal[:].unsqueeze(1).broadcast_to([P, 4, P]), ALU.mult)
                    last.then_inc(AT_ready.sem, 1)
                dve.wait_ge(o_ps.sem, o_ps.at(it, 2))
                dve.wait_ge(qst_ready.sem, qst_ready.at(it))
                nc.vector.tensor_tensor(d_tok[:, bass.ds(it * PT, PT), :], ps01[:].rearrange("p a (b c) -> p (a b) c", c=H),
                                        qstok[:], ALU.add).then_inc(o_ready.sem, 1)
                round_over(dve, it)
            assert dv.k == dv.per, dv.k

        @block.tensor
        def _(pe):
            pe.wait_ge(cleared.sem, 7)
            with pe.Fori(0, ROUNDS) as it:
                pe.wait_ge(xn_ready.sem, xn_ready.at(it))
                for t in range(PT):
                    last = nc.tensor.transpose(ps01[:, t // 4, P * (t % 4):P * (t % 4) + P], xn[:, t, :], ident[:])
                last.then_inc(xT_ps.sem, 1)
                pe.wait_ge(xT_ready.sem, xT_ready.at(it))
                for i, ps in enumerate((ps23[:, 0:2], ps47[:, 0:2], ps47[:, 2:4])):
                    for s in range(PAIR):
                        last = nc.tensor.matmul(ps[:, s, :], wqkv[:, i, :], xT[:, s * L:(s + 1) * L], start=True, stop=True)
                    last.then_inc(proj_ps.sem, 1)
                for t in range(PT):
                    last = nc.tensor.matmul(ps01[:, 0, t * NH:(t + 1) * NH], xT[:, t * P:(t + 1) * P], wb[:], start=True, stop=True)
                last.then_inc(beta_ps.sem, 1)
                for i, ps in enumerate((ps23, ps01)):
                    pe.wait_ge(sq_ready.sem, sq_ready.at(it, i + 1))
                    if i == 0:
                        pe.wait_ge(pre_ready.sem, pre_ready.at(it, 1))
                    else:
                        pe.wait_ge(beta_ready.sem, beta_ready.at(it))
                    for s in range(PAIR):
                        last = nc.tensor.matmul(ps[:, s, :], blk[:], sq[:, i, s * L:(s + 1) * L], start=True, stop=True)
                    last.then_inc(ss_ps.sem, 1)
                pe.wait_ge(silu_ready.sem, silu_ready.at(it, 3))
                pe.wait_ge(norm_ready.sem, norm_ready.at(it, 1))
                for t in range(PT):
                    last = nc.tensor.transpose(ps23[:, t // 4, P * (t % 4):P * (t % 4) + P], vpad[:, t // 4, FS - 1 + P * (t % 4):FS - 1 + P * (t % 4) + P], ident[:])
                last.then_inc(tok_ps.sem, 1)
                pe.wait_ge(qk_ready.sem, qk_ready.at(it, 2))
                for t in range(PT):
                    last = nc.tensor.transpose(ps01[:, t // 4, P * (t % 4):P * (t % 4) + P], kT[:, t * P:(t + 1) * P], ident[:])
                last.then_inc(tok_ps.sem, 1)
                pe.wait_ge(pre_ready.sem, pre_ready.at(it, 3))
                for hf in range(2):
                    if hf:
                        pe.wait_ge(kk_used.sem, kk_used.at(it, 1))
                    for h in range(NH):
                        q = slice(DK * h, DK * h + DK)
                        for t in range(4):
                            s = slice((4 * hf + t) * P, (4 * hf + t + 1) * P)
                            last = nc.tensor.matmul(ps47[:, h, t * P:(t + 1) * P], kT[q, s], kT[q, s], start=True, stop=True)
                    last.then_inc(kk_ps.sem, 1)
                pe.wait_ge(fir_ready.sem, fir_ready.at(it))
                pe.wait_ge(tok_out.sem, tok_out.at(it, 2))
                for t in range(PT):
                    last = nc.tensor.transpose(ps23[:, t // 4, P * (t % 4):P * (t % 4) + P], fir[:, t // 4, P * (t % 4):P * (t % 4) + P], ident[:])
                last.then_inc(tok_ps.sem, 1)
                pe.wait_ge(TT_ready.sem, TT_ready.at(it))
                pe.wait_ge(kk_used.sem, kk_used.at(it, 2))
                for hf in range(2):
                    for t in range(4):
                        for h in range(NH):
                            g = (4 * hf + t) * NH + h
                            last = nc.tensor.matmul(ps47[:, g // 8, 64 * (g % 8):64 * (g % 8) + 64], TT[:, g, :],
                                                    VK[:, g // NH, h].rearrange("p w c -> p (w c)"), start=True, stop=True)
                    last.then_inc(UW_ps.sem, 1)
                pe.wait_ge(UW_ready.sem, UW_ready.at(it, 4))
                pe.wait_ge(tok_out.sem, tok_out.at(it, 3))
                for w, ps in enumerate((ps01, ps23)):
                    for t in range(PT):
                        last = nc.tensor.transpose(ps[:, t // 4, P * (t % 4):P * (t % 4) + P], UW[:, t, w, :], ident[:])
                    last.then_inc(UWT_ps.sem, 1)
                pe.wait_ge(UWT_ready.sem, UWT_ready.at(it, 2))
                pe.wait_ge(S_zero.sem, S_zero.at(it))
                pe.wait_ge(kx_ready.sem, kx_ready.at(it))
                nc.tensor.matmul(ps23[:, 0, 0:PAIR * DK], ident[:], zero[:], start=True, stop=False, skip_group_check=True)
                for n in range(STEPS):
                    if n:
                        pe.wait_ge(S_ready.sem, S_ready.at(it, n))
                    if n >= 2:
                        pe.wait_ge(qs_ready.sem, qs_ready.at(it, n - 1))
                    for s in range(PAIR):
                        last = nc.tensor.matmul(ps01[:, n % 2, 64 * s:64 * s + 64], Sx[:, s, :],
                                                WQ[:, s * STEPS + n].rearrange("p w c -> p (w c)"), start=True, stop=True)
                    last.then_inc(WS_ps.sem, 1)
                    pe.wait_ge(u2_ready.sem, u2_ready.at(it, n + 1))
                    for s in range(PAIR):
                        last = nc.tensor.matmul(ps23[:, 0, DK * s:DK * s + DK], kx[:, s * STEPS + n, :], u2h[:, s, :],
                                                start=False, stop=n == STEPS - 1 and s == PAIR - 1, skip_group_check=True)
                    last.then_inc(S_ps.sem, 1)
                pe.wait_ge(qs_ready.sem, qs_ready.at(it))
                for t in range(PT):
                    last = nc.tensor.transpose(ps01[:, t // 4, P * (t % 4):P * (t % 4) + P], u2T[:, t * P:(t + 1) * P], ident[:])
                last.then_inc(u2t_ps.sem, 1)
                pe.wait_ge(S_ready.sem, S_ready.at(it))
                for t in range(PT):
                    last = nc.tensor.transpose(ps23[:, t // 4, P * (t % 4):P * (t % 4) + P], qsT[:, t * P:(t + 1) * P], ident[:])
                last.then_inc(qst_ps.sem, 1)
                for hf in range(2):
                    if hf:
                        pe.wait_ge(AT_ready.sem, AT_ready.at(it, 1))
                    for h in range(NH):
                        q = slice(DK * h, DK * h + DK)
                        for t in range(4):
                            g = 4 * hf + t
                            last = nc.tensor.matmul(ps47[:, h, t * P:(t + 1) * P].rearrange("p (n c) -> p n c", c=CH), kT[q, g * P:(g + 1) * P],
                                                    WQ[q, 4 * g:4 * g + 4, 1, :], start=True, stop=True)
                    last.then_inc(qk_ps.sem, 1)
                    pe.wait_ge(AT_ready.sem, AT_ready.at(it, hf + 1))
                    pe.wait_ge(u2t_ready.sem, u2t_ready.at(it))
                    for t in range(4):
                        for h in range(NH):
                            last = nc.tensor.matmul(ps01[:, hf, t * P + h * DK:t * P + h * DK + DK], AT[:, t, h, :],
                                                    u2tok[:, 4 * hf + t, h * DK:(h + 1) * DK], start=True, stop=True)
                    last.then_inc(o_ps.sem, 1)
                round_over(pe, it)


HA, DH = 16, 64
T4 = L // P
MH = 256
DVE_STEPS = 175
EPS_RMS = 1e-6
UNITS = HA * T4


def fir_phase(nc, d, keep):
    G = 16
    GROUPS = H // G
    with ExitStack() as ctx:
        def signal(name, per):
            return Signal(ctx.enter_context(nc.semaphore(name)), per)

        band = [ctx.enter_context(nc.sbuf_tensor(f"band{i}", [P, G, P + 64], F32)) for i in range(2)]
        v_back = ctx.enter_context(nc.sbuf_tensor("v_back", [P, TILES, H], F32))
        ps = [ctx.enter_context(nc.psum_tensor(f"fir_ps{i}", [P, TILES, G], F32)) for i in range(2)]
        back_ps = ctx.enter_context(nc.psum_tensor("back_ps", [P, 4, 4, H], F32))
        v_tok, fl_tok, anti = keep["v_tok"], keep["fl_tok"], keep["anti"]
        band_in = [signal(f"band_in{i}", 16) for i in range(2)]
        turned = signal("turned", 0)
        back = signal("back", 0)
        fir_ps = signal("fir_ps", 2)
        fir_free = signal("fir_free", 2)
        block = ctx.enter_context(nc.Block())
        z = d["fir_z"]
        width = z.shape[1]

        @block.sync
        def _(sp):
            for g in range(GROUPS):
                if g >= 2:
                    sp.wait_ge(fir_ps.sem, g - 1)
                src = bass.AP(z.tensor, g * G * width, [[1, P], [width, G], [1, P + 64]])
                sp.dma_start(band[g % 2][:], src).then_inc(band_in[g % 2].sem, 16)
            for s in band_in:
                sp.wait_ge(s.sem, 16 * (GROUPS // 2))

        @block.tensor
        def _(pe):
            for g in range(TILES // 4):
                if g >= 4:
                    pe.wait_ge(back.sem, g - 3)
                nc.tensor.matmul(back_ps[:, g % 4], anti[:], v_tok[:, 4 * g:4 * g + 4, :], start=True, stop=True).then_inc(turned.sem, 1)
            with pe.Fori(0, GROUPS // 2) as it:
                for i in range(2):
                    pe.wait_ge(band_in[i].sem, it * 16 + 16)
                    pe.wait_ge(fir_free.sem, it * 2 + 1)
                    for c in range(G):
                        v1 = v_back[:, :, bass.ds((it * 2 + i) * G + c, 1)]
                        nc.tensor.matmul(ps[i][:, :, c], band[i][:, c, 0:P], v1.rearrange("p t c -> p (t c)"),
                                         start=True, stop=False, skip_group_check=True)
                        last = nc.tensor.matmul(
                            ps[i][0:64, :, c].rearrange("p (b n) -> p b n", n=T4)[:, :, 1:], band[i][:, c, P:P + 64],
                            v1.rearrange("p (b n) c -> p b (n c)", n=T4)[:, :, 0:T4 - 1],
                            start=False, stop=True, skip_group_check=True)
                    last.then_inc(fir_ps.sem, 1)

        @block.scalar
        def _(act):
            for g in range(TILES // 4):
                act.wait_ge(turned.sem, g + 1)
                nc.scalar.activation(v_back[:, 4 * g:4 * g + 4, :], back_ps[:, g % 4], ACT.Copy).then_inc(
                    back.sem if g < TILES // 4 - 1 else fir_free.sem, 1)
            with act.Fori(0, GROUPS // 2) as it:
                for i in range(2):
                    act.wait_ge(fir_ps.sem, it * 2 + i + 1)
                    nc.scalar.activation(fl_tok[:, :, bass.ds((it * 2 + i) * G, G)], ps[i][:], ACT.Copy).then_inc(fir_free.sem, 1)


def mix_phase(nc, d, keep):
    with ExitStack() as ctx:
        def sb(name, shape, dt=F32):
            return ctx.enter_context(nc.sbuf_tensor(name, shape, dt))

        def signal(name, per):
            return Signal(ctx.enter_context(nc.semaphore(name)), per)

        K = keep
        ident, v_tok, d_tok, fs_tok, fl_tok = (K[n] for n in ("ident", "v_tok", "d_tok", "fs_tok", "fl_tok"))
        TH = T4 * NH
        x = sb("mx_x", [P, T4, H])
        st6 = sb("st6", [P, T4, 6])
        mv = sb("mmv", [P, T4, 2])
        rstd = sb("mrstd", [P, T4])
        z = sb("z", [P, T4, H])
        zT = sb("zT", [H, L])
        cen = sb("cen", [P, 4, T4, H])
        br = sb("br", [P, T4, 4, 2, NH])
        sT = sb("sT", [32, L])
        hT = sb("hT", [P, 2, L])
        lg = sb("lg", [P, TH, 4])
        lgm = sb("lgm", [P, TH])
        mix = sb("mix", [P, T4, H])
        rr = sb("rr", [P, TH])
        yT = sb("yT", [H, L])
        V = sb("V", [P, T4, HA, DH])
        sqb = sb("sqb", [P, 2, 512])
        ra = sb("ra", [P, 2, 512])
        rb = sb("rb", [P, 2, 512])
        ss = sb("ss", [P, T4, 2, HA])
        kTh = sb("kTh", [P, HA // 2, L], F16)
        kTl = sb("kTl", [P, HA // 2, L], F16)
        qTh = sb("qTh", [P, HA, L], F16)
        qTl = sb("qTl", [P, HA, L], F16)
        nmx = sb("nmx", [P, 4])
        nb = sb("nb", [P, 4])
        rs = sb("rs", [P, 2, T4])
        Pm = cen[:, 0:2].rearrange("p a t c -> p a (t c)")
        PT = cen[:, 2:4].rearrange("p a t c -> p a (t c)")
        O = sb("O", [P, 2, T4, 2 * DH])
        OT = sb("OT", [P, 2, L])
        ps = [ctx.enter_context(nc.psum_tensor(f"mps{i}", [P, 512], F32)) for i in range(8)]

        loaded = signal("loaded", 16)
        dv = Chain(ctx.enter_context(nc.semaphore("mdve")), DVE_STEPS)
        ac = Chain(ctx.enter_context(nc.semaphore("mact")), 0)
        pl = Chain(ctx.enter_context(nc.semaphore("mpool")), 0)
        z0 = ctx.enter_context(nc.semaphore("z0"))
        var_ready = signal("var_ready", 4)
        std_ready = signal("mstd_ready", 4)
        z_ready = signal("z_ready", 4)
        zT_ps = signal("zT_ps", 4)
        zT_ready = signal("zT_ready", 4)
        cen_ready = signal("cen_ready", 4)
        sqr_ready = signal("sqr_ready", 4)
        var4_ready = signal("var4_ready", 1)
        br_ready = signal("br_ready", 1)
        sT_ps = signal("sT_ps", 1)
        sT_ready = signal("sT_ready", 1)
        h_ps = signal("h_ps", 2)
        h_ready = signal("h_ready", 2)
        lg_ps = signal("lg_ps", 1)
        lg_ready = signal("lg_ready", 1)
        e_ready = signal("e_ready", 1)
        mix_ready = signal("mix_ready", 1)
        msq_ready = signal("msq_ready", 1)
        mvar_ready = signal("mvar_ready", 1)
        mstd2 = signal("mstd2", 1)
        on_ready = signal("on_ready", 1)
        oT_ps = signal("oT_ps", 1)
        oT_ready = signal("oT_ready", 1)
        wo_ps = signal("wo_ps", 1)
        ff_ps = signal("ff_ps", 2)
        ff_done = signal("ff_done", 2)
        proj = signal("proj", 24)
        sq_done = signal("sq_done", 16)
        v_done = signal("v_done", 8)
        ss_done = signal("ss_done", 16)
        rms_done = signal("rms_done", 16)
        rope_done = signal("rope_done", 16)
        tr_ps = signal("tr_ps", 16)
        hi_done = signal("hi_done", 16)
        lo_done = signal("lo_done", 16)
        s_ps = signal("s_ps", UNITS)
        nb_done = signal("nb_done", UNITS)
        p_done = signal("p_done", UNITS)
        pt_ps = signal("pt_ps", UNITS)
        pt_done = signal("pt_done", UNITS)
        o_ps = signal("mo_ps", UNITS)
        o_done = signal("mo_done", HA)
        ot_ps = signal("ot_ps", HA // 2)
        ot_done = signal("ot_done", HA // 2)
        y_ps = signal("y_ps", HA // 2)
        yT_done = signal("yT_done", 1)
        y_tr = signal("y_tr", 1)
        stored = signal("stored", 16)
        everything = [loaded, z_ready, zT_ready, sqr_ready, br_ready, sT_ready, h_ready, lg_ready, e_ready, mix_ready, msq_ready,
                      mstd2, on_ready, oT_ready, ff_done, sq_done, v_done, rms_done, rope_done, hi_done, lo_done,
                      p_done, pt_done, o_done, ot_done, y_ps, yT_done, y_tr, stored]
        block = ctx.enter_context(nc.Block())

        def round_over(eng, it):
            for s in everything:
                eng.wait_ge(s.sem, s.at(it))

        def chained(c, eng, it, ins):
            k = c.next()
            ins.then_inc(c.sem, 1)
            eng.wait_ge(c.sem, it * c.per + k)

        UN = [(h, i) for h in range(HA) for i in range(T4)]
        CHUNKS = [(t, m, hf) for t in range(T4) for m in ("k", "q", "v") for hf in range(2)]
        V_CHUNKS = [c for c in CHUNKS if c[1] == "v"]
        KQ = [c for c in CHUNKS if c[1] != "v"]

        @block.gpsimd
        def _(pool):
            nc.gpsimd.memset(qTh[:], 0.0).then_inc(z0, 1)
            nc.gpsimd.memset(qTl[:], 0.0).then_inc(z0, 1)
            with pool.Fori(0, B) as it:
                round_over(pool, it)

        def hi(act, it, n):
            t, m, hf = KQ[n]
            act.wait_ge(tr_ps.sem, tr_ps.at(it, n + 1))
            src = ps[2 + n % 2][:].rearrange("p (a t) -> p a t", a=4)
            ts = slice(t * P, t * P + P)
            if m == "k":
                nc.scalar.activation(kTh[:, 4 * hf:4 * hf + 4, ts], src, ACT.Copy).then_inc(hi_done.sem, 1)
            else:
                nc.scalar.activation(qTh[0:DH, 8 * hf:8 * hf + 8:2, ts], src[0:DH], ACT.Copy)
                nc.scalar.activation(qTh[DH:P, 8 * hf + 1:8 * hf + 8:2, ts], src[DH:P], ACT.Copy).then_inc(hi_done.sem, 1)

        def ot(act, it, g):
            act.wait_ge(ot_ps.sem, ot_ps.at(it, g + 1))
            if g >= 2:
                act.wait_ge(y_ps.sem, y_ps.at(it, g - 1))
            nc.scalar.activation(OT[:, g % 2, :], ps[6][:], ACT.Copy).then_inc(ot_done.sem, 1)

        @block.scalar
        def _(act):
            act.wait_ge(z0, 2)
            with act.Fori(0, B) as it:
                act.dma_start(x[:], d["x"][:, bass.ds(it * T4, T4), :]).then_inc(loaded.sem, 16)

                def norm(n):
                    act.wait_ge(var_ready.sem, var_ready.at(it, n))
                    nc.scalar.activation(rstd[:], rstd[:], ACT.Sqrt).then_inc(std_ready.sem, 1)

                def zt(n, bank):
                    act.wait_ge(zT_ps.sem, zT_ps.at(it, n))
                    nc.scalar.activation(zT[:], ps[bank][:], ACT.Copy).then_inc(zT_ready.sem, 1)

                norm(1)
                zt(1, 0)
                for j in range(4):
                    act.wait_ge(cen_ready.sem, cen_ready.at(it, j + 1))
                    nc.scalar.activation(cen[:, j], cen[:, j], ACT.Square).then_inc(sqr_ready.sem, 1)
                act.wait_ge(var4_ready.sem, var4_ready.at(it))
                nc.scalar.activation(br[:, :, :, 1, :].rearrange("p t j h -> p (t j) h"), br[:, :, :, 1, :].rearrange("p t j h -> p (t j) h"), ACT.Sqrt).then_inc(br_ready.sem, 1)
                act.wait_ge(sT_ps.sem, sT_ps.at(it))
                nc.scalar.activation(sT[:], ps[1][0:32, :], ACT.Copy).then_inc(sT_ready.sem, 1)
                for m in range(2):
                    act.wait_ge(h_ps.sem, h_ps.at(it, m + 1))
                    nc.scalar.activation(hT[:, m, :], ps[2 + m][:], ACT.Gelu, bias=K["b1"][:, m:m + 1]).then_inc(h_ready.sem, 1)
                act.wait_ge(lg_ready.sem, lg_ready.at(it))
                nc.scalar.activation(lg[:], lg[:], ACT.Exp).then_inc(e_ready.sem, 1)
                act.wait_ge(mix_ready.sem, mix_ready.at(it))
                nc.scalar.activation(cen[:, 0], mix[:], ACT.Square).then_inc(msq_ready.sem, 1)
                act.wait_ge(mvar_ready.sem, mvar_ready.at(it))
                nc.scalar.activation(rr[:], rr[:], ACT.Sqrt).then_inc(mstd2.sem, 1)
                act.wait_ge(oT_ps.sem, oT_ps.at(it))
                nc.scalar.activation(yT[:], ps[1][:], ACT.Copy).then_inc(oT_ready.sem, 1)
                norm(2)
                zt(2, 0)
                norm(3)
                zt(3, 0)
                nkq = nv = 0
                for n, (t, m, hf) in enumerate(CHUNKS):
                    bank = ps[n % 2]
                    act.wait_ge(proj.sem, proj.at(it, n + 1))
                    if m == "v":
                        nc.scalar.activation(V[:, t, 8 * hf:8 * hf + 8, :].rearrange("p h c -> p (h c)"), bank[:], ACT.Copy).then_inc(v_done.sem, 1)
                    else:
                        if nkq >= 2:
                            act.wait_ge(ss_done.sem, ss_done.at(it, nkq - 1))
                        nc.scalar.activation(sqb[:, nkq % 2, :], bank[:], ACT.Square).then_inc(sq_done.sem, 1)
                        act.wait_ge(ss_done.sem, ss_done.at(it, nkq + 1))
                        w = 0 if m == "k" else 1
                        sl = ss[:, t, w, 8 * hf:8 * hf + 8]
                        nc.scalar.activation(sl, sl, ACT.Sqrt, bias=K["eps6"][:, 0:1], scale=1.0 / DH).then_inc(rms_done.sem, 1)
                        nkq += 1
                        if nkq >= 2:
                            hi(act, it, nkq - 2)
                hi(act, it, 15)
                for u, (h, i) in enumerate(UN):
                    w = P * (i + 1)
                    act.wait_ge(nb_done.sem, nb_done.at(it, u + 1))
                    if u >= 2:
                        act.wait_ge(pt_ps.sem, pt_ps.at(it, u - 1))
                    if i == 0 and h >= 2:
                        act.wait_ge(o_done.sem, o_done.at(it, h - 1))
                    nc.scalar.activation(Pm[:, u % 2, 0:w], ps[u % 2][:, 0:w], ACT.Exp, bias=nb[:, u % 4:u % 4 + 1],
                                         scale=ss[:, i, 1, h:h + 1], accum_out=rs[:, h % 2, i:i + 1]).then_inc(p_done.sem, 1)
                    if i == 1 and h % 2 and h >= 3:
                        ot(act, it, h // 2 - 1)
                ot(act, it, HA // 2 - 1)
                act.wait_ge(y_ps.sem, y_ps.at(it))
                nc.scalar.activation(yT[:], ps[7][:], ACT.Copy).then_inc(yT_done.sem, 1)
                norm(4)
                zt(4, 0)
                act.wait_ge(ff_done.sem, ff_done.at(it, 2))
                act.dma_start(d["out"][:, bass.ds(it * T4, T4), :], x[:]).then_inc(stored.sem, 16)
                round_over(act, it)

        def lo(dve, it, n):
            t, m, hf = KQ[n]
            dve.wait_ge(hi_done.sem, hi_done.at(it, n + 1))
            src = ps[2 + n % 2][:].rearrange("p (a t) -> p a t", a=4)
            ts = slice(t * P, t * P + P)
            if m == "k":
                nc.vector.tensor_tensor(kTl[:, 4 * hf:4 * hf + 4, ts], src, kTh[:, 4 * hf:4 * hf + 4, ts], ALU.subtract).then_inc(lo_done.sem, 1)
            else:
                e, o_ = slice(8 * hf, 8 * hf + 8, 2), slice(8 * hf + 1, 8 * hf + 8, 2)
                nc.vector.tensor_tensor(qTl[0:DH, e, ts], src[0:DH], qTh[0:DH, e, ts], ALU.subtract)
                nc.vector.tensor_tensor(qTl[DH:P, o_, ts], src[DH:P], qTh[DH:P, o_, ts], ALU.subtract).then_inc(lo_done.sem, 1)

        def pt_out(dve, it, u):
            w = P * (UN[u][1] + 1)
            dve.wait_ge(pt_ps.sem, pt_ps.at(it, u + 1))
            if u >= 2:
                dve.wait_ge(o_ps.sem, o_ps.at(it, u - 1))
            nc.vector.tensor_copy(PT[:, u % 2, 0:w], ps[2 + u % 2][:, 0:w]).then_inc(pt_done.sem, 1)

        def o_out(dve, it, h, ch):
            dve.wait_ge(p_done.sem, p_done.at(it, T4 * h + T4))
            ch(nc.vector.reciprocal(rs[:, h % 2], rs[:, h % 2]))
            dve.wait_ge(o_ps.sem, o_ps.at(it, T4 * h + T4))
            if h >= 4:
                dve.wait_ge(ot_ps.sem, ot_ps.at(it, h // 2 - 1))
            nc.vector.tensor_tensor(O[:, h // 2 % 2, :, DH * (h % 2):DH * (h % 2) + DH], ps[4 + h % 2][:, 0:T4 * DH].rearrange("p (t c) -> p t c", t=T4),
                                    rs[:, h % 2].unsqueeze(2).broadcast_to([P, T4, DH]), ALU.mult).then_inc(o_done.sem, 1)

        @block.vector
        def _(dve):
            dve.wait_ge(z0, 2)
            with dve.Fori(0, B) as it:
                def ch(ins):
                    chained(dv, dve, it, ins)

                def norm(n):
                    for t in range(T4):
                        last = nc.vector.bn_stats(st6[:, t, :], x[:, t, :])
                    ch(last)
                    nc.vector.memset(K["still"][:], 0.0)
                    for t in range(T4):
                        last = nc.vector.bn_aggr(mv[:, t, :], st6[:, t, :])
                    ch(last)
                    nc.vector.tensor_scalar(rstd[:], mv[:, :, 1], EPS_LN, None, ALU.add).then_inc(var_ready.sem, 1)
                    dve.wait_ge(std_ready.sem, std_ready.at(it, n))
                    ch(nc.vector.reciprocal(rstd[:], rstd[:]))
                    for t in range(T4):
                        last = nc.vector.tensor_scalar(z[:, t, :], x[:, t, :], mv[:, t, 0:1], rstd[:, t:t + 1], ALU.subtract, ALU.mult)
                    last.then_inc(z_ready.sem, 1)

                def linear(n):
                    dve.wait_ge(ff_ps.sem, ff_ps.at(it, n))
                    p3 = ps[1][:].rearrange("p (t c) -> p t c", t=T4)
                    ch(nc.vector.tensor_tensor(z[:], p3, K["scb"][:].unsqueeze(1).broadcast_to([P, T4, H]), ALU.mult))
                    ch(nc.vector.tensor_tensor(z[:], z[:], K["bias"][:].unsqueeze(1).broadcast_to([P, T4, H]), ALU.add))
                    nc.vector.tensor_tensor(x[:], x[:], z[:], ALU.add).then_inc(ff_done.sem, 1)
                    dve.wait_ge(ff_done.sem, ff_done.at(it, n))

                dve.wait_ge(loaded.sem, loaded.at(it))
                norm(1)
                srcs = [t[:, bass.ds(it * T4, T4), :].rearrange("p t c -> p (t c)") for t in (fs_tok, fl_tok, d_tok, v_tok)]
                for j, s in enumerate(srcs):
                    s3 = s.rearrange("p (g c) -> p g c", c=DK)
                    m = br[:, :, j, 0, :]
                    ch(nc.vector.tensor_reduce(lgm[:], s3, AX.X, ALU.add))
                    ch(nc.vector.tensor_scalar(m, lgm[:].rearrange("p (t h) -> p t h", t=T4), 1.0 / DK, None, ALU.mult))
                    for t in range(T4):
                        last = nc.vector.tensor_tensor(cen[:, j, t].rearrange("p (h c) -> p h c", c=DK), s3[:, NH * t:NH * t + NH],
                                                       br[:, t, j, 0, :].unsqueeze(2).broadcast_to([P, NH, DK]), ALU.subtract)
                    last.then_inc(cen_ready.sem, 1)
                for j in range(4):
                    dve.wait_ge(sqr_ready.sem, sqr_ready.at(it, j + 1))
                    ch(nc.vector.tensor_reduce(lgm[:], cen[:, j].rearrange("p t (h c) -> p (t h) c", c=DK), AX.X, ALU.add))
                    last = nc.vector.tensor_scalar(br[:, :, j, 1, :], lgm[:].rearrange("p (t h) -> p t h", t=T4), 1.0 / DK, 1e-6, ALU.mult, ALU.max)
                    if j < 3:
                        ch(last)
                last.then_inc(var4_ready.sem, 1)
                dve.wait_ge(lg_ps.sem, lg_ps.at(it))
                lp = ps[4][:, 0:4 * TH].rearrange("p (t x) -> p t x", t=T4)
                lg3 = lg[:].rearrange("p (t h) j -> p t (h j)", t=T4)
                ch(nc.vector.tensor_tensor(lg3, lp, K["rtemp"][:].unsqueeze(1).broadcast_to([P, T4, 16]), ALU.mult))
                ch(nc.vector.tensor_reduce(lgm[:], lg[:], AX.X, ALU.max))
                nc.vector.tensor_tensor(lg[:], lg[:], lgm[:].unsqueeze(2).broadcast_to([P, TH, 4]), ALU.subtract).then_inc(lg_ready.sem, 1)
                dve.wait_ge(e_ready.sem, e_ready.at(it))
                ch(nc.vector.tensor_reduce(lgm[:], lg[:], AX.X, ALU.add))
                ch(nc.vector.reciprocal(lgm[:], lgm[:]))
                ch(nc.vector.tensor_tensor(lg[:], lg[:], lgm[:].unsqueeze(2).broadcast_to([P, TH, 4]), ALU.mult))
                m3 = mix[:].rearrange("p t (h c) -> p (t h) c", c=DK)
                c3 = cen[:, 1].rearrange("p t (h c) -> p (t h) c", c=DK)
                for j, s in enumerate(srcs):
                    s3 = s.rearrange("p (g c) -> p g c", c=DK)
                    ch(nc.vector.tensor_tensor(m3 if j == 0 else c3, s3, lg[:, :, j:j + 1].broadcast_to([P, TH, DK]), ALU.mult))
                    if j:
                        ins = nc.vector.tensor_tensor(m3, m3, c3, ALU.add)
                        if j < 3:
                            ch(ins)
                ins.then_inc(mix_ready.sem, 1)
                dve.wait_ge(msq_ready.sem, msq_ready.at(it))
                ch(nc.vector.tensor_reduce(rr[:], cen[:, 0].rearrange("p t (h c) -> p (t h) c", c=DK), AX.X, ALU.add))
                nc.vector.tensor_scalar(rr[:], rr[:], 1.0 / DK, 1e-5, ALU.mult, ALU.add).then_inc(mvar_ready.sem, 1)
                dve.wait_ge(mstd2.sem, mstd2.at(it))
                ch(nc.vector.reciprocal(rr[:], rr[:]))
                ch(nc.vector.tensor_tensor(m3, m3, rr[:].unsqueeze(2).broadcast_to([P, TH, DK]), ALU.mult))
                nc.vector.tensor_tensor(m3, m3, K["onorm"][:].unsqueeze(1).broadcast_to([P, TH, DK]), ALU.mult).then_inc(on_ready.sem, 1)
                dve.wait_ge(wo_ps.sem, wo_ps.at(it))
                ch(nc.vector.tensor_tensor(x[:], x[:], ps[2][:].rearrange("p (t c) -> p t c", t=T4), ALU.add))
                norm(2)
                linear(1)
                norm(3)
                for n, (t, m, hf) in enumerate(KQ):
                    bank = ps[CHUNKS.index((t, m, hf)) % 2]
                    w = 0 if m == "k" else 1
                    p_ = n % 2
                    dve.wait_ge(sq_done.sem, sq_done.at(it, n + 1))
                    sl = ss[:, t, w, 8 * hf:8 * hf + 8]
                    nc.vector.tensor_reduce(sl, sqb[:, p_].rearrange("p (h c) -> p h c", c=DH), AX.X, ALU.add).then_inc(ss_done.sem, 1)
                    b4 = bank[:].rearrange("p (h w c) -> p h w c", h=8, w=2)
                    a3 = ra[:, p_].rearrange("p (h c) -> p h c", c=DH)
                    r4 = rb[:, p_].rearrange("p (h w c) -> p h w c", h=8, w=2)
                    tab = K["rope"][:, w, t]
                    if n >= 2:
                        dve.wait_ge(tr_ps.sem, tr_ps.at(it, n - 1))
                    nc.vector.tensor_tensor(a3, bank[:].rearrange("p (h c) -> p h c", c=DH), tab[:, 0:1].broadcast_to([P, 8, DH]), ALU.mult)
                    nc.vector.tensor_tensor(r4[:, :, 0], b4[:, :, 1], tab[:, 1:2, 0:32].broadcast_to([P, 8, 32]), ALU.mult)
                    ch(nc.vector.tensor_tensor(r4[:, :, 1], b4[:, :, 0], tab[:, 1:2, 32:64].broadcast_to([P, 8, 32]), ALU.mult))
                    dve.wait_ge(rms_done.sem, rms_done.at(it, n + 1))
                    ch(nc.vector.reciprocal(sl, sl))
                    if m == "k":
                        ch(nc.vector.tensor_tensor(ra[:, p_], ra[:, p_], rb[:, p_], ALU.add))
                        nc.vector.tensor_tensor(a3, a3, sl.unsqueeze(2).broadcast_to([P, 8, DH]), ALU.mult).then_inc(rope_done.sem, 1)
                    else:
                        ch(nc.vector.tensor_scalar(sl, sl, DH ** -0.5, None, ALU.mult))
                        nc.vector.tensor_tensor(ra[:, p_], ra[:, p_], rb[:, p_], ALU.add).then_inc(rope_done.sem, 1)
                    if n >= 1:
                        lo(dve, it, n - 1)
                lo(dve, it, 15)
                for u, (h, i) in enumerate(UN):
                    w = P * (i + 1)
                    dve.wait_ge(s_ps.sem, s_ps.at(it, u + 1))
                    if u >= 4:
                        dve.wait_ge(p_done.sem, p_done.at(it, u - 3))
                    ch(nc.vector.tensor_reduce(nmx[:, u % 4:u % 4 + 1], ps[u % 2][:, 0:w], AX.X, ALU.max, negate=True))
                    nc.vector.tensor_tensor(nb[:, u % 4:u % 4 + 1], nmx[:, u % 4:u % 4 + 1], ss[:, i, 1, h:h + 1], ALU.mult).then_inc(nb_done.sem, 1)
                    if u >= 1:
                        pt_out(dve, it, u - 1)
                    if i == 2 and h:
                        o_out(dve, it, h - 1, ch)
                pt_out(dve, it, UNITS - 1)
                o_out(dve, it, HA - 1, ch)
                dve.wait_ge(y_tr.sem, y_tr.at(it))
                ch(nc.vector.tensor_tensor(x[:], x[:], ps[1][:].rearrange("p (t c) -> p t c", t=T4), ALU.add))
                norm(4)
                linear(2)
                round_over(dve, it)
            assert dv.k == dv.per, dv.k

        @block.tensor
        def _(pe):
            pe.wait_ge(z0, 2)
            with pe.Fori(0, B) as it:
                def to_T(n, src, bank, rows=P):
                    for t in range(T4):
                        last = nc.tensor.transpose(ps[bank][0:rows, t * P:(t + 1) * P], src(t), ident[:])
                    return last

                def zt(n):
                    pe.wait_ge(z_ready.sem, z_ready.at(it, n))
                    to_T(n, lambda t: z[:, t, :], 0).then_inc(zT_ps.sem, 1)
                    pe.wait_ge(zT_ready.sem, zT_ready.at(it, n))

                def linear(n):
                    zt(2 * n)
                    for t in range(T4):
                        last = nc.tensor.matmul(ps[1][:, t * P:(t + 1) * P], zT[:, t * P:(t + 1) * P], K["cbT"][:], start=True, stop=True)
                    last.then_inc(ff_ps.sem, 1)

                zt(1)
                pe.wait_ge(br_ready.sem, br_ready.at(it))
                to_T(0, lambda t: br[:, t].rearrange("p j m h -> p (j m h)"), 1, 32).then_inc(sT_ps.sem, 1)
                pe.wait_ge(sT_ready.sem, sT_ready.at(it))
                for m in range(2):
                    nc.tensor.matmul(ps[2 + m][:], K["w1x"][:, m * P:(m + 1) * P], zT[:], start=True, stop=False)
                    nc.tensor.matmul(ps[2 + m][:], K["w1s"][0:32, m * P:(m + 1) * P], sT[:], start=False, stop=True).then_inc(h_ps.sem, 1)
                pe.wait_ge(h_ready.sem, h_ready.at(it))
                for t in range(T4):
                    dst = ps[4][:, 16 * t:16 * t + 16]
                    nc.tensor.matmul(dst, K["ones"][0:1, :], K["b2"][0:1, :], start=True, stop=False)
                    for m in range(2):
                        last = nc.tensor.matmul(dst, hT[:, m, t * P:(t + 1) * P], K["w2"][:, m, :], start=False, stop=m == 1)
                last.then_inc(lg_ps.sem, 1)
                pe.wait_ge(on_ready.sem, on_ready.at(it))
                to_T(0, lambda t: mix[:, t, :], 1).then_inc(oT_ps.sem, 1)
                pe.wait_ge(oT_ready.sem, oT_ready.at(it))
                for t in range(T4):
                    last = nc.tensor.matmul(ps[2][:, t * P:(t + 1) * P], yT[:, t * P:(t + 1) * P], K["wo_a"][:], start=True, stop=True)
                last.then_inc(wo_ps.sem, 1)
                linear(1)
                zt(3)
                pe.wait_ge(ff_done.sem, ff_done.at(it, 1))
                order = {"q": 0, "k": 1, "v": 2}

                def turn(n):
                    pe.wait_ge(rope_done.sem, rope_done.at(it, n + 1))
                    if n >= 2:
                        pe.wait_ge(lo_done.sem, lo_done.at(it, n - 1))
                    for a in range(4):
                        last = nc.tensor.transpose(ps[2 + n % 2][:, a * P:(a + 1) * P], ra[:, n % 2, a * P:(a + 1) * P], ident[:])
                    last.then_inc(tr_ps.sem, 1)

                for n, (t, m, hf) in enumerate(CHUNKS):
                    if n >= 2:
                        if CHUNKS[n - 2][1] == "v":
                            pe.wait_ge(v_done.sem, v_done.at(it, V_CHUNKS.index(CHUNKS[n - 2]) + 1))
                        else:
                            pe.wait_ge(rope_done.sem, rope_done.at(it, KQ.index(CHUNKS[n - 2]) + 1))
                    nc.tensor.matmul(ps[n % 2][:], zT[:, t * P:(t + 1) * P], K["wqkvT"][:, order[m] * 1024 + hf * 512:order[m] * 1024 + hf * 512 + 512],
                                     start=True, stop=True).then_inc(proj.sem, 1)
                    if m != "v" and KQ.index((t, m, hf)):
                        turn(KQ.index((t, m, hf)) - 1)
                turn(15)
                pe.wait_ge(lo_done.sem, lo_done.at(it))
                pe.wait_ge(v_done.sem, v_done.at(it))

                def scores(u):
                    h, i = UN[u]
                    w = P * (i + 1)
                    ts = slice(i * P, i * P + P)
                    if u >= 2:
                        pe.wait_ge(p_done.sem, p_done.at(it, u - 1))
                    dst = ps[u % 2]
                    nc.tensor.matmul(dst[:, 0:w], qTh[:, h, ts], kTh[:, h // 2, 0:w], start=True, stop=False)
                    nc.tensor.matmul(dst[:, 0:w], qTl[:, h, ts], kTh[:, h // 2, 0:w], start=False, stop=False)
                    nc.tensor.matmul(dst[:, w - P:w], K["identb"][:], K["maskb"][:], start=False, stop=False, skip_group_check=True)
                    nc.tensor.matmul(dst[:, 0:w], qTh[:, h, ts], kTl[:, h // 2, 0:w], start=False, stop=True).then_inc(s_ps.sem, 1)

                def turn_p(u):
                    pe.wait_ge(p_done.sem, p_done.at(it, u + 1))
                    if u >= 2:
                        pe.wait_ge(pt_done.sem, pt_done.at(it, u - 1))
                    for j in range(UN[u][1] + 1):
                        last = nc.tensor.transpose(ps[2 + u % 2][:, j * P:(j + 1) * P], Pm[:, u % 2, j * P:(j + 1) * P], ident[:])
                    last.then_inc(pt_ps.sem, 1)

                def values(u):
                    h, i = UN[u]
                    pe.wait_ge(pt_done.sem, pt_done.at(it, u + 1))
                    if i == 0 and h >= 2:
                        pe.wait_ge(o_done.sem, o_done.at(it, h - 1))
                    for j in range(i + 1):
                        last = nc.tensor.matmul(ps[4 + h % 2][:, DH * i:DH * i + DH], PT[:, u % 2, j * P:(j + 1) * P], V[:, j, h, :], start=j == 0, stop=j == i)
                    last.then_inc(o_ps.sem, 1)
                    if i == 3 and h % 2 == 0 and h:
                        out_pair(h // 2 - 1)
                    if i == 1 and h % 2 and h > 1:
                        out_product(h // 2 - 1)

                def out_pair(g):
                    pe.wait_ge(o_done.sem, o_done.at(it, 2 * g + 2))
                    if g:
                        pe.wait_ge(ot_done.sem, ot_done.at(it, g))
                    for t in range(T4):
                        last = nc.tensor.transpose(ps[6][:, t * P:(t + 1) * P], O[:, g % 2, t, :], ident[:])
                    last.then_inc(ot_ps.sem, 1)

                def out_product(g):
                    pe.wait_ge(ot_done.sem, ot_done.at(it, g + 1))
                    nc.tensor.matmul(ps[7][:], K["woT"][:, g, :], OT[:, g % 2, :], start=g == 0, stop=g == 7).then_inc(y_ps.sem, 1)

                for u in range(UNITS):
                    scores(u)
                    if u >= 1:
                        turn_p(u - 1)
                    if u >= 2:
                        values(u - 2)
                turn_p(UNITS - 1)
                values(UNITS - 2)
                values(UNITS - 1)
                out_pair(HA // 2 - 1)
                out_product(HA // 2 - 1)
                pe.wait_ge(yT_done.sem, yT_done.at(it))
                to_T(0, lambda t: yT[:, t * P:(t + 1) * P], 1).then_inc(y_tr.sem, 1)
                linear(2)
                round_over(pe, it)

def build_kernel(nc, d, out):
    with ExitStack() as ctx:
        def sb(name, shape, dt=F32):
            return ctx.enter_context(nc.sbuf_tensor(name, shape, dt))

        def load_all(names, sem):
            with nc.Block() as block:
                @block.sync
                def _(sp):
                    for n in names:
                        sp.dma_start(keep[n][:], d[n]).then_inc(sem, 16)
                    sp.wait_ge(sem, 16 * len(names))

        keep = {}
        for n, shape in dict(v_tok=[P, TILES, H], d_tok=[P, TILES, H], fs_tok=[P, TILES, H], ident=[P, P], anti=[P, P], eps6=[P, 1]).items():
            keep[n] = sb(n, shape)
        keep["still"] = sb("still", [P, 1])
        with ExitStack() as own:
            for n, shape in dict(wqkv=[H, 3, H], wb=[H, NH], cw=[H, 3, CONV], fsw=[H, FS], blk=[P, P], causal=[P, P]).items():
                keep[n] = own.enter_context(nc.sbuf_tensor(n, shape, F32))
            load_all(("ident", "anti", "eps6", "wqkv", "wb", "cw", "fsw", "blk", "causal"), own.enter_context(nc.semaphore("first_in")))
            delta_phase(nc, d, keep)
        keep["fl_tok"] = sb("fl_tok", [P, TILES, H])
        fir_phase(nc, d, keep)

        shapes = dict(b1=[P, 2], b2=[1, 16], w1x=[H, MH], w1s=[32, MH], w2=[P, 2, 16], ones=[1, P], wo_a=[H, H], cbT=[H, H],
                      scb=[P, H], bias=[P, H], onorm=[P, DK], rtemp=[P, 16], wqkvT=[H, 3 * HA * DH], woT=[P, HA // 2, H],
                      rope=[P, 2, T4, 2, DH], nw=[P, 2, 2, DH], mask=[P, P])
        for n, shape in shapes.items():
            keep[n] = sb(n, shape)
        keep["identb"] = sb("identb", [P, P], BF16)
        keep["maskb"] = sb("maskb", [P, P], BF16)
        load_all(list(shapes), ctx.enter_context(nc.semaphore("second_in")))
        tables(nc, keep, ctx)
        mix_phase(nc, dict(d, out=out), keep)


def tables(nc, K, ctx):
    g = K["rtemp"]
    t = ctx.enter_context(nc.sbuf_tensor("soft", [P, 3, 16], F32))
    step = ctx.enter_context(nc.semaphore("table_step"))
    expd = ctx.enter_context(nc.semaphore("table_exp"))
    with nc.Block() as block:
        @block.scalar
        def _(act):
            act.wait_ge(step, 2)
            nc.scalar.activation(t[:, 1], t[:, 0], ACT.Exp, scale=-1.0).then_inc(expd, 1)
            act.wait_ge(step, 3)
            nc.scalar.activation(t[:, 2], t[:, 1], ACT.Ln).then_inc(expd, 1)

        @block.vector
        def _(dve):
            n = [0]

            def chain(ins):
                n[0] += 1
                ins.then_inc(step, 1)
                dve.wait_ge(step, n[0])

            chain(nc.vector.tensor_scalar(t[:, 0], g[:], -1.0, None, ALU.mult))
            chain(nc.vector.tensor_tensor(t[:, 0], t[:, 0], g[:], ALU.max))
            dve.wait_ge(expd, 1)
            chain(nc.vector.tensor_scalar(t[:, 1], t[:, 1], 1.0, None, ALU.add))
            dve.wait_ge(expd, 2)
            chain(nc.vector.scalar_tensor_tensor(g[:], g[:], 0.0, t[:, 2], ALU.max, ALU.add))
            chain(nc.vector.tensor_scalar(g[:], g[:], 1e-4, None, ALU.add))
            chain(nc.vector.reciprocal(g[:], g[:]))
            chain(nc.vector.tensor_scalar(K["scb"][:], K["scb"][:], 1.0 / 127.0, None, ALU.mult))
            for w in range(2):
                chain(nc.vector.tensor_tensor(K["rope"][:, w], K["rope"][:, w], K["nw"][:, w].unsqueeze(1).broadcast_to([P, T4, 2, DH]), ALU.mult))
            chain(nc.vector.tensor_copy(K["identb"][:], K["ident"][:]))
            chain(nc.vector.tensor_copy(K["maskb"][:], K["mask"][:]))


def layouts(a):
    q, b = "L0_attn_a_", "L0_attn_b_"
    a = {k: np.asarray(v, np.float32) for k, v in a.items()}
    k = np.arange(P)
    same = k[:, None] // CH == k[None, :] // CH
    f = np.float32
    angles = np.arange(L, dtype=f)[:, None] * (f(1.0) / f(10000.0) ** (np.arange(0, DH, 2, dtype=f) / f(DH)))
    cos, sin = np.cos(angles).astype(f), np.sin(angles).astype(f)
    turn = np.stack([np.concatenate([cos, cos], 1), np.concatenate([-sin, sin], 1)], 1)
    turn = turn.reshape(T4, P, 2, DH).transpose(1, 0, 2, 3)
    wide = lambda v, *s: np.ascontiguousarray(np.broadcast_to(v, (P, *s)))
    nws = [a[b + "k_norm_w"], a[b + "q_norm_w"]]
    nw = np.stack([np.stack([w, np.concatenate([w[32:], w[:32]])]) for w in nws])
    z = np.zeros((H, 2 * P + 64), f)
    z[:, P - 1:P - 1 + FL] = a[q + "fir_long_w"].reshape(H, FL)[:, ::-1]
    return dict(
        x=a[q + "hidden_states"].reshape(B * L, H),
        wqkv=np.stack([a[q + "Wq"], a[q + "Wk"], a[q + "Wv"]], 1), wb=a[q + "Wb"],
        cw=np.stack([a[q + f"conv_{n}_w"] for n in "qkv"], 1), fsw=a[q + "fir_short_w"].reshape(H, FS),
        ident=np.eye(P, dtype=f), anti=np.eye(P, dtype=f)[::-1].copy(), blk=same.astype(f), causal=(same & (k[:, None] <= k[None, :])).astype(f),
        eps6=np.full((P, 1), 1e-6, f), fir_z=z,
        b1=a[q + "mlp_b1"].reshape(2, P).T.copy(), b2=a[q + "mlp_b2"].reshape(1, 16),
        w1x=a[q + "mlp_w1"][:H], w1s=a[q + "mlp_w1"][H:], w2=a[q + "mlp_w2"].reshape(2, P, 16).transpose(1, 0, 2).copy(),
        ones=np.ones((1, P), f), wo_a=a[q + "Wo"], cbT=a["L0_ffn_CB"].T.copy(), scb=wide(a["L0_ffn_SCB"], H), bias=wide(a["L0_ffn_bias"], H),
        onorm=wide(a[q + "o_norm_w"], DK), rtemp=wide(np.repeat(a[q + "gate_log_temp"], 4), 16),
        wqkvT=a[b + "wqkv"].T.copy(), woT=a[b + "wo"].T.reshape(HA // 2, P, H).transpose(1, 0, 2).copy(),
        rope=np.ascontiguousarray(np.broadcast_to(turn[:, None], (P, 2, T4, 2, DH))), nw=wide(nw, 2, 2, DH),
        mask=np.where(k[:, None] >= k[None, :], f(0), f(-1e30)).astype(f),
    )


def kernel(**inputs):
    import concourse.bacc as bacc
    from concourse.bass_utils import run_bass_kernel_spmd

    nc = bacc.Bacc("TRN2", target_bir_lowering=False, num_devices=1)
    arrays = {f"in_{n}": v for n, v in layouts(inputs).items()}
    d = {n[3:]: nc.dram_tensor(n, v.shape, mybir.dt.from_np(v.dtype), kind="ExternalInput").ap() for n, v in arrays.items()}
    out = nc.dram_tensor("out_x", (B * L, H), F32, kind="ExternalOutput").ap()
    d["x"] = d["x"].rearrange("(n p) c -> p n c", p=P)
    build_kernel(nc, d, out.rearrange("(n p) c -> p n c", p=P))
    r = run_bass_kernel_spmd(nc, [arrays], core_ids=[0])
    return r.results[0]["out_x"].reshape(B, L, H)
```

```python
from contextlib import ExitStack

import numpy as np

import concourse.bass as bass
from concourse import mybir

F32 = mybir.dt.float32
F16 = mybir.dt.float16
BF16 = mybir.dt.bfloat16
ALU = mybir.AluOpType
ACT = mybir.ActivationFunctionType
AX = mybir.AxisListType

P = 128
B, L, H = 8, 512, 128
TILES = B * L // P
NH, DK = 4, 32
CH = 32
PAIR = 2
PT = PAIR * L // P
PTOK = PAIR * L
PC = PTOK // CH
ROUNDS = B // PAIR
STEPS = L // CH
CONV = 4
FS, FL = 3, 63
EPS_LN = 1e-5


class Signal:

    def __init__(self, sem, per):
        self.sem, self.per = sem, per

    def at(self, it, k=None):
        return it * self.per + (self.per if k is None else k)


class Chain:

    def __init__(self, sem, per):
        self.sem, self.per, self.k = sem, per, 0

    def next(self):
        self.k += 1
        return self.k



def delta_phase(nc, d, keep):
    with ExitStack() as ctx:
        def sb(name, shape, dt=F32):
            return ctx.enter_context(nc.sbuf_tensor(name, shape, dt))

        def signal(name, per):
            return Signal(ctx.enter_context(nc.semaphore(name)), per)

        x_in = sb("x_in", [P, PT, H])
        stats = sb("stats", [P, PT, 6])
        mv = sb("mv", [P, PT, 2])
        rstd = sb("rstd", [P, PT])
        xn = sb("xn", [P, PT, H])
        xT = sb("xT", [H, PTOK])
        pre = [sb(f"pre_{n}", [H, PAIR, CONV - 1 + L]) for n in "qkv"]
        con = [sb(f"con_{n}", [H, PAIR, L]) for n in "qkv"]
        vpad = sb("vpad", [H, PAIR, FS - 1 + L])
        fir = sb("fir", [H, PAIR, L])
        sq = sb("sq", [H, 2, PTOK])
        kT = sb("kT", [H, PTOK])
        beta = sb("beta", [P, PT, NH])
        VK = sb("VK", [P, PT, NH, 2, DK])
        M = sb("M", [P, PT, NH, CH])
        A = sb("A", [P, CH, CH])
        X = sb("X", [P, CH, CH])
        tmp = sb("tmp", [P, CH * CH])
        TT = sb("TT", [P, PT * NH, P])
        UW = sb("UW", [P, PT, 2, NH * DK])
        uT = sb("uT", [H, PTOK])
        WQ = sb("WQ", [H, PC, 2, CH])
        kx = sb("kx", [P, PC, NH * DK])
        Sx = sb("Sx", [P, PAIR, NH * DK])
        u2T = sb("u2T", [H, PTOK])
        qsT = sb("qsT", [H, PTOK])
        u2h = sb("u2h", [P, PAIR, DK])
        u2tok = xn
        AT = sb("AT", [P, 4, NH, P])
        qstok = x_in
        zero = sb("zero", [P, PAIR * DK])
        ps01 = ctx.enter_context(nc.psum_tensor("ps01", [P, 2, 512], F32))
        ps23 = ctx.enter_context(nc.psum_tensor("ps23", [P, 2, 512], F32))
        ps47 = ctx.enter_context(nc.psum_tensor("ps47", [P, 4, 512], F32))
        wqkv, wb, cw, fsw, ident, blk, causal = (keep[n] for n in ("wqkv", "wb", "cw", "fsw", "ident", "blk", "causal"))
        v_tok, d_tok, fs_tok = keep["v_tok"], keep["d_tok"], keep["fs_tok"]

        x_loaded = signal("x_loaded", 16)
        cleared = signal("cleared", 6)
        dv = Chain(ctx.enter_context(nc.semaphore("dve_step")), 98)
        ac = Chain(ctx.enter_context(nc.semaphore("act_step")), 90)
        std_ready = signal("std_ready", 1)
        xn_std = signal("xn_std", 1)
        xn_ready = signal("xn_ready", 1)
        xT_ps = signal("xT_ps", 1)
        xT_ready = signal("xT_ready", 1)
        proj_ps = signal("proj_ps", 3)
        pre_ready = signal("pre_ready", 3)
        beta_ps = signal("beta_ps", 1)
        beta_ready = signal("beta_ready", 1)
        con_ready = signal("con_ready", 3)
        silu_ready = signal("silu_ready", 3)
        sq_ready = signal("sq_ready", 2)
        ss_ps = signal("ss_ps", 2)
        norm_ready = signal("norm_ready", 2)
        qk_ready = signal("qk_ready", 2)
        fir_ready = signal("fir_ready", 1)
        tok_ps = signal("tok_ps", 3)
        tok_out = signal("tok_out", 3)
        kk_ps = signal("kk_ps", 2)
        kk_used = signal("kk_used", 2)
        TT_ready = signal("TT_ready", 1)
        kx_ready = signal("kx_ready", 1)
        UW_ps = signal("UW_ps", 2)
        UW_ready = signal("UW_ready", 4)
        UWT_ps = signal("UWT_ps", 2)
        UWT_ready = signal("UWT_ready", 2)
        WS_ps = signal("WS_ps", STEPS)
        u2_ready = signal("u2_ready", STEPS)
        qs_ready = signal("qs_ready", STEPS)
        S_ps = signal("S_ps", STEPS)
        S_ready = signal("S_ready", STEPS)
        S_zero = signal("S_zero", 1)
        u2t_ps = signal("u2t_ps", 1)
        u2t_ready = signal("u2t_ready", 1)
        qst_ps = signal("qst_ps", 1)
        qst_ready = signal("qst_ready", 1)
        qk_ps = signal("qk_ps", 2)
        AT_ready = signal("AT_ready", 2)
        o_ps = signal("o_ps", 2)
        o_ready = signal("o_ready", 1)
        everything = [x_loaded, std_ready, xn_ready, xT_ready, pre_ready, beta_ready, con_ready, silu_ready,
                      qk_ready, fir_ready, tok_out, kk_used, TT_ready, kx_ready, UW_ready, UWT_ready,
                      u2_ready, qs_ready, S_ready, u2t_ready, qst_ready, AT_ready, o_ready, o_ps]

        block = ctx.enter_context(nc.Block())

        def round_over(eng, it):
            for s in everything:
                eng.wait_ge(s.sem, s.at(it))

        @block.gpsimd
        def _(pool):
            for t in (*pre, vpad):
                nc.gpsimd.memset(t[:, :, 0:CONV - 1 if t is not vpad else FS - 1], 0.0).then_inc(cleared.sem, 1)
            nc.gpsimd.memset(TT[:], 0.0).then_inc(cleared.sem, 1)
            nc.gpsimd.memset(kx[:], 0.0).then_inc(cleared.sem, 1)
            pool.wait_ge(cleared.sem, 6)
            nc.gpsimd.memset(zero[:], 0.0).then_inc(cleared.sem, 1)
            with pool.Fori(0, ROUNDS) as it:
                nc.gpsimd.memset(Sx[:], 0.0).then_inc(S_zero.sem, 1)
                round_over(pool, it)

        @block.scalar
        def _(act):
            act.wait_ge(cleared.sem, 7)

            def chain(ins, it):
                k = ac.next()
                ins.then_inc(ac.sem, 1)
                act.wait_ge(ac.sem, it * ac.per + k)

            with act.Fori(0, ROUNDS) as it:
                act.dma_start(x_in[:], d["x"][:, bass.ds(it * PT, PT), :]).then_inc(x_loaded.sem, 16)
                act.wait_ge(std_ready.sem, std_ready.at(it))
                nc.scalar.activation(rstd[:], rstd[:], ACT.Sqrt).then_inc(xn_std.sem, 1)
                act.wait_ge(xT_ps.sem, xT_ps.at(it))
                nc.scalar.activation(xT[:], ps01[:].rearrange("p a b -> p (a b)"), ACT.Copy).then_inc(xT_ready.sem, 1)
                for i, ps in enumerate((ps23, ps47[:, 0:2], ps47[:, 2:4])):
                    act.wait_ge(proj_ps.sem, proj_ps.at(it, i + 1))
                    nc.scalar.activation(pre[i][:, :, CONV - 1:], ps[:] if i == 0 else ps, ACT.Copy).then_inc(pre_ready.sem, 1)
                act.wait_ge(beta_ps.sem, beta_ps.at(it))
                nc.scalar.activation(beta[:].rearrange("p a b -> p (a b)"), ps01[:, 0, 0:PT * NH], ACT.Sigmoid).then_inc(beta_ready.sem, 1)
                for i in range(3):
                    act.wait_ge(con_ready.sem, con_ready.at(it, i + 1))
                    dst = vpad[:, :, FS - 1:] if i == 2 else con[i][:]
                    nc.scalar.activation(dst, con[i][:], ACT.Silu).then_inc(silu_ready.sem, 1)
                    if i < 2:
                        act.wait_ge(silu_ready.sem, silu_ready.at(it, i + 1))
                        nc.scalar.activation(sq[:, i, :], con[i][:].rearrange("p a b -> p (a b)"), ACT.Square).then_inc(sq_ready.sem, 1)
                for i, ps in enumerate((ps23, ps01)):
                    act.wait_ge(ss_ps.sem, ss_ps.at(it, i + 1))
                    nc.scalar.activation(sq[:, i, :], ps[:].rearrange("p a b -> p (a b)"), ACT.Sqrt, bias=keep["eps6"][:, 0:1]).then_inc(norm_ready.sem, 1)
                act.wait_ge(tok_ps.sem, tok_ps.at(it, 1))
                nc.scalar.activation(v_tok[:, bass.ds(it * PT, PT), :], ps23[:].rearrange("p a (b c) -> p (a b) c", c=H), ACT.Copy).then_inc(tok_out.sem, 1)
                act.wait_ge(tok_ps.sem, tok_ps.at(it, 3))
                nc.scalar.activation(fs_tok[:, bass.ds(it * PT, PT), :], ps23[:].rearrange("p a (b c) -> p (a b) c", c=H), ACT.Copy).then_inc(tok_out.sem, 1)
                for hf in range(2):
                    act.wait_ge(UW_ps.sem, UW_ps.at(it, hf + 1))
                    for w in range(2):
                        nc.scalar.activation(
                            UW[:, 4 * hf:4 * hf + 4, w, :].rearrange("p t (h c) -> p t h c", h=NH),
                            ps47[:, 2 * hf:2 * hf + 2].rearrange("p a (t h w c) -> p (a t) h w c", h=NH, w=2, c=DK)[:, :, :, w, :],
                            ACT.Copy).then_inc(UW_ready.sem, 1)
                act.wait_ge(UWT_ps.sem, UWT_ps.at(it, 1))
                nc.scalar.activation(uT[:], ps01[:].rearrange("p a b -> p (a b)"), ACT.Copy).then_inc(UWT_ready.sem, 1)
                act.wait_ge(UWT_ps.sem, UWT_ps.at(it, 2))
                nc.scalar.activation(WQ[:, :, 0, :], ps23[:].rearrange("p a (x c) -> p (a x) c", c=CH), ACT.Copy).then_inc(UWT_ready.sem, 1)
                for n in range(STEPS):
                    act.wait_ge(u2_ready.sem, u2_ready.at(it, n + 1))
                    nc.scalar.activation(
                        qsT[:].rearrange("p (s x) -> p s x", s=PAIR)[:, :, n * CH:(n + 1) * CH],
                        ps01[:, n % 2, 0:PAIR * 64].rearrange("p (s x) -> p s x", s=PAIR)[:, :, 32:64], ACT.Copy).then_inc(qs_ready.sem, 1)
                act.wait_ge(u2t_ps.sem, u2t_ps.at(it))
                nc.scalar.activation(u2tok[:].rearrange("p a b -> p (a b)"), ps01[:].rearrange("p a b -> p (a b)"), ACT.Copy).then_inc(u2t_ready.sem, 1)
                act.wait_ge(qst_ps.sem, qst_ps.at(it))
                nc.scalar.activation(qstok[:].rearrange("p a b -> p (a b)"), ps23[:].rearrange("p a b -> p (a b)"), ACT.Copy).then_inc(qst_ready.sem, 1)
                round_over(act, it)

        @block.vector
        def _(dve):
            dve.wait_ge(cleared.sem, 7)

            def chain(ins, it):
                k = dv.next()
                ins.then_inc(dv.sem, 1)
                dve.wait_ge(dv.sem, it * dv.per + k)

            with dve.Fori(0, ROUNDS) as it:
                dve.wait_ge(x_loaded.sem, x_loaded.at(it))
                for t in range(PT):
                    last = nc.vector.bn_stats(stats[:, t, :], x_in[:, t, :])
                chain(last, it)
                nc.vector.memset(keep["still"][:], 0.0)
                for t in range(PT):
                    last = nc.vector.bn_aggr(mv[:, t, :], stats[:, t, :])
                chain(last, it)
                nc.vector.tensor_scalar(rstd[:], mv[:, :, 1], EPS_LN, None, ALU.add).then_inc(std_ready.sem, 1)
                dve.wait_ge(xn_std.sem, xn_std.at(it))
                chain(nc.vector.reciprocal(rstd[:], rstd[:]), it)
                for t in range(PT):
                    last = nc.vector.tensor_scalar(xn[:, t, :], x_in[:, t, :], mv[:, t, 0:1], rstd[:, t:t + 1], ALU.subtract, ALU.mult)
                last.then_inc(xn_ready.sem, 1)
                for i in range(3):
                    dve.wait_ge(pre_ready.sem, pre_ready.at(it, i + 1))
                    for j in range(CONV):
                        w = cw[:, i, j:j + 1]
                        if j == 0:
                            chain(nc.vector.tensor_scalar(con[i][:], pre[i][:, :, j:j + L], w, None, ALU.mult), it)
                        else:
                            ins = nc.vector.scalar_tensor_tensor(con[i][:], pre[i][:, :, j:j + L], w, con[i][:], ALU.mult, ALU.add)
                            if j < CONV - 1:
                                chain(ins, it)
                    ins.then_inc(con_ready.sem, 1)
                dve.wait_ge(silu_ready.sem, silu_ready.at(it, 3))
                for j in range(FS):
                    w = fsw[:, j:j + 1]
                    if j == 0:
                        chain(nc.vector.tensor_scalar(fir[:], vpad[:, :, j:j + L], w, None, ALU.mult), it)
                    else:
                        ins = nc.vector.scalar_tensor_tensor(fir[:], vpad[:, :, j:j + L], w, fir[:], ALU.mult, ALU.add)
                        if j < FS - 1:
                            chain(ins, it)
                ins.then_inc(fir_ready.sem, 1)
                for i in range(2):
                    dve.wait_ge(norm_ready.sem, norm_ready.at(it, i + 1))
                    chain(nc.vector.reciprocal(sq[:, i, :], sq[:, i, :]), it)
                    if i == 0:
                        dst, a, b_ = WQ[:, :, 1, :], con[0][:].rearrange("p s (n c) -> p (s n) c", c=CH), sq[:, 0, :].rearrange("p (n c) -> p n c", c=CH)
                    else:
                        dst, a, b_ = kT[:], con[1][:].rearrange("p s n -> p (s n)"), sq[:, 1, :]
                    nc.vector.tensor_tensor(dst, a, b_, ALU.mult).then_inc(qk_ready.sem, 1)
                dve.wait_ge(beta_ready.sem, beta_ready.at(it))
                dve.wait_ge(tok_out.sem, tok_out.at(it, 1))
                bb = beta[:].rearrange("p t h -> p (t h)").unsqueeze(2).broadcast_to([P, PT * NH, DK])
                chain(nc.vector.tensor_tensor(VK[:, :, :, 0, :].rearrange("p t h c -> p (t h) c"),
                                        ps23[:].rearrange("p a (b c) -> p (a b) c", c=DK), bb, ALU.mult), it)
                dve.wait_ge(tok_ps.sem, tok_ps.at(it, 2))
                nc.vector.tensor_tensor(VK[:, :, :, 1, :].rearrange("p t h c -> p (t h) c"),
                                        ps01[:].rearrange("p a (b c) -> p (a b) c", c=DK), bb, ALU.mult).then_inc(tok_out.sem, 1)
                dve.wait_ge(qk_ready.sem, qk_ready.at(it, 2))
                for h in range(NH):
                    last = nc.vector.transpose(kx[DK * h:DK * h + DK, :, DK * h:DK * h + DK],
                                               kT[DK * h:DK * h + DK, :].rearrange("p (n c) -> p n c", c=CH))
                last.then_inc(kx_ready.sem, 1)
                for hf in range(2):
                    dve.wait_ge(kk_ps.sem, kk_ps.at(it, hf + 1))
                    for c in range(4):
                        q = slice(CH * c, CH * c + CH)
                        last = nc.vector.tensor_tensor(
                            M[q, 4 * hf:4 * hf + 4].rearrange("p t h c -> p h t c"),
                            ps47[q, :, :].rearrange("p h (t c) -> p h t c", t=4)[:, :, :, CH * c:CH * c + CH],
                            beta[q, 4 * hf:4 * hf + 4].rearrange("p t h -> p h t").unsqueeze(3).broadcast_to([CH, NH, 4, CH]), ALU.mult)
                    last.then_inc(kk_used.sem, 1)
                dve.wait_ge(kk_used.sem, kk_used.at(it, 2))
                nc.vector.memset(X[:], 0.0).then_inc(dv.sem, 1)
                dv.next()
                nc.vector.transpose(A[:], M[:].rearrange("p t h j -> p j (t h)")).then_inc(dv.sem, 1)
                dv.next()
                dve.wait_ge(dv.sem, it * dv.per + dv.k)
                chain(nc.vector.memset(X[:].rearrange("p a b -> p (a b)")[:, 0:CH * CH:CH + 1], 1.0), it)
                for j in range(CH - 1):
                    r, c = CH - 1 - j, j + 1
                    t3 = tmp[:, 0:r * c].rearrange("p (r c) -> p r c", c=c)
                    chain(nc.vector.tensor_tensor(t3, A[:, j, j + 1:].unsqueeze(2).broadcast_to([P, r, c]),
                                                  X[:, j:j + 1, 0:c].broadcast_to([P, r, c]), ALU.mult), it)
                    chain(nc.vector.tensor_tensor(X[:, j + 1:, 0:c], X[:, j + 1:, 0:c], t3, ALU.subtract), it)
                for c in range(4):
                    q = slice(CH * c, CH * c + CH)
                    last = nc.vector.transpose(TT[q, :, CH * c:CH * c + CH].rearrange("p b i -> p i b"), X[q, :, :])
                last.then_inc(TT_ready.sem, 1)
                dve.wait_ge(UWT_ready.sem, UWT_ready.at(it, 2))
                for n in range(STEPS):
                    dve.wait_ge(WS_ps.sem, WS_ps.at(it, n + 1))
                    u3 = u2T[:].rearrange("p (s x) -> p s x", s=PAIR)[:, :, n * CH:(n + 1) * CH]
                    chain(nc.vector.tensor_tensor(
                        u3, uT[:].rearrange("p (s x) -> p s x", s=PAIR)[:, :, n * CH:(n + 1) * CH],
                        ps01[:, n % 2, 0:PAIR * 64].rearrange("p (s x) -> p s x", s=PAIR)[:, :, 0:32], ALU.subtract), it)
                    if n:
                        dve.wait_ge(S_ps.sem, S_ps.at(it, n))
                    nc.vector.transpose(u2h[:], u3).then_inc(u2_ready.sem, 1)
                    dve.wait_ge(S_ps.sem, S_ps.at(it, n + 1))
                    for h in range(NH):
                        last = nc.vector.tensor_copy(
                            Sx[DK * h:DK * h + DK, :, DK * h:DK * h + DK],
                            ps23[DK * h:DK * h + DK, 0, 0:PAIR * DK].rearrange("p (s x) -> p s x", s=PAIR))
                    last.then_inc(S_ready.sem, 1)
                for hf in range(2):
                    dve.wait_ge(qk_ps.sem, qk_ps.at(it, hf + 1))
                    if hf:
                        dve.wait_ge(o_ps.sem, o_ps.at(it, 1))
                    for h in range(NH):
                        last = nc.vector.tensor_tensor(
                            AT[:, :, h, :], ps47[:, h, :].rearrange("p (t i) -> p t i", t=4),
                            causal[:].unsqueeze(1).broadcast_to([P, 4, P]), ALU.mult)
                    last.then_inc(AT_ready.sem, 1)
                dve.wait_ge(o_ps.sem, o_ps.at(it, 2))
                dve.wait_ge(qst_ready.sem, qst_ready.at(it))
                nc.vector.tensor_tensor(d_tok[:, bass.ds(it * PT, PT), :], ps01[:].rearrange("p a (b c) -> p (a b) c", c=H),
                                        qstok[:], ALU.add).then_inc(o_ready.sem, 1)
                round_over(dve, it)
            assert dv.k == dv.per, dv.k

        @block.tensor
        def _(pe):
            pe.wait_ge(cleared.sem, 7)
            with pe.Fori(0, ROUNDS) as it:
                pe.wait_ge(xn_ready.sem, xn_ready.at(it))
                for t in range(PT):
                    last = nc.tensor.transpose(ps01[:, t // 4, P * (t % 4):P * (t % 4) + P], xn[:, t, :], ident[:])
                last.then_inc(xT_ps.sem, 1)
                pe.wait_ge(xT_ready.sem, xT_ready.at(it))
                for i, ps in enumerate((ps23[:, 0:2], ps47[:, 0:2], ps47[:, 2:4])):
                    for s in range(PAIR):
                        last = nc.tensor.matmul(ps[:, s, :], wqkv[:, i, :], xT[:, s * L:(s + 1) * L], start=True, stop=True)
                    last.then_inc(proj_ps.sem, 1)
                for t in range(PT):
                    last = nc.tensor.matmul(ps01[:, 0, t * NH:(t + 1) * NH], xT[:, t * P:(t + 1) * P], wb[:], start=True, stop=True)
                last.then_inc(beta_ps.sem, 1)
                for i, ps in enumerate((ps23, ps01)):
                    pe.wait_ge(sq_ready.sem, sq_ready.at(it, i + 1))
                    if i == 0:
                        pe.wait_ge(pre_ready.sem, pre_ready.at(it, 1))
                    else:
                        pe.wait_ge(beta_ready.sem, beta_ready.at(it))
                    for s in range(PAIR):
                        last = nc.tensor.matmul(ps[:, s, :], blk[:], sq[:, i, s * L:(s + 1) * L], start=True, stop=True)
                    last.then_inc(ss_ps.sem, 1)
                pe.wait_ge(silu_ready.sem, silu_ready.at(it, 3))
                pe.wait_ge(norm_ready.sem, norm_ready.at(it, 1))
                for t in range(PT):
                    last = nc.tensor.transpose(ps23[:, t // 4, P * (t % 4):P * (t % 4) + P], vpad[:, t // 4, FS - 1 + P * (t % 4):FS - 1 + P * (t % 4) + P], ident[:])
                last.then_inc(tok_ps.sem, 1)
                pe.wait_ge(qk_ready.sem, qk_ready.at(it, 2))
                for t in range(PT):
                    last = nc.tensor.transpose(ps01[:, t // 4, P * (t % 4):P * (t % 4) + P], kT[:, t * P:(t + 1) * P], ident[:])
                last.then_inc(tok_ps.sem, 1)
                pe.wait_ge(pre_ready.sem, pre_ready.at(it, 3))
                for hf in range(2):
                    if hf:
                        pe.wait_ge(kk_used.sem, kk_used.at(it, 1))
                    for h in range(NH):
                        q = slice(DK * h, DK * h + DK)
                        for t in range(4):
                            s = slice((4 * hf + t) * P, (4 * hf + t + 1) * P)
                            last = nc.tensor.matmul(ps47[:, h, t * P:(t + 1) * P], kT[q, s], kT[q, s], start=True, stop=True)
                    last.then_inc(kk_ps.sem, 1)
                pe.wait_ge(fir_ready.sem, fir_ready.at(it))
                pe.wait_ge(tok_out.sem, tok_out.at(it, 2))
                for t in range(PT):
                    last = nc.tensor.transpose(ps23[:, t // 4, P * (t % 4):P * (t % 4) + P], fir[:, t // 4, P * (t % 4):P * (t % 4) + P], ident[:])
                last.then_inc(tok_ps.sem, 1)
                pe.wait_ge(TT_ready.sem, TT_ready.at(it))
                pe.wait_ge(kk_used.sem, kk_used.at(it, 2))
                for hf in range(2):
                    for t in range(4):
                        for h in range(NH):
                            g = (4 * hf + t) * NH + h
                            last = nc.tensor.matmul(ps47[:, g // 8, 64 * (g % 8):64 * (g % 8) + 64], TT[:, g, :],
                                                    VK[:, g // NH, h].rearrange("p w c -> p (w c)"), start=True, stop=True)
                    last.then_inc(UW_ps.sem, 1)
                pe.wait_ge(UW_ready.sem, UW_ready.at(it, 4))
                pe.wait_ge(tok_out.sem, tok_out.at(it, 3))
                for w, ps in enumerate((ps01, ps23)):
                    for t in range(PT):
                        last = nc.tensor.transpose(ps[:, t // 4, P * (t % 4):P * (t % 4) + P], UW[:, t, w, :], ident[:])
                    last.then_inc(UWT_ps.sem, 1)
                pe.wait_ge(UWT_ready.sem, UWT_ready.at(it, 2))
                pe.wait_ge(S_zero.sem, S_zero.at(it))
                pe.wait_ge(kx_ready.sem, kx_ready.at(it))
                nc.tensor.matmul(ps23[:, 0, 0:PAIR * DK], ident[:], zero[:], start=True, stop=False, skip_group_check=True)
                for n in range(STEPS):
                    if n:
                        pe.wait_ge(S_ready.sem, S_ready.at(it, n))
                    if n >= 2:
                        pe.wait_ge(qs_ready.sem, qs_ready.at(it, n - 1))
                    for s in range(PAIR):
                        last = nc.tensor.matmul(ps01[:, n % 2, 64 * s:64 * s + 64], Sx[:, s, :],
                                                WQ[:, s * STEPS + n].rearrange("p w c -> p (w c)"), start=True, stop=True)
                    last.then_inc(WS_ps.sem, 1)
                    pe.wait_ge(u2_ready.sem, u2_ready.at(it, n + 1))
                    for s in range(PAIR):
                        last = nc.tensor.matmul(ps23[:, 0, DK * s:DK * s + DK], kx[:, s * STEPS + n, :], u2h[:, s, :],
                                                start=False, stop=n == STEPS - 1 and s == PAIR - 1, skip_group_check=True)
                    last.then_inc(S_ps.sem, 1)
                pe.wait_ge(qs_ready.sem, qs_ready.at(it))
                for t in range(PT):
                    last = nc.tensor.transpose(ps01[:, t // 4, P * (t % 4):P * (t % 4) + P], u2T[:, t * P:(t + 1) * P], ident[:])
                last.then_inc(u2t_ps.sem, 1)
                pe.wait_ge(S_ready.sem, S_ready.at(it))
                for t in range(PT):
                    last = nc.tensor.transpose(ps23[:, t // 4, P * (t % 4):P * (t % 4) + P], qsT[:, t * P:(t + 1) * P], ident[:])
                last.then_inc(qst_ps.sem, 1)
                for hf in range(2):
                    if hf:
                        pe.wait_ge(AT_ready.sem, AT_ready.at(it, 1))
                    for h in range(NH):
                        q = slice(DK * h, DK * h + DK)
                        for t in range(4):
                            g = 4 * hf + t
                            last = nc.tensor.matmul(ps47[:, h, t * P:(t + 1) * P].rearrange("p (n c) -> p n c", c=CH), kT[q, g * P:(g + 1) * P],
                                                    WQ[q, 4 * g:4 * g + 4, 1, :], start=True, stop=True)
                    last.then_inc(qk_ps.sem, 1)
                    pe.wait_ge(AT_ready.sem, AT_ready.at(it, hf + 1))
                    pe.wait_ge(u2t_ready.sem, u2t_ready.at(it))
                    for t in range(4):
                        for h in range(NH):
                            last = nc.tensor.matmul(ps01[:, hf, t * P + h * DK:t * P + h * DK + DK], AT[:, t, h, :],
                                                    u2tok[:, 4 * hf + t, h * DK:(h + 1) * DK], start=True, stop=True)
                    last.then_inc(o_ps.sem, 1)
                round_over(pe, it)


HA, DH = 16, 64
T4 = L // P
MH = 256
EPS_RMS = 1e-6
UNITS = HA * T4


def fir_phase(nc, d, keep, loads):
    G = 16
    GROUPS = H // G
    with ExitStack() as ctx:
        def signal(name, per):
            return Signal(ctx.enter_context(nc.semaphore(name)), per)

        band = [ctx.enter_context(nc.sbuf_tensor(f"band{i}", [P, G, P + 64], F32)) for i in range(2)]
        v_back = ctx.enter_context(nc.sbuf_tensor("v_back", [P, TILES, H], F32))
        ps = [ctx.enter_context(nc.psum_tensor(f"fir_ps{i}", [P, TILES, G], F32)) for i in range(2)]
        back_ps = ctx.enter_context(nc.psum_tensor("back_ps", [P, 4, 4, H], F32))
        v_tok, fl_tok, anti = keep["v_tok"], keep["fl_tok"], keep["anti"]
        band_in = [signal(f"band_in{i}", 16) for i in range(2)]
        turned = signal("turned", 0)
        back = signal("back", 0)
        fir_ps = signal("fir_ps", 2)
        fir_free = signal("fir_free", 2)
        weights_in = signal("weights_in", 0)
        block = ctx.enter_context(nc.Block())
        z = d["fir_z"]
        width = z.shape[1]

        @block.sync
        def _(sp):
            for g in range(GROUPS):
                if g >= 2:
                    sp.wait_ge(fir_ps.sem, g - 1)
                src = bass.AP(z.tensor, g * G * width, [[1, P], [width, G], [1, P + 64]])
                sp.dma_start(band[g % 2][:], src).then_inc(band_in[g % 2].sem, 16)
            for n in loads:
                sp.dma_start(keep[n][:], d[n]).then_inc(weights_in.sem, 16)
            for s in band_in:
                sp.wait_ge(s.sem, 16 * (GROUPS // 2))
            sp.wait_ge(weights_in.sem, 16 * len(loads))

        @block.tensor
        def _(pe):
            for g in range(TILES // 4):
                if g >= 4:
                    pe.wait_ge(back.sem, g - 3)
                nc.tensor.matmul(back_ps[:, g % 4], anti[:], v_tok[:, 4 * g:4 * g + 4, :], start=True, stop=True).then_inc(turned.sem, 1)
            with pe.Fori(0, GROUPS // 2) as it:
                for i in range(2):
                    pe.wait_ge(band_in[i].sem, it * 16 + 16)
                    pe.wait_ge(fir_free.sem, it * 2 + 1)
                    for c in range(G):
                        v1 = v_back[:, :, bass.ds((it * 2 + i) * G + c, 1)]
                        nc.tensor.matmul(ps[i][:, :, c], band[i][:, c, 0:P], v1.rearrange("p t c -> p (t c)"),
                                         start=True, stop=False, skip_group_check=True)
                        last = nc.tensor.matmul(
                            ps[i][0:64, :, c].rearrange("p (b n) -> p b n", n=T4)[:, :, 1:], band[i][:, c, P:P + 64],
                            v1.rearrange("p (b n) c -> p b (n c)", n=T4)[:, :, 0:T4 - 1],
                            start=False, stop=True, skip_group_check=True)
                    last.then_inc(fir_ps.sem, 1)

        @block.scalar
        def _(act):
            for g in range(TILES // 4):
                act.wait_ge(turned.sem, g + 1)
                nc.scalar.activation(v_back[:, 4 * g:4 * g + 4, :], back_ps[:, g % 4], ACT.Copy).then_inc(
                    back.sem if g < TILES // 4 - 1 else fir_free.sem, 1)
            with act.Fori(0, GROUPS // 2) as it:
                for i in range(2):
                    act.wait_ge(fir_ps.sem, it * 2 + i + 1)
                    nc.scalar.activation(fl_tok[:, :, bass.ds((it * 2 + i) * G, G)], ps[i][:], ACT.Copy).then_inc(fir_free.sem, 1)


class Normer:

    def __init__(self, nc, ctx, name, norms, steps, ident, still, eps):
        def sb(part, shape):
            return ctx.enter_context(nc.sbuf_tensor(f"{name}_{part}", shape, F32))

        def signal(part, per):
            return Signal(ctx.enter_context(nc.semaphore(f"{name}_{part}")), per)

        self.nc, self.ident, self.still, self.eps = nc, ident, still, eps
        self.st6, self.mv, self.std, self.z = sb("st6", [P, PAIR, T4, 6]), sb("mv", [P, PAIR, T4, 2]), sb("std", [P, PAIR, T4]), sb("z", [P, PAIR, T4, H])
        self.aggregated = signal("aggregated", PAIR * norms)
        self.std_ready = signal("std_ready", PAIR * norms)
        self.z_ready = signal("z_ready", PAIR * norms)
        self.zT_ps = signal("zT_ps", PAIR * norms)
        self.zT_ready = signal("zT_ready", PAIR * norms)
        self.steps = Chain(ctx.enter_context(nc.semaphore(f"{name}_dve")), steps)

    def all(self):
        return [self.z_ready, self.std_ready, self.zT_ready]

    def step(self, ins):
        ins.then_inc(self.steps.sem, 1)
        return self.steps.next()

    def need(self, dve, it, k):
        dve.wait_ge(self.steps.sem, it * self.steps.per + k)

    def vector(self, dve, it, n, xs):
        nc = self.nc
        done = [0] * PAIR
        nc.vector.memset(self.still[:, PAIR:PAIR + 1], 0.0)
        for s in range(PAIR):
            for t in range(T4):
                last = nc.vector.bn_stats(self.st6[:, s, t, :], xs(s)[:, t, :])
            done[s] = self.step(last)
        for s in range(PAIR):
            self.need(dve, it, done[s])
            nc.vector.memset(self.still[:, s:s + 1], 0.0)
            for t in range(T4):
                last = nc.vector.bn_aggr(self.mv[:, s, t, :], self.st6[:, s, t, :])
            last.then_inc(self.aggregated.sem, 1)
        for s in range(PAIR):
            dve.wait_ge(self.std_ready.sem, self.std_ready.at(it, PAIR * n + s + 1))
            done[s] = self.step(nc.vector.reciprocal(self.std[:, s], self.std[:, s]))
        for s in range(PAIR):
            self.need(dve, it, done[s])
            for t in range(T4):
                last = nc.vector.tensor_scalar(self.z[:, s, t, :], xs(s)[:, t, :], self.mv[:, s, t, 0:1], self.std[:, s, t:t + 1], ALU.subtract, ALU.mult)
            last.then_inc(self.z_ready.sem, 1)

    def scalar(self, act, it, n):
        for s in range(PAIR):
            act.wait_ge(self.aggregated.sem, self.aggregated.at(it, PAIR * n + s + 1))
            self.nc.scalar.activation(self.std[:, s], self.mv[:, s, :, 1], ACT.Sqrt, bias=self.eps[:, 0:1]).then_inc(self.std_ready.sem, 1)

    def scalar_out(self, act, it, n, s, dst, bank):
        act.wait_ge(self.zT_ps.sem, self.zT_ps.at(it, PAIR * n + s + 1))
        self.nc.scalar.activation(dst, bank[:], ACT.Copy).then_inc(self.zT_ready.sem, 1)

    def tensor(self, pe, it, n, s, bank):
        pe.wait_ge(self.z_ready.sem, self.z_ready.at(it, PAIR * n + s + 1))
        for t in range(T4):
            last = self.nc.tensor.transpose(bank[:, t * P:(t + 1) * P], self.z[:, s, t, :], self.ident[:])
        last.then_inc(self.zT_ps.sem, 1)

    def turned(self, pe, it, n, s):
        pe.wait_ge(self.zT_ready.sem, self.zT_ready.at(it, PAIR * n + s + 1))


def gate_phase(nc, d, keep):
    with ExitStack() as ctx:
        def sb(name, shape, dt=F32):
            return ctx.enter_context(nc.sbuf_tensor(name, shape, dt))

        def signal(name, per):
            return Signal(ctx.enter_context(nc.semaphore(name)), per)

        K = keep
        ident, v_tok, d_tok, fs_tok, fl_tok, x_all = (K[n] for n in ("ident", "v_tok", "d_tok", "fs_tok", "fl_tok", "x_all"))
        x_new, zT_all = v_tok, d_tok
        TH = T4 * NH
        zT = sb("zT", [H, PAIR, L])
        cen = sb("cen", [P, PAIR, 4, T4 * H])
        br = sb("br", [P, PAIR, T4, 2, 4 * NH])
        sT = sb("sT", [32, PAIR, L])
        hT = sb("hT", [P, PAIR, 2, L])
        lg = sb("lg", [P, PAIR, TH, 4])
        lgm = sb("lgm", [P, PAIR, TH])
        mix = sb("mix", [P, PAIR, T4 * H])
        rr = sb("rr", [P, PAIR, TH])
        oT = sb("oT", [H, PAIR, L])
        xb = sb("xb", [P, PAIR, T4, H])
        ps = [[ctx.enter_context(nc.psum_tensor(f"gps{s}{i}", [P, 512], F32)) for i in range(4)] for s in range(PAIR)]

        N = Normer(nc, ctx, "gn", 3, 30, ident, K["still"], K["eps5"])
        pool_step = Chain(ctx.enter_context(nc.semaphore("gpool")), PAIR)
        mean_ready = signal("mean_ready", PAIR)
        cen_ready = signal("cen_ready", 3 * PAIR)
        cen_v_ready = signal("cen_v_ready", PAIR)
        sqr_ready = signal("sqr_ready", 4 * PAIR)
        var4_ready = signal("var4_ready", PAIR)
        br_ready = signal("br_ready", PAIR)
        sT_ps = signal("sT_ps", PAIR)
        sT_ready = signal("sT_ready", PAIR)
        h_ps = signal("h_ps", 2 * PAIR)
        h_ready = signal("h_ready", 2 * PAIR)
        lg_ps = signal("lg_ps", PAIR)
        lg_ready = signal("lg_ready", PAIR)
        e_ready = signal("e_ready", PAIR)
        w_ready = signal("w_ready", PAIR)
        firs_mixed = signal("firs_mixed", PAIR)
        mix_ready = signal("mix_ready", PAIR)
        msq_ready = signal("msq_ready", PAIR)
        mvar_ready = signal("mvar_ready", PAIR)
        mstd = signal("gstd", PAIR)
        on_ready = signal("on_ready", PAIR)
        oT_ps = signal("oT_ps", PAIR)
        oT_ready = signal("oT_ready", PAIR)
        wo_ps = signal("wo_ps", PAIR)
        x_mixed = signal("x_mixed", PAIR)
        xb_ready = signal("xb_ready", PAIR)
        ff_ps = signal("ff_ps", PAIR)
        ff_done = signal("ff_done", PAIR)
        everything = N.all() + [sqr_ready, cen_v_ready, br_ready, sT_ready, h_ready, lg_ready, e_ready, firs_mixed, mix_ready,
                                msq_ready, mstd, on_ready, oT_ready, xb_ready, ff_done]
        block = ctx.enter_context(nc.Block())

        def round_over(eng, it):
            for s in everything:
                eng.wait_ge(s.sem, s.at(it))

        def tiles(a, it, s):
            return a[:, bass.ds(it * PT + T4 * s, T4), :]

        def by_head(a, it, s):
            return tiles(a, it, s).rearrange("p t (h c) -> p (t h) c", c=DK)

        def heads(a):
            return a.rearrange("p (g c) -> p g c", c=DK)

        def wide(a):
            return a.unsqueeze(2).broadcast_to([P, TH, DK])

        def by_head4(a, it, s):
            return tiles(a, it, s).rearrange("p t (h c) -> p t h c", c=DK)

        def heads4(a):
            return a.rearrange("p (t h c) -> p t h c", t=T4, c=DK)

        def stat(s, m, j):
            return br[:, s, :, m, NH * j:NH * j + NH]

        def wide4(a):
            return a.unsqueeze(3).broadcast_to([P, T4, NH, DK])

        SRCS = (fs_tok, fl_tok, d_tok, v_tok)

        @block.gpsimd
        def _(pool):
            with pool.Fori(0, B // PAIR) as it:
                for s in range(PAIR):
                    pool.wait_ge(mean_ready.sem, mean_ready.at(it, s + 1))
                    nc.gpsimd.tensor_tensor(heads4(cen[:, s, 3]), by_head4(v_tok, it, s), wide4(stat(s, 0, 3)), ALU.subtract).then_inc(cen_v_ready.sem, 1)
                for s in range(PAIR):
                    pool.wait_ge(w_ready.sem, w_ready.at(it, s + 1))
                    for j in range(2):
                        last = nc.gpsimd.tensor_tensor(heads(cen[:, s, j]), by_head(SRCS[j], it, s), lg[:, s, :, j:j + 1].broadcast_to([P, TH, DK]), ALU.mult)
                    last.then_inc(pool_step.sem, 1)
                    pool.wait_ge(pool_step.sem, it * pool_step.per + pool_step.next())
                    nc.gpsimd.tensor_tensor(cen[:, s, 0], cen[:, s, 0], cen[:, s, 1], ALU.add).then_inc(firs_mixed.sem, 1)
                for s in range(PAIR):
                    pool.wait_ge(x_mixed.sem, x_mixed.at(it, s + 1))
                    nc.gpsimd.tensor_tensor(xb[:, s], tiles(x_all, it, s), K["bias"][:].unsqueeze(1).broadcast_to([P, T4, H]), ALU.add).then_inc(xb_ready.sem, 1)
                round_over(pool, it)

        @block.scalar
        def _(act):
            with act.Fori(0, B // PAIR) as it:
                N.scalar(act, it, 0)
                for s in range(PAIR):
                    N.scalar_out(act, it, 0, s, zT[:, s], ps[s][0])
                for s in range(PAIR):
                    for j in (0, 1, 2, 3):
                        if j < 3:
                            act.wait_ge(cen_ready.sem, cen_ready.at(it, 3 * s + j + 1))
                        else:
                            act.wait_ge(cen_v_ready.sem, cen_v_ready.at(it, s + 1))
                        nc.scalar.activation(cen[:, s, j], cen[:, s, j], ACT.Square).then_inc(sqr_ready.sem, 1)
                for s in range(PAIR):
                    act.wait_ge(var4_ready.sem, var4_ready.at(it, s + 1))
                    v = br[:, s, :, 1]
                    nc.scalar.activation(v, v, ACT.Sqrt).then_inc(br_ready.sem, 1)
                for s in range(PAIR):
                    act.wait_ge(sT_ps.sem, sT_ps.at(it, s + 1))
                    nc.scalar.activation(sT[:, s], ps[s][1][0:32, :], ACT.Copy).then_inc(sT_ready.sem, 1)
                for s in range(PAIR):
                    for m in range(2):
                        act.wait_ge(h_ps.sem, h_ps.at(it, 2 * s + m + 1))
                        nc.scalar.activation(hT[:, s, m, :], ps[s][2 + m][:], ACT.Gelu, bias=K["b1"][:, m:m + 1]).then_inc(h_ready.sem, 1)
                for s in range(PAIR):
                    act.wait_ge(lg_ready.sem, lg_ready.at(it, s + 1))
                    nc.scalar.activation(lg[:, s], lg[:, s], ACT.Exp).then_inc(e_ready.sem, 1)
                for s in range(PAIR):
                    act.wait_ge(mix_ready.sem, mix_ready.at(it, s + 1))
                    nc.scalar.activation(cen[:, s, 3], mix[:, s], ACT.Square).then_inc(msq_ready.sem, 1)
                for s in range(PAIR):
                    act.wait_ge(mvar_ready.sem, mvar_ready.at(it, s + 1))
                    nc.scalar.activation(rr[:, s], rr[:, s], ACT.Sqrt, bias=K["eps5"][:, 0:1], scale=1.0 / DK).then_inc(mstd.sem, 1)
                for s in range(PAIR):
                    act.wait_ge(oT_ps.sem, oT_ps.at(it, s + 1))
                    nc.scalar.activation(oT[:, s], ps[s][1][:], ACT.Copy).then_inc(oT_ready.sem, 1)
                N.scalar(act, it, 1)
                for s in range(PAIR):
                    N.scalar_out(act, it, 1, s, zT[:, s], ps[s][0])
                N.scalar(act, it, 2)
                for s in range(PAIR):
                    N.scalar_out(act, it, 2, s, tiles(zT_all, it, s).rearrange("p t c -> p (t c)"), ps[s][0])
                round_over(act, it)

        @block.vector
        def _(dve):
            with dve.Fori(0, B // PAIR) as it:
                def xs(s):
                    return tiles(x_all, it, s)

                done = [0] * PAIR
                N.vector(dve, it, 0, xs)
                for s in range(PAIR):
                    for j in range(4):
                        last = nc.vector.tensor_reduce(stat(s, 0, j), by_head4(SRCS[j], it, s), AX.X, ALU.add)
                    done[s] = N.step(last)
                for s in range(PAIR):
                    N.need(dve, it, done[s])
                    m = br[:, s, :, 0]
                    nc.vector.tensor_scalar(m, m, 1.0 / DK, None, ALU.mult).then_inc(mean_ready.sem, 1)
                for s in range(PAIR):
                    dve.wait_ge(mean_ready.sem, mean_ready.at(it, s + 1))
                    for j in range(3):
                        nc.vector.tensor_tensor(heads4(cen[:, s, j]), by_head4(SRCS[j], it, s), wide4(stat(s, 0, j)), ALU.subtract).then_inc(cen_ready.sem, 1)
                for s in range(PAIR):
                    for j in range(4):
                        dve.wait_ge(sqr_ready.sem, sqr_ready.at(it, 4 * s + j + 1))
                        last = nc.vector.tensor_reduce(stat(s, 1, j), heads4(cen[:, s, j]), AX.X, ALU.add)
                    done[s] = N.step(last)
                for s in range(PAIR):
                    N.need(dve, it, done[s])
                    v = br[:, s, :, 1]
                    nc.vector.tensor_scalar(v, v, 1.0 / DK, 1e-6, ALU.mult, ALU.max).then_inc(var4_ready.sem, 1)
                for s in range(PAIR):
                    dve.wait_ge(lg_ps.sem, lg_ps.at(it, s + 1))
                    done[s] = N.step(nc.vector.tensor_tensor(
                        lg[:, s].rearrange("p (t h) j -> p t (h j)", t=T4), ps[s][0][:, 0:4 * TH].rearrange("p (t x) -> p t x", t=T4),
                        K["rtemp"][:].unsqueeze(1).broadcast_to([P, T4, 4 * NH]), ALU.mult))
                for s in range(PAIR):
                    N.need(dve, it, done[s])
                    done[s] = N.step(nc.vector.tensor_reduce(lgm[:, s], lg[:, s], AX.X, ALU.max))
                for s in range(PAIR):
                    N.need(dve, it, done[s])
                    nc.vector.tensor_tensor(lg[:, s], lg[:, s], lgm[:, s].unsqueeze(2).broadcast_to([P, TH, 4]), ALU.subtract).then_inc(lg_ready.sem, 1)
                for s in range(PAIR):
                    dve.wait_ge(e_ready.sem, e_ready.at(it, s + 1))
                    done[s] = N.step(nc.vector.tensor_reduce(lgm[:, s], lg[:, s], AX.X, ALU.add))
                for s in range(PAIR):
                    N.need(dve, it, done[s])
                    done[s] = N.step(nc.vector.reciprocal(lgm[:, s], lgm[:, s]))
                for s in range(PAIR):
                    N.need(dve, it, done[s])
                    nc.vector.tensor_tensor(lg[:, s], lg[:, s], lgm[:, s].unsqueeze(2).broadcast_to([P, TH, 4]), ALU.mult).then_inc(w_ready.sem, 1)
                for s in range(PAIR):
                    dve.wait_ge(w_ready.sem, w_ready.at(it, s + 1))
                    for j, dst in ((2, mix[:, s]), (3, cen[:, s, 2])):
                        last = nc.vector.tensor_tensor(heads(dst), by_head(SRCS[j], it, s), lg[:, s, :, j:j + 1].broadcast_to([P, TH, DK]), ALU.mult)
                    done[s] = N.step(last)
                for s in range(PAIR):
                    N.need(dve, it, done[s])
                    done[s] = N.step(nc.vector.tensor_tensor(mix[:, s], mix[:, s], cen[:, s, 2], ALU.add))
                for s in range(PAIR):
                    N.need(dve, it, done[s])
                    dve.wait_ge(firs_mixed.sem, firs_mixed.at(it, s + 1))
                    nc.vector.tensor_tensor(mix[:, s], mix[:, s], cen[:, s, 0], ALU.add).then_inc(mix_ready.sem, 1)
                for s in range(PAIR):
                    dve.wait_ge(msq_ready.sem, msq_ready.at(it, s + 1))
                    nc.vector.tensor_reduce(rr[:, s], heads(cen[:, s, 3]), AX.X, ALU.add).then_inc(mvar_ready.sem, 1)
                for s in range(PAIR):
                    dve.wait_ge(mstd.sem, mstd.at(it, s + 1))
                    done[s] = N.step(nc.vector.reciprocal(rr[:, s], rr[:, s]))
                for s in range(PAIR):
                    N.need(dve, it, done[s])
                    nc.vector.tensor_tensor(heads(mix[:, s]), heads(mix[:, s]), wide(rr[:, s]), ALU.mult).then_inc(on_ready.sem, 1)
                for s in range(PAIR):
                    dve.wait_ge(wo_ps.sem, wo_ps.at(it, s + 1))
                    nc.vector.tensor_tensor(xs(s), xs(s), ps[s][2][:].rearrange("p (t c) -> p t c", t=T4), ALU.add).then_inc(x_mixed.sem, 1)
                dve.wait_ge(x_mixed.sem, x_mixed.at(it))
                N.vector(dve, it, 1, xs)
                for s in range(PAIR):
                    dve.wait_ge(ff_ps.sem, ff_ps.at(it, s + 1))
                    dve.wait_ge(xb_ready.sem, xb_ready.at(it, s + 1))
                    nc.vector.tensor_tensor(tiles(x_new, it, s), xb[:, s], ps[s][1][:].rearrange("p (t c) -> p t c", t=T4), ALU.add).then_inc(ff_done.sem, 1)
                dve.wait_ge(ff_done.sem, ff_done.at(it))
                N.vector(dve, it, 2, lambda s: tiles(x_new, it, s))
                round_over(dve, it)
            assert N.steps.k == N.steps.per, N.steps.k

        @block.tensor
        def _(pe):
            with pe.Fori(0, B // PAIR) as it:
                for s in range(PAIR):
                    N.tensor(pe, it, 0, s, ps[s][0])
                for s in range(PAIR):
                    N.turned(pe, it, 0, s)
                for s in range(PAIR):
                    pe.wait_ge(br_ready.sem, br_ready.at(it, s + 1))
                    for t in range(T4):
                        last = nc.tensor.transpose(ps[s][1][0:32, t * P:(t + 1) * P], br[:, s, t].rearrange("p m x -> p (m x)"), ident[:])
                    last.then_inc(sT_ps.sem, 1)
                for s in range(PAIR):
                    for m in range(2):
                        nc.tensor.matmul(ps[s][2 + m][:], K["w1x"][:, m * P:(m + 1) * P], zT[:, s], start=True, stop=False)
                    pe.wait_ge(sT_ready.sem, sT_ready.at(it, s + 1))
                    for m in range(2):
                        nc.tensor.matmul(ps[s][2 + m][:], K["w1s"][0:32, m * P:(m + 1) * P], sT[:, s], start=False, stop=True).then_inc(h_ps.sem, 1)
                for s in range(PAIR):
                    pe.wait_ge(h_ready.sem, h_ready.at(it, 2 * s + 2))
                    for t in range(T4):
                        dst = ps[s][0][:, 16 * t:16 * t + 16]
                        nc.tensor.matmul(dst, K["ones"][0:1, :], K["b2"][0:1, :], start=True, stop=False)
                        for m in range(2):
                            last = nc.tensor.matmul(dst, hT[:, s, m, t * P:(t + 1) * P], K["w2"][:, m, :], start=False, stop=m == 1)
                    last.then_inc(lg_ps.sem, 1)
                for s in range(PAIR):
                    pe.wait_ge(on_ready.sem, on_ready.at(it, s + 1))
                    for t in range(T4):
                        last = nc.tensor.transpose(ps[s][1][:, t * P:(t + 1) * P], mix[:, s, t * P:(t + 1) * P], ident[:])
                    last.then_inc(oT_ps.sem, 1)
                for s in range(PAIR):
                    pe.wait_ge(oT_ready.sem, oT_ready.at(it, s + 1))
                    for t in range(T4):
                        last = nc.tensor.matmul(ps[s][2][:, t * P:(t + 1) * P], oT[:, s, t * P:(t + 1) * P], K["wo_a"][:], start=True, stop=True)
                    last.then_inc(wo_ps.sem, 1)
                for s in range(PAIR):
                    N.tensor(pe, it, 1, s, ps[s][0])
                for s in range(PAIR):
                    N.turned(pe, it, 1, s)
                    for t in range(T4):
                        last = nc.tensor.matmul(ps[s][1][:, t * P:(t + 1) * P], zT[:, s, t * P:(t + 1) * P], K["cbT"][:], start=True, stop=True)
                    last.then_inc(ff_ps.sem, 1)
                for s in range(PAIR):
                    N.tensor(pe, it, 2, s, ps[s][0])
                round_over(pe, it)


def last_phase(nc, d, keep):
    with ExitStack() as ctx:
        def sb(name, shape, dt=F32):
            return ctx.enter_context(nc.sbuf_tensor(name, shape, dt))

        def signal(name, per):
            return Signal(ctx.enter_context(nc.semaphore(name)), per)

        K, x_all = keep, keep["v_tok"]
        zT = sb("lzT", [H, PAIR, L])
        xb = sb("lxb", [P, PAIR, T4, H])
        y = sb("ly", [P, 2, PAIR * T4, H])
        ps = [[ctx.enter_context(nc.psum_tensor(f"lps{s}{i}", [P, 512], F32)) for i in range(2)] for s in range(PAIR)]
        N = Normer(nc, ctx, "ln", 1, 4, K["ident"], K["still"], K["eps5"])
        xb_ready = signal("lxb_ready", PAIR)
        ff_ps = signal("lff_ps", PAIR)
        ff_done = signal("lff_done", PAIR)
        stored = signal("stored", 16)
        everything = N.all() + [xb_ready, ff_done]
        block = ctx.enter_context(nc.Block())

        def round_over(eng, it):
            for s in everything:
                eng.wait_ge(s.sem, s.at(it))

        def tiles(a, it, s):
            return a[:, bass.ds(it * PT + T4 * s, T4), :]

        @block.gpsimd
        def _(pool):
            with pool.Fori(0, B // PAIR) as it:
                for s in range(PAIR):
                    nc.gpsimd.tensor_tensor(xb[:, s], tiles(x_all, it, s), K["bias"][:].unsqueeze(1).broadcast_to([P, T4, H]), ALU.add).then_inc(xb_ready.sem, 1)
                round_over(pool, it)

        @block.scalar
        def _(act):
            with act.Fori(0, B // PAIR) as it:
                N.scalar(act, it, 0)
                for s in range(PAIR):
                    N.scalar_out(act, it, 0, s, zT[:, s], ps[s][0])
                act.wait_ge(ff_done.sem, ff_done.at(it))
                act.dma_start(d["out"][:, bass.ds(it * PT, PT), :], x_all[:, bass.ds(it * PT, PT), :]).then_inc(stored.sem, 16)
                round_over(act, it)
            act.wait_ge(stored.sem, 16 * (B // PAIR))

        @block.vector
        def _(dve):
            with dve.Fori(0, B // PAIR) as it:
                N.vector(dve, it, 0, lambda s: tiles(x_all, it, s))
                for s in range(PAIR):
                    dve.wait_ge(ff_ps.sem, ff_ps.at(it, s + 1))
                    dve.wait_ge(xb_ready.sem, xb_ready.at(it, s + 1))
                    nc.vector.tensor_tensor(tiles(x_all, it, s), xb[:, s], ps[s][1][:].rearrange("p (t c) -> p t c", t=T4), ALU.add).then_inc(ff_done.sem, 1)
                round_over(dve, it)
            assert N.steps.k == N.steps.per, N.steps.k

        @block.tensor
        def _(pe):
            with pe.Fori(0, B // PAIR) as it:
                for s in range(PAIR):
                    N.tensor(pe, it, 0, s, ps[s][0])
                for s in range(PAIR):
                    N.turned(pe, it, 0, s)
                    for t in range(T4):
                        last = nc.tensor.matmul(ps[s][1][:, t * P:(t + 1) * P], zT[:, s, t * P:(t + 1) * P], K["cbT"][:], start=True, stop=True)
                    last.then_inc(ff_ps.sem, 1)
                round_over(pe, it)


def attention_phase(nc, keep):
    with ExitStack() as ctx:
        def sb(name, shape, dt=F32):
            return ctx.enter_context(nc.sbuf_tensor(name, shape, dt))

        def signal(name, per):
            return Signal(ctx.enter_context(nc.semaphore(name)), per)

        K = keep
        ident, x_all, zT_all = K["ident"], K["v_tok"], K["d_tok"]
        W = HA * DH
        zT = sb("azT", [H, L])
        V = K["fs_tok"][:].rearrange("p (t a) c -> p t (a c)", t=T4)
        sqb = sb("sqb", [P, 2, W])
        ra = K["fl_tok"][:].rearrange("p (n a) c -> p n (a c)", n=4)
        rb = sb("rb", [P, 2, W])
        ss = sb("ss", [P, 2 * T4, HA])
        kTh = sb("kTh", [P, HA // 2, L], F16)
        kTl = sb("kTl", [P, HA // 2, L], F16)
        qTh = sb("qTh", [P, HA, L], F16)
        qTl = sb("qTl", [P, HA, L], F16)
        nmx = sb("nmx", [P, 4])
        rs = sb("rs", [P, 2, T4])
        Pm = sb("Pm", [P, 3, L])
        PT_ = sb("PTs", [P, 3, L])
        O = sb("O", [P, 2, T4, 2 * DH])
        OT = sb("OT", [P, 2, L])
        ps = ctx.enter_context(nc.psum_tensor("aps", [P, 8, 512], F32))
        S_BANK, PT_BANK, O_BANK, Y_BANK = (0, 1, 2), (3, 4), (5, 6), 7
        OT_BANK = O_BANK[1]

        z0 = ctx.enter_context(nc.semaphore("z0"))
        z_in = signal("az_in", 1)
        proj = signal("proj", 12)
        sq_done = signal("sq_done", 8)
        v_done = signal("v_done", 4)
        ss_done = signal("ss_done", 8)
        rms_done = signal("rms_done", 8)
        inv_done = signal("inv_done", 8)
        rot_done = signal("rot_done", 8)
        add_done = signal("add_done", 8)
        rope_done = signal("rope_done", 8)
        tr_ps = signal("tr_ps", 8)
        hi_done = signal("hi_done", 8)
        lo_done = signal("lo_done", 8)
        s_ps = signal("s_ps", UNITS)
        max_done = signal("max_done", UNITS)
        p_done = signal("p_done", UNITS)
        pt_ps = signal("pt_ps", UNITS)
        pt_done = signal("pt_done", UNITS)
        o_ps = signal("mo_ps", UNITS)
        rs_done = signal("rs_done", HA)
        o_done = signal("mo_done", HA)
        ot_ps = signal("ot_ps", HA // 2)
        ot_done = signal("ot_done", HA // 2)
        y_ps = signal("y_ps", HA // 2)
        x_done = signal("x_done", 1)
        everything = [v_done, rope_done, lo_done, p_done, pt_done, o_done, ot_done, x_done]
        block = ctx.enter_context(nc.Block())

        def round_over(eng, it):
            for s in everything:
                eng.wait_ge(s.sem, s.at(it))

        UN = [(h, i) for h in range(HA) for i in range(T4)]
        CHUNKS = [(t, m) for t in range(T4) for m in "kqv"]
        KQ = [c for c in CHUNKS if c[1] != "v"]

        def chunk_banks(n):
            return ps[:, 2 * (n % 2):2 * (n % 2) + 2]

        def turn_banks(n):
            return ps[:, 4 + 2 * (n % 2):6 + 2 * (n % 2)]

        def turned(n):
            return turn_banks(n).rearrange("p b (a t) -> p (b a) t", t=P)

        @block.gpsimd
        def _(pool):
            nc.gpsimd.memset(qTh[:], 0.0).then_inc(z0, 1)
            nc.gpsimd.memset(qTl[:], 0.0).then_inc(z0, 1)
            with pool.Fori(0, B) as it:
                for n in range(len(KQ)):
                    a = ra[:, n % 4]
                    pool.wait_ge(rot_done.sem, rot_done.at(it, n + 1))
                    nc.gpsimd.tensor_tensor(a, a, rb[:, n % 2], ALU.add).then_inc(add_done.sem, 1)
                    pool.wait_ge(add_done.sem, add_done.at(it, n + 1))
                    pool.wait_ge(inv_done.sem, inv_done.at(it, n + 1))
                    a3 = a.rearrange("p (h c) -> p h c", c=DH)
                    nc.gpsimd.tensor_tensor(a3, a3, ss[:, n].unsqueeze(2).broadcast_to([P, HA, DH]), ALU.mult).then_inc(rope_done.sem, 1)
                round_over(pool, it)

        @block.scalar
        def _(act):
            act.wait_ge(z0, 2)

            def hi(it, n):
                t, m = KQ[n]
                act.wait_ge(tr_ps.sem, tr_ps.at(it, n + 1))
                ts = slice(t * P, t * P + P)
                if m == "k":
                    nc.scalar.activation(kTh[:, :, ts], turned(n), ACT.Copy).then_inc(hi_done.sem, 1)
                else:
                    nc.scalar.activation(qTh[0:DH, 0::2, ts], turned(n)[0:DH], ACT.Copy)
                    nc.scalar.activation(qTh[DH:P, 1::2, ts], turned(n)[DH:P], ACT.Copy).then_inc(hi_done.sem, 1)

            def ot(it, g):
                act.wait_ge(ot_ps.sem, ot_ps.at(it, g + 1))
                if g >= 2:
                    act.wait_ge(y_ps.sem, y_ps.at(it, g - 1))
                nc.scalar.activation(OT[:, g % 2, :], ps[:, OT_BANK], ACT.Copy).then_inc(ot_done.sem, 1)

            with act.Fori(0, B) as it:
                nc.scalar.activation(zT[:], zT_all[:, bass.ds(it * T4, T4), :].rearrange("p t c -> p (t c)"), ACT.Copy).then_inc(z_in.sem, 1)
                k_ = 0
                for n, (t, m) in enumerate(CHUNKS):
                    act.wait_ge(proj.sem, proj.at(it, n + 1))
                    if m == "v":
                        nc.scalar.activation(V[:, t].rearrange("p (b c) -> p b c", b=2), chunk_banks(n), ACT.Copy).then_inc(v_done.sem, 1)
                        continue
                    if k_ >= 2:
                        act.wait_ge(ss_done.sem, ss_done.at(it, k_ - 1))
                    nc.scalar.activation(sqb[:, k_ % 2].rearrange("p (b c) -> p b c", b=2), chunk_banks(n), ACT.Square).then_inc(sq_done.sem, 1)
                    if k_ >= 3:
                        hi(it, k_ - 3)
                    act.wait_ge(ss_done.sem, ss_done.at(it, k_ + 1))
                    nc.scalar.activation(ss[:, k_], ss[:, k_], ACT.Sqrt, bias=K["eps6"][:, 0:1], scale=1.0 / DH).then_inc(rms_done.sem, 1)
                    k_ += 1
                for j in (3, 2, 1):
                    hi(it, k_ - j)
                for u, (h, i) in enumerate(UN):
                    w = P * (i + 1)
                    act.wait_ge(max_done.sem, max_done.at(it, u + 1))
                    if u >= 3:
                        act.wait_ge(pt_ps.sem, pt_ps.at(it, u - 2))
                    if i == 0 and h >= 2:
                        act.wait_ge(o_done.sem, o_done.at(it, h - 1))
                    nc.scalar.activation(Pm[:, u % 3, 0:w], ps[:, S_BANK[u % 3], 0:w], ACT.Exp, bias=nmx[:, u % 4:u % 4 + 1],
                                         accum_out=rs[:, h % 2, i:i + 1]).then_inc(p_done.sem, 1)
                    if i == 1 and h % 2 and h >= 3:
                        ot(it, h // 2 - 1)
                ot(it, HA // 2 - 1)
                round_over(act, it)

        @block.vector
        def _(dve):
            dve.wait_ge(z0, 2)

            def lo(it, n):
                t, m = KQ[n]
                dve.wait_ge(hi_done.sem, hi_done.at(it, n + 1))
                ts = slice(t * P, t * P + P)
                if m == "k":
                    nc.vector.tensor_tensor(kTl[:, :, ts], turned(n), kTh[:, :, ts], ALU.subtract).then_inc(lo_done.sem, 1)
                else:
                    nc.vector.tensor_tensor(qTl[0:DH, 0::2, ts], turned(n)[0:DH], qTh[0:DH, 0::2, ts], ALU.subtract)
                    nc.vector.tensor_tensor(qTl[DH:P, 1::2, ts], turned(n)[DH:P], qTh[DH:P, 1::2, ts], ALU.subtract).then_inc(lo_done.sem, 1)

            def pt_out(it, u):
                w = P * (UN[u][1] + 1)
                dve.wait_ge(pt_ps.sem, pt_ps.at(it, u + 1))
                if u >= 3:
                    dve.wait_ge(o_ps.sem, o_ps.at(it, u - 2))
                nc.vector.tensor_copy(PT_[:, u % 3, 0:w], ps[:, PT_BANK[u % 2], 0:w]).then_inc(pt_done.sem, 1)

            def o_out(it, h):
                dve.wait_ge(rs_done.sem, rs_done.at(it, h + 1))
                dve.wait_ge(o_ps.sem, o_ps.at(it, T4 * h + T4))
                if h >= 4:
                    dve.wait_ge(ot_ps.sem, ot_ps.at(it, h // 2 - 1))
                nc.vector.tensor_tensor(O[:, h // 2 % 2, :, DH * (h % 2):DH * (h % 2) + DH], ps[:, O_BANK[h % 2], 0:T4 * DH].rearrange("p (t c) -> p t c", t=T4),
                                        rs[:, h % 2].unsqueeze(2).broadcast_to([P, T4, DH]), ALU.mult).then_inc(o_done.sem, 1)

            def inverse_sums(it, h):
                dve.wait_ge(p_done.sem, p_done.at(it, T4 * h + T4))
                nc.vector.reciprocal(rs[:, h % 2], rs[:, h % 2]).then_inc(rs_done.sem, 1)

            with dve.Fori(0, B) as it:
                for n, (t, m) in enumerate(KQ):
                    banks = chunk_banks(CHUNKS.index((t, m)))
                    p_ = n % 2
                    w = 0 if m == "k" else 1
                    dve.wait_ge(sq_done.sem, sq_done.at(it, n + 1))
                    nc.vector.tensor_reduce(ss[:, n], sqb[:, p_].rearrange("p (h c) -> p h c", c=DH), AX.X, ALU.add).then_inc(ss_done.sem, 1)
                    b4 = banks.rearrange("p b (h w c) -> p (b h) w c", w=2, c=DH // 2)
                    r4 = rb[:, p_].rearrange("p (h w c) -> p h w c", w=2, c=DH // 2)
                    tab = K["rope"][:, w, t]
                    if n >= 4:
                        dve.wait_ge(tr_ps.sem, tr_ps.at(it, n - 3))
                    if n >= 2:
                        dve.wait_ge(add_done.sem, add_done.at(it, n - 1))
                    nc.vector.tensor_tensor(ra[:, n % 4].rearrange("p (h c) -> p h c", c=DH), banks.rearrange("p b (h c) -> p (b h) c", c=DH),
                                            tab[:, 0:1].broadcast_to([P, HA, DH]), ALU.mult)
                    nc.vector.tensor_tensor(r4[:, :, 0], b4[:, :, 1], tab[:, 1:2, 0:32].broadcast_to([P, HA, 32]), ALU.mult)
                    nc.vector.tensor_tensor(r4[:, :, 1], b4[:, :, 0], tab[:, 1:2, 32:64].broadcast_to([P, HA, 32]), ALU.mult).then_inc(rot_done.sem, 1)
                    dve.wait_ge(rms_done.sem, rms_done.at(it, n + 1))
                    nc.vector.reciprocal(ss[:, n], ss[:, n]).then_inc(inv_done.sem, 1)
                    if n >= 3:
                        lo(it, n - 3)
                for j in (3, 2, 1):
                    lo(it, len(KQ) - j)
                for u, (h, i) in enumerate(UN):
                    w = P * (i + 1)
                    dve.wait_ge(s_ps.sem, s_ps.at(it, u + 1))
                    if u >= 4:
                        dve.wait_ge(p_done.sem, p_done.at(it, u - 3))
                    nc.vector.tensor_reduce(nmx[:, u % 4:u % 4 + 1], ps[:, S_BANK[u % 3], 0:w], AX.X, ALU.max, negate=True).then_inc(max_done.sem, 1)
                    if u >= 2:
                        pt_out(it, u - 2)
                    if i == 2 and h:
                        inverse_sums(it, h - 1)
                    if i == 3 and h:
                        o_out(it, h - 1)
                pt_out(it, UNITS - 2)
                pt_out(it, UNITS - 1)
                inverse_sums(it, HA - 1)
                o_out(it, HA - 1)
                dve.wait_ge(y_ps.sem, y_ps.at(it))
                nc.vector.tensor_copy(x_all[:, bass.ds(it * T4, T4), :], ps[:, Y_BANK].rearrange("p (t c) -> p t c", t=T4)).then_inc(x_done.sem, 1)
                round_over(dve, it)

        @block.tensor
        def _(pe):
            pe.wait_ge(z0, 2)
            order = {"q": 0, "k": 1, "v": 2}

            def turn(it, n):
                pe.wait_ge(rope_done.sem, rope_done.at(it, n + 1))
                if n >= 2:
                    pe.wait_ge(lo_done.sem, lo_done.at(it, n - 1))
                for a in range(HA // 2):
                    last = nc.tensor.transpose(turned(n)[:, a], ra[:, n % 4, a * P:(a + 1) * P], ident[:])
                last.then_inc(tr_ps.sem, 1)

            def scores(it, u):
                h, i = UN[u]
                w = P * (i + 1)
                ts = slice(i * P, i * P + P)
                if u >= 3:
                    pe.wait_ge(p_done.sem, p_done.at(it, u - 2))
                dst = ps[:, S_BANK[u % 3]]
                nc.tensor.matmul(dst[:, 0:w], qTh[:, h, ts], kTh[:, h // 2, 0:w], start=True, stop=False)
                nc.tensor.matmul(dst[:, 0:w], qTl[:, h, ts], kTh[:, h // 2, 0:w], start=False, stop=False)
                nc.tensor.matmul(dst[:, w - P:w], K["identb"][:], K["maskb"][:], start=False, stop=False, skip_group_check=True)
                nc.tensor.matmul(dst[:, 0:w], qTh[:, h, ts], kTl[:, h // 2, 0:w], start=False, stop=True).then_inc(s_ps.sem, 1)

            def turn_p(it, u):
                pe.wait_ge(p_done.sem, p_done.at(it, u + 1))
                if u >= 2:
                    pe.wait_ge(pt_done.sem, pt_done.at(it, u - 1))
                for j in range(UN[u][1] + 1):
                    last = nc.tensor.transpose(ps[:, PT_BANK[u % 2], j * P:(j + 1) * P], Pm[:, u % 3, j * P:(j + 1) * P], ident[:])
                last.then_inc(pt_ps.sem, 1)

            def values(it, u):
                h, i = UN[u]
                pe.wait_ge(pt_done.sem, pt_done.at(it, u + 1))
                if i == 0 and h >= 2:
                    pe.wait_ge(o_done.sem, o_done.at(it, h - 1))
                if i == 0 and h % 2 and h >= 3:
                    pe.wait_ge(ot_done.sem, ot_done.at(it, h // 2))
                for j in range(i + 1):
                    last = nc.tensor.matmul(ps[:, O_BANK[h % 2], DH * i:DH * i + DH], PT_[:, u % 3, j * P:(j + 1) * P], V[:, j, DH * h:DH * h + DH], start=j == 0, stop=j == i)
                last.then_inc(o_ps.sem, 1)

            def out_pair(it, g):
                pe.wait_ge(o_done.sem, o_done.at(it, 2 * g + 2))
                if g:
                    pe.wait_ge(ot_done.sem, ot_done.at(it, g))
                for t in range(T4):
                    last = nc.tensor.transpose(ps[:, OT_BANK, t * P:(t + 1) * P], O[:, g % 2, t, :], ident[:])
                last.then_inc(ot_ps.sem, 1)

            def out_product(it, g):
                pe.wait_ge(ot_done.sem, ot_done.at(it, g + 1))
                for t in range(T4):
                    last = nc.tensor.matmul(ps[:, Y_BANK, t * P:(t + 1) * P], OT[:, g % 2, t * P:(t + 1) * P], K["woT"][:, g, :],
                                            start=False, stop=g == HA // 2 - 1, skip_group_check=True)
                last.then_inc(y_ps.sem, 1)

            with pe.Fori(0, B) as it:
                pe.wait_ge(z_in.sem, z_in.at(it))
                n_kq = 0
                for n, (t, m) in enumerate(CHUNKS):
                    if n >= 2:
                        before = CHUNKS[n - 2]
                        if before[1] == "v":
                            pe.wait_ge(v_done.sem, v_done.at(it, before[0] + 1))
                        else:
                            pe.wait_ge(rot_done.sem, rot_done.at(it, KQ.index(before) + 1))
                    for b in range(2):
                        c0 = order[m] * W + b * 512
                        last = nc.tensor.matmul(chunk_banks(n)[:, b], zT[:, t * P:(t + 1) * P], K["wqkvT"][:, c0:c0 + 512], start=True, stop=True)
                    last.then_inc(proj.sem, 1)
                    if m != "v":
                        if n_kq >= 2:
                            turn(it, n_kq - 2)
                        n_kq += 1
                turn(it, n_kq - 2)
                turn(it, n_kq - 1)
                pe.wait_ge(lo_done.sem, lo_done.at(it))
                pe.wait_ge(v_done.sem, v_done.at(it))
                nc.tensor.matmul(ps[:, Y_BANK], ident[:], x_all[:, bass.ds(it * T4, T4), :].rearrange("p t c -> p (t c)"),
                                 start=True, stop=False, skip_group_check=True)
                for u in range(UNITS):
                    scores(it, u)
                    if u >= 2:
                        turn_p(it, u - 2)
                    if u >= 3:
                        values(it, u - 3)
                    h, i = UN[u]
                    if h % 2 and h >= 3:
                        if i == 0:
                            out_pair(it, h // 2 - 1)
                        if i == 2:
                            out_product(it, h // 2 - 1)
                turn_p(it, UNITS - 2)
                values(it, UNITS - 3)
                turn_p(it, UNITS - 1)
                values(it, UNITS - 2)
                values(it, UNITS - 1)
                out_pair(it, HA // 2 - 1)
                out_product(it, HA // 2 - 1)
                round_over(pe, it)

def build_kernel(nc, d, out):
    with ExitStack() as ctx:
        def sb(name, shape, dt=F32):
            return ctx.enter_context(nc.sbuf_tensor(name, shape, dt))

        def load_all(names, sem):
            with nc.Block() as block:
                @block.sync
                def _(sp):
                    for n in names:
                        sp.dma_start(keep[n][:], d[n]).then_inc(sem, 16)
                    sp.wait_ge(sem, 16 * len(names))

        def loaded(names_shapes, stack):
            for n, shape in names_shapes.items():
                keep[n] = stack.enter_context(nc.sbuf_tensor(n, shape, F32))
            return list(names_shapes)

        keep = {}
        loaded(dict(ident=[P, P], anti=[P, P], eps6=[P, 1], eps5=[P, 1], still=[P, PAIR + 1]), ctx)
        loaded(dict(v_tok=[P, TILES, H], d_tok=[P, TILES, H], fs_tok=[P, TILES, H]), ctx)
        with ExitStack() as own:
            names = loaded(dict(wqkv=[H, 3, H], wb=[H, NH], cw=[H, 3, CONV], fsw=[H, FS], blk=[P, P], causal=[P, P]), own)
            load_all(["ident", "anti", "eps6", "eps5"] + names, own.enter_context(nc.semaphore("first_in")))
            delta_phase(nc, d, keep)
        names = loaded(dict(fl_tok=[P, TILES, H], bias=[P, H], cbT=[H, H], wqkvT=[H, 3 * HA * DH], woT=[P, HA // 2, H], rope=[P, 2, T4, 2, DH]), ctx)[1:]
        for n in ("identb", "maskb"):
            keep[n] = ctx.enter_context(nc.sbuf_tensor(n, [P, P], BF16))
        with ExitStack() as own:
            names += loaded(dict(x_all=[P, TILES, H], b1=[P, 2], b2=[1, 16], w1x=[H, MH], w1s=[32, MH], w2=[P, 2, 16], ones=[1, P], wo_a=[H, H],
                                 scb=[P, H], onorm=[H, 1], rtemp=[P, 16], mask=[P, P], nw=[P, 2, 2, DH]), own)
            fir_phase(nc, d, keep, names)
            tables(nc, keep, own)
            gate_phase(nc, d, keep)
        attention_phase(nc, keep)
        last_phase(nc, dict(out=out), keep)


def tables(nc, K, ctx):
    g = K["rtemp"]
    t = ctx.enter_context(nc.sbuf_tensor("soft", [P, 3, 16], F32))
    step = ctx.enter_context(nc.semaphore("table_step"))
    expd = ctx.enter_context(nc.semaphore("table_exp"))
    with nc.Block() as block:
        @block.scalar
        def _(act):
            act.wait_ge(step, 2)
            nc.scalar.activation(t[:, 1], t[:, 0], ACT.Exp, scale=-1.0).then_inc(expd, 1)
            act.wait_ge(step, 3)
            nc.scalar.activation(t[:, 2], t[:, 1], ACT.Ln).then_inc(expd, 1)

        @block.vector
        def _(dve):
            n = [0]

            def chain(ins):
                n[0] += 1
                ins.then_inc(step, 1)
                dve.wait_ge(step, n[0])

            chain(nc.vector.tensor_scalar(t[:, 0], g[:], -1.0, None, ALU.mult))
            chain(nc.vector.tensor_tensor(t[:, 0], t[:, 0], g[:], ALU.max))
            dve.wait_ge(expd, 1)
            chain(nc.vector.tensor_scalar(t[:, 1], t[:, 1], 1.0, None, ALU.add))
            dve.wait_ge(expd, 2)
            chain(nc.vector.scalar_tensor_tensor(g[:], g[:], 0.0, t[:, 2], ALU.max, ALU.add))
            chain(nc.vector.tensor_scalar(g[:], g[:], 1e-4, None, ALU.add))
            chain(nc.vector.reciprocal(g[:], g[:]))
            chain(nc.vector.tensor_scalar(K["scb"][:], K["scb"][:], 1.0 / 127.0, None, ALU.mult))
            chain(nc.vector.tensor_tensor(K["cbT"][:], K["cbT"][:], K["scb"][:], ALU.mult))
            chain(nc.vector.tensor_scalar(K["wo_a"][:], K["wo_a"][:], K["onorm"][:, 0:1], None, ALU.mult))
            for w in range(2):
                chain(nc.vector.tensor_tensor(K["rope"][:, w], K["rope"][:, w], K["nw"][:, w].unsqueeze(1).broadcast_to([P, T4, 2, DH]), ALU.mult))
            q_table = K["rope"][:, 1].rearrange("p t w c -> p (t w c)")
            chain(nc.vector.tensor_scalar(q_table, q_table, DH ** -0.5, None, ALU.mult))
            chain(nc.vector.tensor_copy(K["identb"][:], K["ident"][:]))
            chain(nc.vector.tensor_copy(K["maskb"][:], K["mask"][:]))


def layouts(a):
    q, b = "L0_attn_a_", "L0_attn_b_"
    a = {k: np.asarray(v, np.float32) for k, v in a.items()}
    k = np.arange(P)
    same = k[:, None] // CH == k[None, :] // CH
    f = np.float32
    angles = np.arange(L, dtype=f)[:, None] * (f(1.0) / f(10000.0) ** (np.arange(0, DH, 2, dtype=f) / f(DH)))
    cos, sin = np.cos(angles).astype(f), np.sin(angles).astype(f)
    turn = np.stack([np.concatenate([cos, cos], 1), np.concatenate([-sin, sin], 1)], 1)
    turn = turn.reshape(T4, P, 2, DH).transpose(1, 0, 2, 3)
    wide = lambda v, *s: np.ascontiguousarray(np.broadcast_to(v, (P, *s)))
    nws = [a[b + "k_norm_w"], a[b + "q_norm_w"]]
    nw = np.stack([np.stack([w, np.concatenate([w[32:], w[:32]])]) for w in nws])
    z = np.zeros((H, 2 * P + 64), f)
    z[:, P - 1:P - 1 + FL] = a[q + "fir_long_w"].reshape(H, FL)[:, ::-1]
    return dict(
        x=a[q + "hidden_states"].reshape(B * L, H),
        wqkv=np.stack([a[q + "Wq"], a[q + "Wk"], a[q + "Wv"]], 1), wb=a[q + "Wb"],
        cw=np.stack([a[q + f"conv_{n}_w"] for n in "qkv"], 1), fsw=a[q + "fir_short_w"].reshape(H, FS),
        ident=np.eye(P, dtype=f), anti=np.eye(P, dtype=f)[::-1].copy(), blk=same.astype(f), causal=(same & (k[:, None] <= k[None, :])).astype(f),
        eps6=np.full((P, 1), 1e-6, f), eps5=np.full((P, 1), 1e-5, f), fir_z=z,
        b1=a[q + "mlp_b1"].reshape(2, P).T.copy(), b2=a[q + "mlp_b2"].reshape(1, 16),
        w1x=a[q + "mlp_w1"][:H],
        w1s=a[q + "mlp_w1"][H:].reshape(4, 2, NH, MH).transpose(1, 0, 2, 3).reshape(32, MH).copy(), w2=a[q + "mlp_w2"].reshape(2, P, 16).transpose(1, 0, 2).copy(),
        ones=np.ones((1, P), f), wo_a=a[q + "Wo"], cbT=a["L0_ffn_CB"].T.copy(), scb=wide(a["L0_ffn_SCB"], H), bias=wide(a["L0_ffn_bias"], H),
        onorm=np.tile(a[q + "o_norm_w"], NH)[:, None].copy(), rtemp=wide(np.repeat(a[q + "gate_log_temp"], 4), 16),
        wqkvT=a[b + "wqkv"].T.copy(), woT=a[b + "wo"].T.reshape(HA // 2, P, H).transpose(1, 0, 2).copy(),
        rope=np.ascontiguousarray(np.broadcast_to(turn[:, None], (P, 2, T4, 2, DH))), nw=wide(nw, 2, 2, DH),
        mask=np.where(k[:, None] >= k[None, :], f(0), f(-1e30)).astype(f),
    )


def kernel(**inputs):
    import concourse.bacc as bacc
    from concourse.bass_utils import run_bass_kernel_spmd

    nc = bacc.Bacc("TRN2", target_bir_lowering=False, num_devices=1)
    arrays = {f"in_{n}": v for n, v in layouts(inputs).items()}
    d = {n[3:]: nc.dram_tensor(n, v.shape, mybir.dt.from_np(v.dtype), kind="ExternalInput").ap() for n, v in arrays.items()}
    out = nc.dram_tensor("out_x", (B * L, H), F32, kind="ExternalOutput").ap()
    d["x"] = d["x"].rearrange("(n p) c -> p n c", p=P)
    d["x_all"] = d["x"]
    build_kernel(nc, d, out.rearrange("(n p) c -> p n c", p=P))
    r = run_bass_kernel_spmd(nc, [arrays], core_ids=[0])
    return r.results[0]["out_x"].reshape(B, L, H)
```

```python
from contextlib import ExitStack

import numpy as np

import concourse.bass as bass
from concourse import mybir

F32 = mybir.dt.float32
F16 = mybir.dt.float16
BF16 = mybir.dt.bfloat16
ALU = mybir.AluOpType
ACT = mybir.ActivationFunctionType
AX = mybir.AxisListType

P = 128
B, L, H = 8, 512, 128
TILES = B * L // P
NH, DK = 4, 32
CH = 32
PAIR = 2
PT = PAIR * L // P
PTOK = PAIR * L
PC = PTOK // CH
ROUNDS = B // PAIR
TS = L // P
STEPS = L // CH
CONV = 4
FS, FL = 3, 63
EPS_LN = 1e-5


class Signal:

    def __init__(self, sem, per):
        self.sem, self.per = sem, per

    def at(self, it, k=None):
        return it * self.per + (self.per if k is None else k)


class Chain:

    def __init__(self, sem, per):
        self.sem, self.per, self.k = sem, per, 0

    def next(self):
        self.k += 1
        return self.k



def delta_phase(nc, d, keep):
    with ExitStack() as ctx:
        def sb(name, shape, dt=F32):
            return ctx.enter_context(nc.sbuf_tensor(name, shape, dt))

        def signal(name, per):
            return Signal(ctx.enter_context(nc.semaphore(name)), per)

        x_in = sb("x_in", [P, PT, H])
        stats = sb("stats", [P, PT, 6])
        mv = sb("mv", [P, PT, 2])
        rstd = sb("rstd", [P, PT])
        xn = sb("xn", [P, PT, H])
        xT = sb("xT", [H, PTOK])
        pre = [sb(f"pre_{n}", [H, PAIR, CONV - 1 + L]) for n in "qkv"]
        con = [sb(f"con_{n}", [H, PAIR, L]) for n in "qkv"]
        vpad = sb("vpad", [H, PAIR, FS - 1 + L])
        fir = sb("fir", [H, PAIR, L])
        sq = sb("sq", [H, 2, PTOK])
        kT = sb("kT", [H, PTOK])
        beta = sb("beta", [P, PT, NH])
        VK = sb("VK", [P, PT, NH, 2, DK])
        M = sb("M", [P, PT, NH, CH])
        A = sb("A", [P, CH, CH])
        X = sb("X", [P, CH, CH])
        tmp = sb("tmp", [P, CH * CH])
        TT = sb("TT", [P, PT * NH, P])
        UW = sb("UW", [P, PT, 2, NH * DK])
        uT = sb("uT", [H, PTOK])
        WQ = sb("WQ", [H, PC, 2, CH])
        kx = sb("kx", [P, PC, NH * DK])
        Sx = sb("Sx", [P, PAIR, NH * DK])
        u2T = sb("u2T", [H, PTOK])
        qsT = sb("qsT", [H, PTOK])
        u2h = sb("u2h", [P, PAIR, DK])
        u2tok = UW[:, 0:PT // 2].rearrange("p (a b) w c -> p (a b w) c", b=1)
        AT = sb("AT", [P, 4, NH, P])
        qstok = UW[:, PT // 2:].rearrange("p (a b) w c -> p (a b w) c", b=1)
        ss = sb("ss_qk", [P, 2, PT * NH])
        zero = sb("zero", [P, PAIR * DK])
        ps01 = ctx.enter_context(nc.psum_tensor("ps01", [P, 2, 512], F32))
        ps23 = ctx.enter_context(nc.psum_tensor("ps23", [P, 2, 512], F32))
        ps47 = ctx.enter_context(nc.psum_tensor("ps47", [P, 4, 512], F32))
        wqkv, wb, cw, fsw, ident, blk, causal = (keep[n] for n in ("wqkv", "wb", "cw", "fsw", "ident", "blk", "causal"))
        v_tok, d_tok, fs_tok = keep["v_tok"], keep["d_tok"], keep["fs_tok"]

        x_loaded = signal("x_loaded", 16)
        cleared = signal("cleared", 6)
        dv = Chain(ctx.enter_context(nc.semaphore("dve_step")), 82)
        fdv = Chain(ctx.enter_context(nc.semaphore("front_dve")), 14)
        std_ready = signal("std_ready", 1)
        xn_std = signal("xn_std", 1)
        xn_ready = signal("xn_ready", 1)
        xT_ps = signal("xT_ps", 1)
        xT_ready = signal("xT_ready", 1)
        proj_ps = signal("proj_ps", 3)
        pre_ready = signal("pre_ready", 3)
        beta_ps = signal("beta_ps", 1)
        beta_ready = signal("beta_ready", 1)
        con_ready = signal("con_ready", 3)
        silu_ready = signal("silu_ready", 3)
        sq_ready = signal("sq_ready", 2)
        ss_ps = signal("ss_ps", 2)
        norm_ready = signal("norm_ready", 2)
        inv_ready = signal("inv_ready", 2)
        wide_ready = signal("wide_ready", 2)
        wide_ps = signal("wide_ps", 2)
        normed = signal("normed", 2)
        qk_ready = signal("qk_ready", 2)
        fir_ready = signal("fir_ready", 1)
        tok_ps = signal("tok_ps", 3)
        tok_out = signal("tok_out", 3)
        kk_ps = signal("kk_ps", 2)
        kk_used = signal("kk_used", 2)
        TT_ready = signal("TT_ready", 1)
        kx_ready = signal("kx_ready", 1)
        UW_ps = signal("UW_ps", 2)
        UW_ready = signal("UW_ready", 4)
        UWT_ps = signal("UWT_ps", 2)
        UWT_ready = signal("UWT_ready", 2)
        WS_ps = signal("WS_ps", STEPS)
        u2_ready = signal("u2_ready", STEPS)
        qs_ready = signal("qs_ready", STEPS)
        S_ps = signal("S_ps", STEPS)
        S_ready = signal("S_ready", STEPS)
        S_zero = signal("S_zero", 1)
        u2t_ps = signal("u2t_ps", 1)
        u2t_ready = signal("u2t_ready", 1)
        qst_ps = signal("qst_ps", 1)
        qst_ready = signal("qst_ready", 1)
        qk_ps = signal("qk_ps", 2)
        AT_ready = signal("AT_ready", 2)
        o_ps = signal("o_ps", 2)
        o_ready = signal("o_ready", 1)
        everything = [tok_out, qk_ready, kk_used, TT_ready, kx_ready, UW_ready, UWT_ready,
                      u2_ready, qs_ready, S_ready, u2t_ready, qst_ready, AT_ready, o_ready, o_ps]

        block = ctx.enter_context(nc.Block())

        def round_over(eng, it):
            for s in everything:
                eng.wait_ge(s.sem, s.at(it))

        STEP = dict(stats=-1, std=-1, xn=-1, xT=0, proj0=2, proj1=4, proj2=6, beta=7, silu0=5, silu1=7, silu2=9,
                    ss0=8, ss1=10, root0=8, root1=10, inv0=9, inv1=11, wide0=11, wide1=13, normed0=12, normed1=14, fir0=10.5, fir1=11.5, fir2=12.5)
        for i in range(3):
            for j in range(CONV):
                STEP[f"con{i}_{j}"] = 3 + 2 * i + j / 2

        for name in ("xT", "proj0", "proj1", "proj2", "beta", "ss0", "ss1", "wide0", "wide1"):
            STEP[name + "_2"] = STEP[name] + 0.5

        def stands(step, n):
            return n is None or STEP[step] == n

        @block.gpsimd
        def _(pool):
            for t in (*pre, vpad):
                nc.gpsimd.memset(t[:, :, 0:CONV - 1 if t is not vpad else FS - 1], 0.0).then_inc(cleared.sem, 1)
            nc.gpsimd.memset(TT[:], 0.0).then_inc(cleared.sem, 1)
            nc.gpsimd.memset(kx[:], 0.0).then_inc(cleared.sem, 1)
            pool.wait_ge(cleared.sem, 6)
            nc.gpsimd.memset(zero[:], 0.0).then_inc(cleared.sem, 1)

            def front(it):
                for i in range(2):
                    pool.wait_ge(inv_ready.sem, inv_ready.at(it, i + 1))
                    nc.gpsimd.tensor_tensor(sq[:, i, :].rearrange("p (g c) -> p g c", c=DK), ss[:, i].unsqueeze(2).broadcast_to([P, PT * NH, DK]),
                                            zero[:, 0:1].unsqueeze(2).broadcast_to([P, PT * NH, DK]), ALU.add).then_inc(wide_ready.sem, 1)

            def main(it):
                nc.gpsimd.memset(Sx[:], 0.0).then_inc(S_zero.sem, 1)

            front(0)
            with pool.Fori(0, ROUNDS - 1) as it:
                main(it)
                front(it + 1)
                round_over(pool, it)
            main(ROUNDS - 1)

        @block.scalar
        def _(act):
            act.wait_ge(cleared.sem, 7)

            def load(it):
                act.dma_start(x_in[:], d["x"][:, bass.ds(it * PT, PT), :]).then_inc(x_loaded.sem, 16)

            def front(it, n):
                def std():
                    act.wait_ge(std_ready.sem, std_ready.at(it))
                    nc.scalar.activation(rstd[:], rstd[:], ACT.Sqrt).then_inc(xn_std.sem, 1)

                def turned():
                    act.wait_ge(xT_ps.sem, xT_ps.at(it))
                    nc.scalar.activation(xT[:], ps47[:, 0:2].rearrange("p a b -> p (a b)"), ACT.Copy).then_inc(xT_ready.sem, 1)

                def projected(i):
                    act.wait_ge(proj_ps.sem, proj_ps.at(it, i + 1))
                    nc.scalar.activation(pre[i][:, :, CONV - 1:], (ps47[:, 2:4], ps47[:, 0:2])[i % 2], ACT.Copy).then_inc(pre_ready.sem, 1)

                def gate():
                    act.wait_ge(beta_ps.sem, beta_ps.at(it))
                    nc.scalar.activation(beta[:].rearrange("p a b -> p (a b)"), ps23[:, 1, 0:PT * NH], ACT.Sigmoid).then_inc(beta_ready.sem, 1)

                def silu(i):
                    act.wait_ge(con_ready.sem, con_ready.at(it, i + 1))
                    dst = vpad[:, :, FS - 1:] if i == 2 else con[i][:]
                    nc.scalar.activation(dst, con[i][:], ACT.Silu).then_inc(silu_ready.sem, 1)
                    if i < 2:
                        act.wait_ge(silu_ready.sem, silu_ready.at(it, i + 1))
                        nc.scalar.activation(sq[:, i, :], con[i][:].rearrange("p a b -> p (a b)"), ACT.Square).then_inc(sq_ready.sem, 1)

                def root(i):
                    act.wait_ge(ss_ps.sem, ss_ps.at(it, i + 1))
                    nc.scalar.activation(ss[:, i], ps23[:, 1, 64 * i + 64:64 * i + 64 + PT * NH], ACT.Sqrt, bias=keep["eps6"][:, 0:1]).then_inc(norm_ready.sem, 1)

                if stands("std", n):
                    std()
                if stands("xT", n):
                    turned()
                for i in range(3):
                    if stands(f"proj{i}", n):
                        projected(i)
                if stands("silu0", n):
                    silu(0)
                if stands("beta", n):
                    gate()
                if stands("silu1", n):
                    silu(1)
                if stands("root0", n):
                    root(0)
                if stands("silu2", n):
                    silu(2)
                if stands("root1", n):
                    root(1)

            def main(it, more):
                if more:
                    load(it + 1)
                act.wait_ge(normed.sem, normed.at(it, 1))
                nc.scalar.activation(WQ[:, :, 1, :], con[0][:].rearrange("p s (n c) -> p (s n) c", c=CH), ACT.Copy).then_inc(qk_ready.sem, 1)
                act.wait_ge(normed.sem, normed.at(it, 2))
                nc.scalar.activation(kT[:], con[1][:].rearrange("p s n -> p (s n)"), ACT.Copy).then_inc(qk_ready.sem, 1)
                act.wait_ge(tok_ps.sem, tok_ps.at(it, 1))
                nc.scalar.activation(v_tok[:, bass.ds(it * PT, PT), :], ps23[:].rearrange("p a (b c) -> p (a b) c", c=H), ACT.Copy).then_inc(tok_out.sem, 1)
                act.wait_ge(tok_ps.sem, tok_ps.at(it, 3))
                nc.scalar.activation(fs_tok[:, bass.ds(it * PT, PT), :], ps23[:].rearrange("p a (b c) -> p (a b) c", c=H), ACT.Copy).then_inc(tok_out.sem, 1)
                for hf in range(2):
                    act.wait_ge(UW_ps.sem, UW_ps.at(it, hf + 1))
                    for w in range(2):
                        nc.scalar.activation(
                            UW[:, 4 * hf:4 * hf + 4, w, :].rearrange("p t (h c) -> p t h c", h=NH),
                            ps47[:, 2 * hf:2 * hf + 2].rearrange("p a (t h w c) -> p (a t) h w c", h=NH, w=2, c=DK)[:, :, :, w, :],
                            ACT.Copy).then_inc(UW_ready.sem, 1)
                if more:
                    front(it + 1, -1)
                act.wait_ge(UWT_ps.sem, UWT_ps.at(it, 1))
                nc.scalar.activation(uT[:], ps01[:].rearrange("p a b -> p (a b)"), ACT.Copy).then_inc(UWT_ready.sem, 1)
                act.wait_ge(UWT_ps.sem, UWT_ps.at(it, 2))
                nc.scalar.activation(WQ[:, :, 0, :], ps23[:].rearrange("p a (x c) -> p (a x) c", c=CH), ACT.Copy).then_inc(UWT_ready.sem, 1)
                for n in range(STEPS):
                    act.wait_ge(u2_ready.sem, u2_ready.at(it, n + 1))
                    nc.scalar.activation(
                        qsT[:].rearrange("p (s x) -> p s x", s=PAIR)[:, :, n * CH:(n + 1) * CH],
                        ps01[:, n % 2, 0:PAIR * 64].rearrange("p (s x) -> p s x", s=PAIR)[:, :, 32:64], ACT.Copy).then_inc(qs_ready.sem, 1)
                    if more:
                        front(it + 1, n)
                act.wait_ge(u2t_ps.sem, u2t_ps.at(it))
                nc.scalar.activation(u2tok.rearrange("p a b -> p (a b)"), ps01[:].rearrange("p a b -> p (a b)"), ACT.Copy).then_inc(u2t_ready.sem, 1)
                act.wait_ge(qst_ps.sem, qst_ps.at(it))
                nc.scalar.activation(qstok.rearrange("p a b -> p (a b)"), ps23[:].rearrange("p a b -> p (a b)"), ACT.Copy).then_inc(qst_ready.sem, 1)

            load(0)
            front(0, None)
            with act.Fori(0, ROUNDS - 1) as it:
                main(it, True)
                round_over(act, it)
            main(ROUNDS - 1, False)

        @block.vector
        def _(dve):
            dve.wait_ge(cleared.sem, 7)

            def chain(ins, it):
                k = dv.next()
                ins.then_inc(dv.sem, 1)
                dve.wait_ge(dv.sem, it * dv.per + k)

            def front_chain(ins, it):
                k = fdv.next()
                ins.then_inc(fdv.sem, 1)
                dve.wait_ge(fdv.sem, it * fdv.per + k)

            def front(it, n):
                def moments():
                    dve.wait_ge(x_loaded.sem, x_loaded.at(it))
                    nc.vector.memset(keep["still"][:, 1:2], 0.0)
                    for t in range(PT):
                        last = nc.vector.bn_stats(stats[:, t, :], x_in[:, t, :])
                    front_chain(last, it)
                    nc.vector.memset(keep["still"][:, 0:1], 0.0)
                    for t in range(PT):
                        last = nc.vector.bn_aggr(mv[:, t, :], stats[:, t, :])
                    front_chain(last, it)
                    nc.vector.tensor_scalar(rstd[:], mv[:, :, 1], EPS_LN, None, ALU.add).then_inc(std_ready.sem, 1)

                def norm():
                    dve.wait_ge(xn_std.sem, xn_std.at(it))
                    front_chain(nc.vector.reciprocal(rstd[:], rstd[:]), it)
                    for t in range(PT):
                        last = nc.vector.tensor_scalar(xn[:, t, :], x_in[:, t, :], mv[:, t, 0:1], rstd[:, t:t + 1], ALU.subtract, ALU.mult)
                    last.then_inc(xn_ready.sem, 1)

                def tap(i, j):
                    w = cw[:, i, j:j + 1]
                    if j == 0:
                        dve.wait_ge(pre_ready.sem, pre_ready.at(it, i + 1))
                        front_chain(nc.vector.tensor_scalar(con[i][:], pre[i][:, :, j:j + L], w, None, ALU.mult), it)
                    else:
                        ins = nc.vector.scalar_tensor_tensor(con[i][:], pre[i][:, :, j:j + L], w, con[i][:], ALU.mult, ALU.add)
                        if j < CONV - 1:
                            front_chain(ins, it)
                        else:
                            ins.then_inc(con_ready.sem, 1)

                def short_fir(j):
                    w = fsw[:, j:j + 1]
                    if j == 0:
                        dve.wait_ge(silu_ready.sem, silu_ready.at(it, 3))
                        front_chain(nc.vector.tensor_scalar(fir[:], vpad[:, :, j:j + L], w, None, ALU.mult), it)
                    else:
                        ins = nc.vector.scalar_tensor_tensor(fir[:], vpad[:, :, j:j + L], w, fir[:], ALU.mult, ALU.add)
                        if j < FS - 1:
                            front_chain(ins, it)
                        else:
                            ins.then_inc(fir_ready.sem, 1)

                def inverse(i):
                    dve.wait_ge(norm_ready.sem, norm_ready.at(it, i + 1))
                    nc.vector.reciprocal(ss[:, i], ss[:, i]).then_inc(inv_ready.sem, 1)

                def over_norm(i):
                    dve.wait_ge(wide_ps.sem, wide_ps.at(it, i + 1))
                    nc.vector.tensor_tensor(con[i][:], con[i][:], ps47[:, 2 * i:2 * i + 2], ALU.mult).then_inc(normed.sem, 1)

                if stands("stats", n):
                    moments()
                if stands("xn", n):
                    norm()
                for i in range(3):
                    for j in range(CONV):
                        if stands(f"con{i}_{j}", n):
                            tap(i, j)
                if stands("inv0", n):
                    inverse(0)
                if stands("normed0", n):
                    over_norm(0)
                if stands("inv1", n):
                    inverse(1)
                for j in range(FS):
                    if stands(f"fir{j}", n):
                        short_fir(j)
                if stands("normed1", n):
                    over_norm(1)

            def main(it, more):
                dve.wait_ge(beta_ready.sem, beta_ready.at(it))
                dve.wait_ge(tok_out.sem, tok_out.at(it, 1))
                bb = beta[:].rearrange("p t h -> p (t h)").unsqueeze(2).broadcast_to([P, PT * NH, DK])
                chain(nc.vector.tensor_tensor(VK[:, :, :, 0, :].rearrange("p t h c -> p (t h) c"),
                                        ps23[:].rearrange("p a (b c) -> p (a b) c", c=DK), bb, ALU.mult), it)
                dve.wait_ge(tok_ps.sem, tok_ps.at(it, 2))
                nc.vector.tensor_tensor(VK[:, :, :, 1, :].rearrange("p t h c -> p (t h) c"),
                                        ps01[:].rearrange("p a (b c) -> p (a b) c", c=DK), bb, ALU.mult).then_inc(tok_out.sem, 1)
                for hf in range(2):
                    dve.wait_ge(kk_ps.sem, kk_ps.at(it, hf + 1))
                    for c in range(4):
                        q = slice(CH * c, CH * c + CH)
                        last = nc.vector.tensor_tensor(
                            M[q, 4 * hf:4 * hf + 4].rearrange("p t h c -> p h t c"),
                            ps47[q, :, :].rearrange("p h (t c) -> p h t c", t=4)[:, :, :, CH * c:CH * c + CH],
                            beta[q, 4 * hf:4 * hf + 4].rearrange("p t h -> p h t").unsqueeze(3).broadcast_to([CH, NH, 4, CH]), ALU.mult)
                    last.then_inc(kk_used.sem, 1)
                dve.wait_ge(kk_used.sem, kk_used.at(it, 2))
                nc.vector.memset(X[:], 0.0).then_inc(dv.sem, 1)
                dv.next()
                nc.vector.transpose(A[:], M[:].rearrange("p t h j -> p j (t h)")).then_inc(dv.sem, 1)
                dv.next()
                dve.wait_ge(dv.sem, it * dv.per + dv.k)
                chain(nc.vector.memset(X[:].rearrange("p a b -> p (a b)")[:, 0:CH * CH:CH + 1], 1.0), it)
                for j in range(CH - 1):
                    r, c = CH - 1 - j, j + 1
                    t3 = tmp[:, 0:r * c].rearrange("p (r c) -> p r c", c=c)
                    chain(nc.vector.tensor_tensor(t3, A[:, j, j + 1:].unsqueeze(2).broadcast_to([P, r, c]),
                                                  X[:, j:j + 1, 0:c].broadcast_to([P, r, c]), ALU.mult), it)
                    chain(nc.vector.tensor_tensor(X[:, j + 1:, 0:c], X[:, j + 1:, 0:c], t3, ALU.subtract), it)
                for c in range(4):
                    q = slice(CH * c, CH * c + CH)
                    last = nc.vector.transpose(TT[q, :, CH * c:CH * c + CH].rearrange("p b i -> p i b"), X[q, :, :])
                last.then_inc(TT_ready.sem, 1)
                dve.wait_ge(qk_ready.sem, qk_ready.at(it, 2))
                for h in range(NH):
                    last = nc.vector.transpose(kx[DK * h:DK * h + DK, :, DK * h:DK * h + DK],
                                               kT[DK * h:DK * h + DK, :].rearrange("p (n c) -> p n c", c=CH))
                last.then_inc(kx_ready.sem, 1)
                if more:
                    front(it + 1, -1)
                dve.wait_ge(UWT_ready.sem, UWT_ready.at(it, 2))
                for n in range(STEPS):
                    dve.wait_ge(WS_ps.sem, WS_ps.at(it, n + 1))
                    u3 = u2T[:].rearrange("p (s x) -> p s x", s=PAIR)[:, :, n * CH:(n + 1) * CH]
                    chain(nc.vector.tensor_tensor(
                        u3, uT[:].rearrange("p (s x) -> p s x", s=PAIR)[:, :, n * CH:(n + 1) * CH],
                        ps01[:, n % 2, 0:PAIR * 64].rearrange("p (s x) -> p s x", s=PAIR)[:, :, 0:32], ALU.subtract), it)
                    if n:
                        dve.wait_ge(S_ps.sem, S_ps.at(it, n))
                    nc.vector.transpose(u2h[:], u3).then_inc(u2_ready.sem, 1)
                    if more:
                        front(it + 1, n - 0.5)
                    dve.wait_ge(S_ps.sem, S_ps.at(it, n + 1))
                    for h in range(NH):
                        last = nc.vector.tensor_copy(
                            Sx[DK * h:DK * h + DK, :, DK * h:DK * h + DK],
                            ps23[DK * h:DK * h + DK, 0, 0:PAIR * DK].rearrange("p (s x) -> p s x", s=PAIR))
                    last.then_inc(S_ready.sem, 1)
                    if more:
                        front(it + 1, n)
                for hf in range(2):
                    dve.wait_ge(qk_ps.sem, qk_ps.at(it, hf + 1))
                    if hf:
                        dve.wait_ge(o_ps.sem, o_ps.at(it, 1))
                    for h in range(NH):
                        last = nc.vector.tensor_tensor(
                            AT[:, :, h, :], ps47[:, h, :].rearrange("p (t i) -> p t i", t=4),
                            causal[:].unsqueeze(1).broadcast_to([P, 4, P]), ALU.mult)
                    last.then_inc(AT_ready.sem, 1)
                dve.wait_ge(o_ps.sem, o_ps.at(it, 2))
                dve.wait_ge(qst_ready.sem, qst_ready.at(it))
                nc.vector.tensor_tensor(d_tok[:, bass.ds(it * PT, PT), :], ps01[:].rearrange("p a (b c) -> p (a b) c", c=H),
                                        qstok, ALU.add).then_inc(o_ready.sem, 1)

            def chains_over():
                assert (dv.k, fdv.k) == (dv.per, fdv.per), (dv.k, fdv.k)
                dv.k = fdv.k = 0

            front(0, None)
            fdv.k = 0
            with dve.Fori(0, ROUNDS - 1) as it:
                main(it, True)
                chains_over()
                round_over(dve, it)
            main(ROUNDS - 1, False)

        @block.tensor
        def _(pe):
            pe.wait_ge(cleared.sem, 7)

            def front(it, n):
                def turn(s):
                    if s == 0:
                        pe.wait_ge(xn_ready.sem, xn_ready.at(it))
                    for t in range(TS * s, TS * s + TS):
                        last = nc.tensor.transpose(ps47[:, t // 4, P * (t % 4):P * (t % 4) + P], xn[:, t, :], ident[:])
                    if s:
                        last.then_inc(xT_ps.sem, 1)

                def project(i, s):
                    if i == 0 and s == 0:
                        pe.wait_ge(xT_ready.sem, xT_ready.at(it))
                    if i == 2 and s == 0:
                        pe.wait_ge(pre_ready.sem, pre_ready.at(it, 1))
                    last = nc.tensor.matmul((ps47[:, 2 + s], ps47[:, s])[i % 2], wqkv[:, i, :], xT[:, s * L:(s + 1) * L], start=True, stop=True)
                    if s:
                        last.then_inc(proj_ps.sem, 1)

                def gates(s):
                    for t in range(TS * s, TS * s + TS):
                        last = nc.tensor.matmul(ps23[:, 1, t * NH:(t + 1) * NH], xT[:, t * P:(t + 1) * P], wb[:], start=True, stop=True)
                    if s:
                        last.then_inc(beta_ps.sem, 1)

                def sums(i, s):
                    if s == 0:
                        pe.wait_ge(sq_ready.sem, sq_ready.at(it, i + 1))
                        if i == 0:
                            pe.wait_ge(beta_ready.sem, beta_ready.at(it))
                        else:
                            pe.wait_ge(norm_ready.sem, norm_ready.at(it, 1))
                    for t in range(TS * s, TS * s + TS):
                        last = nc.tensor.matmul(ps23[:, 1, 64 * i + 64 + t * NH:64 * i + 64 + (t + 1) * NH], sq[:, i, t * P:(t + 1) * P], blk[:, 0:P:DK], start=True, stop=True)
                    if s:
                        last.then_inc(ss_ps.sem, 1)

                def widen(i, s):
                    if s == 0:
                        pe.wait_ge(wide_ready.sem, wide_ready.at(it, i + 1))
                        pe.wait_ge(pre_ready.sem, pre_ready.at(it, 2 if i == 0 else 3))
                    for t in range(TS * s, TS * s + TS):
                        last = nc.tensor.transpose(ps47[:, 2 * i + t // 4, P * (t % 4):P * (t % 4) + P], sq[:, i, t * P:(t + 1) * P], ident[:])
                    if s:
                        last.then_inc(wide_ps.sem, 1)

                for s in range(PAIR):
                    if stands(("xT", "xT_2")[s], n):
                        turn(s)
                for i in range(3):
                    for s in range(PAIR):
                        if stands((f"proj{i}", f"proj{i}_2")[s], n):
                            project(i, s)
                for s in range(PAIR):
                    if stands(("beta", "beta_2")[s], n):
                        gates(s)
                for i in range(2):
                    for s in range(PAIR):
                        if stands((f"ss{i}", f"ss{i}_2")[s], n):
                            sums(i, s)
                for i in range(2):
                    for s in range(PAIR):
                        if stands((f"wide{i}", f"wide{i}_2")[s], n):
                            widen(i, s)

            def main(it, more):
                pe.wait_ge(silu_ready.sem, silu_ready.at(it, 3))
                pe.wait_ge(norm_ready.sem, norm_ready.at(it, 2))
                for t in range(PT):
                    last = nc.tensor.transpose(ps23[:, t // 4, P * (t % 4):P * (t % 4) + P], vpad[:, t // 4, FS - 1 + P * (t % 4):FS - 1 + P * (t % 4) + P], ident[:])
                last.then_inc(tok_ps.sem, 1)
                pe.wait_ge(qk_ready.sem, qk_ready.at(it, 2))
                for t in range(PT):
                    last = nc.tensor.transpose(ps01[:, t // 4, P * (t % 4):P * (t % 4) + P], kT[:, t * P:(t + 1) * P], ident[:])
                last.then_inc(tok_ps.sem, 1)
                pe.wait_ge(normed.sem, normed.at(it, 2))
                for hf in range(2):
                    if hf:
                        pe.wait_ge(kk_used.sem, kk_used.at(it, 1))
                    for h in range(NH):
                        q = slice(DK * h, DK * h + DK)
                        for t in range(4):
                            s = slice((4 * hf + t) * P, (4 * hf + t + 1) * P)
                            last = nc.tensor.matmul(ps47[:, h, t * P:(t + 1) * P], kT[q, s], kT[q, s], start=True, stop=True)
                    last.then_inc(kk_ps.sem, 1)
                pe.wait_ge(fir_ready.sem, fir_ready.at(it))
                pe.wait_ge(tok_out.sem, tok_out.at(it, 2))
                for t in range(PT):
                    last = nc.tensor.transpose(ps23[:, t // 4, P * (t % 4):P * (t % 4) + P], fir[:, t // 4, P * (t % 4):P * (t % 4) + P], ident[:])
                last.then_inc(tok_ps.sem, 1)
                pe.wait_ge(TT_ready.sem, TT_ready.at(it))
                pe.wait_ge(kk_used.sem, kk_used.at(it, 2))
                for hf in range(2):
                    for t in range(4):
                        for h in range(NH):
                            g = (4 * hf + t) * NH + h
                            last = nc.tensor.matmul(ps47[:, g // 8, 64 * (g % 8):64 * (g % 8) + 64], TT[:, g, :],
                                                    VK[:, g // NH, h].rearrange("p w c -> p (w c)"), start=True, stop=True)
                    last.then_inc(UW_ps.sem, 1)
                pe.wait_ge(UW_ready.sem, UW_ready.at(it, 4))
                pe.wait_ge(tok_out.sem, tok_out.at(it, 3))
                for w, ps in enumerate((ps01, ps23)):
                    for t in range(PT):
                        last = nc.tensor.transpose(ps[:, t // 4, P * (t % 4):P * (t % 4) + P], UW[:, t, w, :], ident[:])
                    last.then_inc(UWT_ps.sem, 1)
                pe.wait_ge(UWT_ready.sem, UWT_ready.at(it, 2))
                pe.wait_ge(S_zero.sem, S_zero.at(it))
                pe.wait_ge(kx_ready.sem, kx_ready.at(it))
                nc.tensor.matmul(ps23[:, 0, 0:PAIR * DK], ident[:], zero[:], start=True, stop=False, skip_group_check=True)
                for n in range(STEPS):
                    if n:
                        pe.wait_ge(S_ready.sem, S_ready.at(it, n))
                    if n >= 2:
                        pe.wait_ge(qs_ready.sem, qs_ready.at(it, n - 1))
                    for s in range(PAIR):
                        last = nc.tensor.matmul(ps01[:, n % 2, 64 * s:64 * s + 64], Sx[:, s, :],
                                                WQ[:, s * STEPS + n].rearrange("p w c -> p (w c)"), start=True, stop=True)
                    last.then_inc(WS_ps.sem, 1)
                    if more:
                        front(it + 1, n - 0.5)
                    pe.wait_ge(u2_ready.sem, u2_ready.at(it, n + 1))
                    for s in range(PAIR):
                        last = nc.tensor.matmul(ps23[:, 0, DK * s:DK * s + DK], kx[:, s * STEPS + n, :], u2h[:, s, :],
                                                start=False, stop=n == STEPS - 1 and s == PAIR - 1, skip_group_check=True)
                    last.then_inc(S_ps.sem, 1)
                    if more:
                        front(it + 1, n)
                pe.wait_ge(qs_ready.sem, qs_ready.at(it))
                for t in range(PT):
                    last = nc.tensor.transpose(ps01[:, t // 4, P * (t % 4):P * (t % 4) + P], u2T[:, t * P:(t + 1) * P], ident[:])
                last.then_inc(u2t_ps.sem, 1)
                pe.wait_ge(S_ready.sem, S_ready.at(it))
                for t in range(PT):
                    last = nc.tensor.transpose(ps23[:, t // 4, P * (t % 4):P * (t % 4) + P], qsT[:, t * P:(t + 1) * P], ident[:])
                last.then_inc(qst_ps.sem, 1)
                if more:
                    pe.wait_ge(normed.sem, normed.at(it + 1))
                for hf in range(2):
                    if hf:
                        pe.wait_ge(AT_ready.sem, AT_ready.at(it, 1))
                    for h in range(NH):
                        q = slice(DK * h, DK * h + DK)
                        for t in range(4):
                            g = 4 * hf + t
                            last = nc.tensor.matmul(ps47[:, h, t * P:(t + 1) * P].rearrange("p (n c) -> p n c", c=CH), kT[q, g * P:(g + 1) * P],
                                                    WQ[q, 4 * g:4 * g + 4, 1, :], start=True, stop=True)
                    last.then_inc(qk_ps.sem, 1)
                    pe.wait_ge(AT_ready.sem, AT_ready.at(it, hf + 1))
                    pe.wait_ge(u2t_ready.sem, u2t_ready.at(it))
                    for t in range(4):
                        for h in range(NH):
                            last = nc.tensor.matmul(ps01[:, hf, t * P + h * DK:t * P + h * DK + DK], AT[:, t, h, :],
                                                    u2tok[:, 4 * hf + t, h * DK:(h + 1) * DK], start=True, stop=True)
                    last.then_inc(o_ps.sem, 1)

            front(0, None)
            with pe.Fori(0, ROUNDS - 1) as it:
                main(it, True)
                round_over(pe, it)
            main(ROUNDS - 1, False)


HA, DH = 16, 64
T4 = L // P
MH = 256
UNITS = HA * T4


def fir_phase(nc, d, keep, loads):
    G = 16
    GROUPS = H // G
    HP = P // 2
    with ExitStack() as ctx:
        def signal(name, per):
            return Signal(ctx.enter_context(nc.semaphore(name)), per)

        band = [ctx.enter_context(nc.sbuf_tensor(f"band{i}", [P, G, HP], F32)) for i in range(2)]
        windows = [ctx.enter_context(nc.sbuf_tensor(f"windows{i}", [P, TILES, H], F32)) for i in range(2)]
        staged = [ctx.enter_context(nc.sbuf_tensor(f"staged{i}", [P, 2, TILES, G], F32)) for i in range(2)]
        ps = [ctx.enter_context(nc.psum_tensor(f"fir_ps{i}", [P, TILES, G], F32)) for i in range(2)]
        turn_ps = ctx.enter_context(nc.psum_tensor("turn_ps", [P, 4, T4, H], F32))
        v_tok, fl_tok, anti = keep["v_tok"], keep["fl_tok"], keep["anti"]
        band_in = [signal(f"band_in{i}", 16) for i in range(2)]
        turned = signal("turned", 0)
        copied = signal("copied", 0)
        stage_ready = signal("stage_ready", 2)
        fir_ps = signal("fir_ps", 2)
        fir_free = signal("fir_free", 2)
        weights_in = signal("weights_in", 0)
        block = ctx.enter_context(nc.Block())
        z = d["fir_z"]
        width = z.shape[1]

        @block.sync
        def _(sp):
            for g in range(GROUPS):
                if g >= 2:
                    sp.wait_ge(fir_ps.sem, g - 1)
                src = bass.AP(z.tensor, g * G * width, [[1, P], [width, G], [1, HP]])
                sp.dma_start(band[g % 2][:], src).then_inc(band_in[g % 2].sem, 16)
            for s in band_in:
                sp.wait_ge(s.sem, 16 * (GROUPS // 2))

        @block.tensor
        def _(pe):
            for n in range(2 * B):
                b, w = n // 2, n % 2
                if n >= 4:
                    pe.wait_ge(copied.sem, n - 3)
                tiles = v_tok[:, T4 * b:T4 * b + T4, :]
                if w:
                    nc.tensor.matmul(turn_ps[:, n % 4], anti[:, HP:HP + P], tiles, start=True, stop=True).then_inc(turned.sem, 1)
                else:
                    nc.tensor.matmul(turn_ps[:, n % 4], anti[:, P:2 * P], tiles, start=True, stop=False, skip_group_check=True)
                    nc.tensor.matmul(turn_ps[:, n % 4, 1:], anti[:, 0:P], v_tok[:, T4 * b:T4 * b + T4 - 1, :],
                                     start=False, stop=True, skip_group_check=True).then_inc(turned.sem, 1)
            with pe.Fori(0, GROUPS // 2) as it:
                for i in range(2):
                    pe.wait_ge(band_in[i].sem, it * 16 + 16)
                    pe.wait_ge(stage_ready.sem, stage_ready.at(it, i + 1))
                    for c in range(G):
                        for w in range(2):
                            last = nc.tensor.matmul(ps[i][HP * w:HP * w + HP, :, c], band[i][:, c, :], staged[i][:, w, :, c], start=True, stop=True)
                    last.then_inc(fir_ps.sem, 1)

        @block.vector
        def _(dve):
            for b in range(B):
                dve.wait_ge(turned.sem, 2 * b + 1)
                if b:
                    dve.wait_ge(copied.sem, 2 * b)
                nc.vector.tensor_copy(windows[0][:, T4 * b:T4 * b + T4, :], turn_ps[:, (2 * b) % 4]).then_inc(copied.sem, 1)
            with dve.Fori(0, GROUPS // 2) as it:
                for i in range(2):
                    dve.wait_ge(fir_free.sem, it * 2 + i + 1)
                    for w in range(2):
                        last = nc.vector.tensor_copy(staged[i][:, w], windows[w][:, :, bass.ds((it * 2 + i) * G, G)])
                    last.then_inc(stage_ready.sem, 1)

        @block.scalar
        def _(act):
            for n in loads:
                act.dma_start(keep[n][:], d[n]).then_inc(weights_in.sem, 16)
            for b in range(B):
                act.wait_ge(turned.sem, 2 * b + 2)
                act.wait_ge(copied.sem, 2 * b + 1)
                last = nc.scalar.activation(windows[1][:, T4 * b:T4 * b + T4, :], turn_ps[:, (2 * b + 1) % 4], ACT.Copy)
                if b < B - 1:
                    last.then_inc(copied.sem, 1)
                else:
                    last.then_inc(fir_free.sem, 2)
            with act.Fori(0, GROUPS // 2) as it:
                for i in range(2):
                    act.wait_ge(fir_ps.sem, it * 2 + i + 1)
                    nc.scalar.activation(fl_tok[:, :, bass.ds((it * 2 + i) * G, G)], ps[i][:], ACT.Copy).then_inc(fir_free.sem, 1)
            act.wait_ge(weights_in.sem, 16 * len(loads))


GROUP = 4
GT = GROUP * T4


class Normer:

    def __init__(self, nc, ctx, name, norms, steps, ident, still, eps, z=None):
        def sb(part, shape):
            return ctx.enter_context(nc.sbuf_tensor(f"{name}_{part}", shape, F32))

        def signal(part, per):
            return Signal(ctx.enter_context(nc.semaphore(f"{name}_{part}")), per)

        self.nc, self.ident, self.still, self.eps = nc, ident, still, eps
        self.st6, self.mv, self.std, self.z = sb("st6", [P, GROUP, T4, 6]), sb("mv", [P, GROUP, T4, 2]), sb("std", [P, GROUP, T4]), z if z is not None else sb("z", [P, GROUP, T4, H])
        self.aggregated = signal("aggregated", GROUP * norms)
        self.std_ready = signal("std_ready", GROUP * norms)
        self.z_ready = signal("z_ready", GROUP * norms)
        self.zT_ps = signal("zT_ps", GROUP * norms)
        self.zT_ready = signal("zT_ready", GROUP * norms)
        self.steps = Chain(ctx.enter_context(nc.semaphore(f"{name}_dve")), steps)

    def all(self):
        return [self.z_ready, self.std_ready, self.zT_ready]

    def step(self, ins):
        ins.then_inc(self.steps.sem, 1)
        return self.steps.next()

    def need(self, dve, it, k):
        dve.wait_ge(self.steps.sem, it * self.steps.per + k)

    def vector(self, dve, it, n, xs):
        nc = self.nc
        done = [0] * GROUP
        nc.vector.memset(self.still[:, GROUP:GROUP + 1], 0.0)
        for s in range(GROUP):
            for t in range(T4):
                last = nc.vector.bn_stats(self.st6[:, s, t, :], xs(s)[:, t, :])
            done[s] = self.step(last)
        for s in range(GROUP):
            self.need(dve, it, done[s])
            nc.vector.memset(self.still[:, s:s + 1], 0.0)
            for t in range(T4):
                last = nc.vector.bn_aggr(self.mv[:, s, t, :], self.st6[:, s, t, :])
            last.then_inc(self.aggregated.sem, 1)
        for s in range(GROUP):
            dve.wait_ge(self.std_ready.sem, self.std_ready.at(it, GROUP * n + s + 1))
            done[s] = self.step(nc.vector.reciprocal(self.std[:, s], self.std[:, s]))
        for s in range(GROUP):
            self.need(dve, it, done[s])
            for t in range(T4):
                last = nc.vector.tensor_scalar(self.z[:, s, t, :], xs(s)[:, t, :], self.mv[:, s, t, 0:1], self.std[:, s, t:t + 1], ALU.subtract, ALU.mult)
            last.then_inc(self.z_ready.sem, 1)

    def scalar(self, act, it, n):
        for s in range(GROUP):
            act.wait_ge(self.aggregated.sem, self.aggregated.at(it, GROUP * n + s + 1))
            self.nc.scalar.activation(self.std[:, s], self.mv[:, s, :, 1], ACT.Sqrt, bias=self.eps[:, 0:1]).then_inc(self.std_ready.sem, 1)

    def scalar_out(self, act, it, n, s, dst, bank):
        act.wait_ge(self.zT_ps.sem, self.zT_ps.at(it, GROUP * n + s + 1))
        self.nc.scalar.activation(dst, bank[:], ACT.Copy).then_inc(self.zT_ready.sem, 1)

    def tensor(self, pe, it, n, s, bank):
        pe.wait_ge(self.z_ready.sem, self.z_ready.at(it, GROUP * n + s + 1))
        for t in range(T4):
            last = self.nc.tensor.transpose(bank[:, t * P:(t + 1) * P], self.z[:, s, t, :], self.ident[:])
        last.then_inc(self.zT_ps.sem, 1)

    def turned(self, pe, it, n, s):
        pe.wait_ge(self.zT_ready.sem, self.zT_ready.at(it, GROUP * n + s + 1))


def gate_phase(nc, d, keep):
    with ExitStack() as ctx:
        def sb(name, shape, dt=F32):
            return ctx.enter_context(nc.sbuf_tensor(name, shape, dt))

        def signal(name, per):
            return Signal(ctx.enter_context(nc.semaphore(name)), per)

        K = keep
        ident, v_tok, d_tok, fs_tok, fl_tok, x_all = (K[n] for n in ("ident", "v_tok", "d_tok", "fs_tok", "fl_tok", "x_all"))
        x_new, zT_all = v_tok, d_tok
        TH = T4 * NH
        zT = sb("zT", [H, GROUP, L])
        cen = sb("cen", [P, GROUP, 4, T4 * H])
        br = sb("br", [P, GROUP, T4, 2, 4 * NH])
        sT = sb("sT", [32, GROUP, L])
        hT = sb("hT", [P, GROUP, 2, L])
        lg = sb("lg", [P, GROUP, TH, 4])
        lgm = sb("lgm", [P, GROUP, TH])
        mix = sb("mix", [P, GROUP, T4 * H])
        rr = sb("rr", [P, GROUP, TH])
        oT = cen[:, :, 1]
        xb = mix.rearrange("p s (t c) -> p s t c", t=T4)
        ps = [[ctx.enter_context(nc.psum_tensor(f"gps{s}{i}", [P, 512], F32)) for i in range(2)] for s in range(GROUP)]

        N = Normer(nc, ctx, "gn", 3, 15 * GROUP, ident, K["still"], K["eps5"], z=hT[:, :, 0].rearrange("p s (t c) -> p s t c", t=T4))
        pool_step = Chain(ctx.enter_context(nc.semaphore("gpool")), GROUP)
        mean_ready = signal("mean_ready", GROUP)
        cen_ready = signal("cen_ready", 3 * GROUP)
        cen_v_ready = signal("cen_v_ready", GROUP)
        sqr_ready = signal("sqr_ready", 4 * GROUP)
        var4_ready = signal("var4_ready", GROUP)
        br_ready = signal("br_ready", GROUP)
        sT_ps = signal("sT_ps", GROUP)
        sT_ready = signal("sT_ready", GROUP)
        h_ps = signal("h_ps", 2 * GROUP)
        h_ready = signal("h_ready", 2 * GROUP)
        lg_ps = signal("lg_ps", GROUP)
        lg_ready = signal("lg_ready", GROUP)
        e_ready = signal("e_ready", GROUP)
        w_ready = signal("w_ready", GROUP)
        firs_mixed = signal("firs_mixed", GROUP)
        mix_ready = signal("mix_ready", GROUP)
        msq_ready = signal("msq_ready", GROUP)
        mvar_ready = signal("mvar_ready", GROUP)
        mstd = signal("gstd", GROUP)
        on_ready = signal("on_ready", GROUP)
        oT_ps = signal("oT_ps", GROUP)
        oT_ready = signal("oT_ready", GROUP)
        wo_ps = signal("wo_ps", GROUP)
        x_mixed = signal("x_mixed", GROUP)
        xb_ready = signal("xb_ready", GROUP)
        ff_ps = signal("ff_ps", GROUP)
        ff_done = signal("ff_done", GROUP)
        everything = N.all() + [sqr_ready, cen_v_ready, br_ready, sT_ready, h_ready, lg_ready, e_ready, firs_mixed, mix_ready,
                                msq_ready, mstd, on_ready, oT_ready, xb_ready, ff_done]
        block = ctx.enter_context(nc.Block())

        def round_over(eng, it):
            for s in everything:
                eng.wait_ge(s.sem, s.at(it))

        def tiles(a, it, s):
            return a[:, bass.ds(it * GT + T4 * s, T4), :]

        def by_head(a, it, s):
            return tiles(a, it, s).rearrange("p t (h c) -> p (t h) c", c=DK)

        def heads(a):
            return a.rearrange("p (g c) -> p g c", c=DK)

        def wide(a):
            return a.unsqueeze(2).broadcast_to([P, TH, DK])

        def by_head4(a, it, s):
            return tiles(a, it, s).rearrange("p t (h c) -> p t h c", c=DK)

        def heads4(a):
            return a.rearrange("p (t h c) -> p t h c", t=T4, c=DK)

        def stat(s, m, j):
            return br[:, s, :, m, NH * j:NH * j + NH]

        def wide4(a):
            return a.unsqueeze(3).broadcast_to([P, T4, NH, DK])

        SRCS = (fs_tok, fl_tok, d_tok, v_tok)

        @block.gpsimd
        def _(pool):
            with pool.Fori(0, B // GROUP) as it:
                for s in range(GROUP):
                    pool.wait_ge(mean_ready.sem, mean_ready.at(it, s + 1))
                    nc.gpsimd.tensor_tensor(heads4(cen[:, s, 3]), by_head4(v_tok, it, s), wide4(stat(s, 0, 3)), ALU.subtract).then_inc(cen_v_ready.sem, 1)
                for s in range(GROUP):
                    pool.wait_ge(w_ready.sem, w_ready.at(it, s + 1))
                    for j in range(2):
                        last = nc.gpsimd.tensor_tensor(heads(cen[:, s, j]), by_head(SRCS[j], it, s), lg[:, s, :, j:j + 1].broadcast_to([P, TH, DK]), ALU.mult)
                    last.then_inc(pool_step.sem, 1)
                    pool.wait_ge(pool_step.sem, it * pool_step.per + pool_step.next())
                    nc.gpsimd.tensor_tensor(cen[:, s, 0], cen[:, s, 0], cen[:, s, 1], ALU.add).then_inc(firs_mixed.sem, 1)
                for s in range(GROUP):
                    pool.wait_ge(x_mixed.sem, x_mixed.at(it, s + 1))
                    nc.gpsimd.tensor_tensor(xb[:, s], tiles(x_all, it, s), K["bias"][:].unsqueeze(1).broadcast_to([P, T4, H]), ALU.add).then_inc(xb_ready.sem, 1)
                round_over(pool, it)

        @block.scalar
        def _(act):
            with act.Fori(0, B // GROUP) as it:
                N.scalar(act, it, 0)
                for s in range(GROUP):
                    N.scalar_out(act, it, 0, s, zT[:, s], ps[s][0])
                for s in range(GROUP):
                    for j in (0, 1, 2, 3):
                        if j < 3:
                            act.wait_ge(cen_ready.sem, cen_ready.at(it, 3 * s + j + 1))
                        else:
                            act.wait_ge(cen_v_ready.sem, cen_v_ready.at(it, s + 1))
                        nc.scalar.activation(cen[:, s, j], cen[:, s, j], ACT.Square).then_inc(sqr_ready.sem, 1)
                for s in range(GROUP):
                    act.wait_ge(var4_ready.sem, var4_ready.at(it, s + 1))
                    v = br[:, s, :, 1]
                    nc.scalar.activation(v, v, ACT.Sqrt).then_inc(br_ready.sem, 1)
                for s in range(GROUP):
                    act.wait_ge(sT_ps.sem, sT_ps.at(it, s + 1))
                    nc.scalar.activation(sT[:, s], ps[s][1][0:32, :], ACT.Copy).then_inc(sT_ready.sem, 1)
                for s in range(GROUP):
                    for m in range(2):
                        act.wait_ge(h_ps.sem, h_ps.at(it, 2 * s + m + 1))
                        nc.scalar.activation(hT[:, s, m, :], ps[s][m][:], ACT.Gelu, bias=K["b1"][:, m:m + 1]).then_inc(h_ready.sem, 1)
                for s in range(GROUP):
                    act.wait_ge(lg_ready.sem, lg_ready.at(it, s + 1))
                    nc.scalar.activation(lg[:, s], lg[:, s], ACT.Exp).then_inc(e_ready.sem, 1)
                for s in range(GROUP):
                    act.wait_ge(mix_ready.sem, mix_ready.at(it, s + 1))
                    nc.scalar.activation(cen[:, s, 3], mix[:, s], ACT.Square).then_inc(msq_ready.sem, 1)
                for s in range(GROUP):
                    act.wait_ge(mvar_ready.sem, mvar_ready.at(it, s + 1))
                    nc.scalar.activation(rr[:, s], rr[:, s], ACT.Sqrt, bias=K["eps5"][:, 0:1], scale=1.0 / DK).then_inc(mstd.sem, 1)
                for s in range(GROUP):
                    act.wait_ge(oT_ps.sem, oT_ps.at(it, s + 1))
                    nc.scalar.activation(oT[:, s], ps[s][1][:], ACT.Copy).then_inc(oT_ready.sem, 1)
                N.scalar(act, it, 1)
                for s in range(GROUP):
                    N.scalar_out(act, it, 1, s, zT[:, s], ps[s][1])
                N.scalar(act, it, 2)
                for s in range(GROUP):
                    N.scalar_out(act, it, 2, s, tiles(zT_all, it, s).rearrange("p t c -> p (t c)"), ps[s][1])
                round_over(act, it)

        @block.vector
        def _(dve):
            with dve.Fori(0, B // GROUP) as it:
                def xs(s):
                    return tiles(x_all, it, s)

                done = [0] * GROUP
                N.vector(dve, it, 0, xs)
                for s in range(GROUP):
                    for j in range(4):
                        last = nc.vector.tensor_reduce(stat(s, 0, j), by_head4(SRCS[j], it, s), AX.X, ALU.add)
                    done[s] = N.step(last)
                for s in range(GROUP):
                    N.need(dve, it, done[s])
                    m = br[:, s, :, 0]
                    nc.vector.tensor_scalar(m, m, 1.0 / DK, None, ALU.mult).then_inc(mean_ready.sem, 1)
                for s in range(GROUP):
                    dve.wait_ge(mean_ready.sem, mean_ready.at(it, s + 1))
                    for j in range(3):
                        nc.vector.tensor_tensor(heads4(cen[:, s, j]), by_head4(SRCS[j], it, s), wide4(stat(s, 0, j)), ALU.subtract).then_inc(cen_ready.sem, 1)
                for s in range(GROUP):
                    for j in range(4):
                        dve.wait_ge(sqr_ready.sem, sqr_ready.at(it, 4 * s + j + 1))
                        last = nc.vector.tensor_reduce(stat(s, 1, j), heads4(cen[:, s, j]), AX.X, ALU.add)
                    done[s] = N.step(last)
                for s in range(GROUP):
                    N.need(dve, it, done[s])
                    v = br[:, s, :, 1]
                    nc.vector.tensor_scalar(v, v, 1.0 / DK, 1e-6, ALU.mult, ALU.max).then_inc(var4_ready.sem, 1)
                for s in range(GROUP):
                    dve.wait_ge(lg_ps.sem, lg_ps.at(it, s + 1))
                    done[s] = N.step(nc.vector.tensor_tensor(
                        lg[:, s].rearrange("p (t h) j -> p t (h j)", t=T4), ps[s][0][:, 0:4 * TH].rearrange("p (t x) -> p t x", t=T4),
                        K["b2"][:].unsqueeze(1).broadcast_to([P, T4, 4 * NH]), ALU.add))
                for s in range(GROUP):
                    N.need(dve, it, done[s])
                    done[s] = N.step(nc.vector.tensor_reduce(lgm[:, s], lg[:, s], AX.X, ALU.max))
                for s in range(GROUP):
                    N.need(dve, it, done[s])
                    nc.vector.tensor_tensor(lg[:, s], lg[:, s], lgm[:, s].unsqueeze(2).broadcast_to([P, TH, 4]), ALU.subtract).then_inc(lg_ready.sem, 1)
                for s in range(GROUP):
                    dve.wait_ge(e_ready.sem, e_ready.at(it, s + 1))
                    done[s] = N.step(nc.vector.tensor_reduce(lgm[:, s], lg[:, s], AX.X, ALU.add))
                for s in range(GROUP):
                    N.need(dve, it, done[s])
                    done[s] = N.step(nc.vector.reciprocal(lgm[:, s], lgm[:, s]))
                for s in range(GROUP):
                    N.need(dve, it, done[s])
                    nc.vector.tensor_tensor(lg[:, s], lg[:, s], lgm[:, s].unsqueeze(2).broadcast_to([P, TH, 4]), ALU.mult).then_inc(w_ready.sem, 1)
                for s in range(GROUP):
                    dve.wait_ge(w_ready.sem, w_ready.at(it, s + 1))
                    for j, dst in ((2, mix[:, s]), (3, cen[:, s, 2])):
                        last = nc.vector.tensor_tensor(heads(dst), by_head(SRCS[j], it, s), lg[:, s, :, j:j + 1].broadcast_to([P, TH, DK]), ALU.mult)
                    done[s] = N.step(last)
                for s in range(GROUP):
                    N.need(dve, it, done[s])
                    done[s] = N.step(nc.vector.tensor_tensor(mix[:, s], mix[:, s], cen[:, s, 2], ALU.add))
                for s in range(GROUP):
                    N.need(dve, it, done[s])
                    dve.wait_ge(firs_mixed.sem, firs_mixed.at(it, s + 1))
                    nc.vector.tensor_tensor(mix[:, s], mix[:, s], cen[:, s, 0], ALU.add).then_inc(mix_ready.sem, 1)
                for s in range(GROUP):
                    dve.wait_ge(msq_ready.sem, msq_ready.at(it, s + 1))
                    nc.vector.tensor_reduce(rr[:, s], heads(cen[:, s, 3]), AX.X, ALU.add).then_inc(mvar_ready.sem, 1)
                for s in range(GROUP):
                    dve.wait_ge(mstd.sem, mstd.at(it, s + 1))
                    done[s] = N.step(nc.vector.reciprocal(rr[:, s], rr[:, s]))
                for s in range(GROUP):
                    N.need(dve, it, done[s])
                    nc.vector.tensor_tensor(heads(mix[:, s]), heads(mix[:, s]), wide(rr[:, s]), ALU.mult).then_inc(on_ready.sem, 1)
                for s in range(GROUP):
                    dve.wait_ge(wo_ps.sem, wo_ps.at(it, s + 1))
                    nc.vector.tensor_tensor(xs(s), xs(s), ps[s][0][:].rearrange("p (t c) -> p t c", t=T4), ALU.add).then_inc(x_mixed.sem, 1)
                dve.wait_ge(x_mixed.sem, x_mixed.at(it))
                N.vector(dve, it, 1, xs)
                for s in range(GROUP):
                    dve.wait_ge(ff_ps.sem, ff_ps.at(it, s + 1))
                    dve.wait_ge(xb_ready.sem, xb_ready.at(it, s + 1))
                    nc.vector.tensor_tensor(tiles(x_new, it, s), xb[:, s], ps[s][0][:].rearrange("p (t c) -> p t c", t=T4), ALU.add).then_inc(ff_done.sem, 1)
                dve.wait_ge(ff_done.sem, ff_done.at(it))
                N.vector(dve, it, 2, lambda s: tiles(x_new, it, s))
                round_over(dve, it)
            assert N.steps.k == N.steps.per, N.steps.k

        @block.tensor
        def _(pe):
            with pe.Fori(0, B // GROUP) as it:
                for s in range(GROUP):
                    N.tensor(pe, it, 0, s, ps[s][0])
                N.turned(pe, it, 0, GROUP - 1)
                for s in range(GROUP):
                    nc.tensor.matmul(ps[s][0][:], K["w1x"][:, 0:P], zT[:, s], start=True, stop=False)
                for s in range(GROUP):
                    pe.wait_ge(br_ready.sem, br_ready.at(it, s + 1))
                    for t in range(T4):
                        last = nc.tensor.transpose(ps[s][1][0:32, t * P:(t + 1) * P], br[:, s, t].rearrange("p m x -> p (m x)"), ident[:])
                    last.then_inc(sT_ps.sem, 1)
                for s in range(GROUP):
                    pe.wait_ge(sT_ready.sem, sT_ready.at(it, s + 1))
                    nc.tensor.matmul(ps[s][0][:], K["w1s"][0:32, 0:P], sT[:, s], start=False, stop=True).then_inc(h_ps.sem, 1)
                    nc.tensor.matmul(ps[s][1][:], K["w1x"][:, P:MH], zT[:, s], start=True, stop=False)
                    nc.tensor.matmul(ps[s][1][:], K["w1s"][0:32, P:MH], sT[:, s], start=False, stop=True).then_inc(h_ps.sem, 1)
                for s in range(GROUP):
                    pe.wait_ge(h_ready.sem, h_ready.at(it, 2 * s + 2))
                    for t in range(T4):
                        dst = ps[s][0][:, 16 * t:16 * t + 16]
                        for m in range(2):
                            last = nc.tensor.matmul(dst, hT[:, s, m, t * P:(t + 1) * P], K["w2"][:, m, :], start=m == 0, stop=m == 1)
                    last.then_inc(lg_ps.sem, 1)
                for s in range(GROUP):
                    pe.wait_ge(on_ready.sem, on_ready.at(it, s + 1))
                    for t in range(T4):
                        last = nc.tensor.transpose(ps[s][1][:, t * P:(t + 1) * P], mix[:, s, t * P:(t + 1) * P], ident[:])
                    last.then_inc(oT_ps.sem, 1)
                for s in range(GROUP):
                    pe.wait_ge(oT_ready.sem, oT_ready.at(it, s + 1))
                    for t in range(T4):
                        last = nc.tensor.matmul(ps[s][0][:, t * P:(t + 1) * P], oT[:, s, t * P:(t + 1) * P], K["wo_a"][:], start=True, stop=True)
                    last.then_inc(wo_ps.sem, 1)
                for s in range(GROUP):
                    N.tensor(pe, it, 1, s, ps[s][1])
                for s in range(GROUP):
                    N.turned(pe, it, 1, s)
                    for t in range(T4):
                        last = nc.tensor.matmul(ps[s][0][:, t * P:(t + 1) * P], zT[:, s, t * P:(t + 1) * P], K["cbT"][:], start=True, stop=True)
                    last.then_inc(ff_ps.sem, 1)
                for s in range(GROUP):
                    N.tensor(pe, it, 2, s, ps[s][1])
                round_over(pe, it)


def last_phase(nc, d, keep):
    with ExitStack() as ctx:
        def sb(name, shape, dt=F32):
            return ctx.enter_context(nc.sbuf_tensor(name, shape, dt))

        def signal(name, per):
            return Signal(ctx.enter_context(nc.semaphore(name)), per)

        K, x_all = keep, keep["v_tok"]
        zT = sb("lzT", [H, GROUP, L])
        xb = sb("lxb", [P, GROUP, T4, H])
        ps = [[ctx.enter_context(nc.psum_tensor(f"lps{s}{i}", [P, 512], F32)) for i in range(2)] for s in range(GROUP)]
        N = Normer(nc, ctx, "ln", 1, 2 * GROUP, K["ident"], K["still"], K["eps5"])
        xb_ready = signal("lxb_ready", GROUP)
        ff_ps = signal("lff_ps", GROUP)
        ff_done = signal("lff_done", GROUP)
        stored = signal("stored", 16)
        everything = N.all() + [xb_ready, ff_done]
        block = ctx.enter_context(nc.Block())

        def round_over(eng, it):
            for s in everything:
                eng.wait_ge(s.sem, s.at(it))

        def tiles(a, it, s):
            return a[:, bass.ds(it * GT + T4 * s, T4), :]

        @block.gpsimd
        def _(pool):
            with pool.Fori(0, B // GROUP) as it:
                for s in range(GROUP):
                    nc.gpsimd.tensor_tensor(xb[:, s], tiles(x_all, it, s), K["bias"][:].unsqueeze(1).broadcast_to([P, T4, H]), ALU.add).then_inc(xb_ready.sem, 1)
                round_over(pool, it)

        @block.scalar
        def _(act):
            with act.Fori(0, B // GROUP) as it:
                N.scalar(act, it, 0)
                for s in range(GROUP):
                    N.scalar_out(act, it, 0, s, zT[:, s], ps[s][0])
                act.wait_ge(ff_done.sem, ff_done.at(it))
                act.dma_start(d["out"][:, bass.ds(it * GT, GT), :], x_all[:, bass.ds(it * GT, GT), :]).then_inc(stored.sem, 16)
                round_over(act, it)
            act.wait_ge(stored.sem, 16 * (B // GROUP))

        @block.vector
        def _(dve):
            with dve.Fori(0, B // GROUP) as it:
                N.vector(dve, it, 0, lambda s: tiles(x_all, it, s))
                for s in range(GROUP):
                    dve.wait_ge(ff_ps.sem, ff_ps.at(it, s + 1))
                    dve.wait_ge(xb_ready.sem, xb_ready.at(it, s + 1))
                    nc.vector.tensor_tensor(tiles(x_all, it, s), xb[:, s], ps[s][1][:].rearrange("p (t c) -> p t c", t=T4), ALU.add).then_inc(ff_done.sem, 1)
                round_over(dve, it)
            assert N.steps.k == N.steps.per, N.steps.k

        @block.tensor
        def _(pe):
            with pe.Fori(0, B // GROUP) as it:
                for s in range(GROUP):
                    N.tensor(pe, it, 0, s, ps[s][0])
                for s in range(GROUP):
                    N.turned(pe, it, 0, s)
                    for t in range(T4):
                        last = nc.tensor.matmul(ps[s][1][:, t * P:(t + 1) * P], zT[:, s, t * P:(t + 1) * P], K["cbT"][:], start=True, stop=True)
                    last.then_inc(ff_ps.sem, 1)
                round_over(pe, it)


def attention_phase(nc, keep):
    with ExitStack() as ctx:
        def sb(name, shape, dt=F32):
            return ctx.enter_context(nc.sbuf_tensor(name, shape, dt))

        def signal(name, per):
            return Signal(ctx.enter_context(nc.semaphore(name)), per)

        K = keep
        ident, x_all, zT_all = K["ident"], K["v_tok"], K["d_tok"]
        HH = HA // 2
        W = HH * DH
        zT = sb("azT", [H, L])
        V = K["fs_tok"][:].rearrange("p (g t a) c -> p g t (a c)", g=2, t=T4)
        ra = K["fl_tok"][:].rearrange("p (n a) c -> p n (a c)", n=2 * T4)
        rb = sb("rb", [P, 2, W])
        sqb = sb("sqb", [P, 2, W])
        ss = sb("ss", [P, 2 * T4, HH])
        kTh = sb("kTh", [P, 2, HH // 2, L], F16)
        kTl = sb("kTl", [P, 2, HH // 2, L], F16)
        qTh = sb("qTh", [P, 2, HH, L], F16)
        qTl = sb("qTl", [P, 2, HH, L], F16)
        nmx = sb("nmx", [P, 4])
        rs = sb("rs", [P, 2, T4])
        Pm = sb("Pm", [P, 4, L])
        PT_ = sb("PTs", [P, 4, L])
        O = sb("O", [P, 2, T4, 2 * DH])
        OT = sb("OT", [P, 2, L])
        ps = [ctx.enter_context(nc.psum_tensor(f"aps{i}", [P, 512], F32)) for i in range(8)]
        S_BANK, PT_BANK, O_BANK, Q_BANK = ps[0:3], ps[3:5], ps[5:7], ps[7]
        OT_BANK = O_BANK[1]

        z0 = ctx.enter_context(nc.semaphore("z0"))
        z_in = signal("az_in", 1)
        proj = signal("proj", 12)
        sq_done = signal("sq_done", 8)
        v_done = signal("v_done", 4)
        ss_done = signal("ss_done", 8)
        rms_done = signal("rms_done", 1)
        inv_done = signal("inv_done", 1)
        rot_done = signal("rot_done", 8)
        add_done = signal("add_done", 8)
        rope_done = signal("rope_done", 8)
        tr_ps = signal("tr_ps", 8)
        hi_done = signal("hi_done", 8)
        lo_done = signal("lo_done", 8)
        s_ps = signal("s_ps", UNITS)
        max_done = signal("max_done", UNITS)
        p_done = signal("p_done", UNITS)
        pt_ps = signal("pt_ps", UNITS)
        pt_done = [signal("pt_done_dve", UNITS - HA), signal("pt_done_act", HA)]
        o_ps = signal("mo_ps", UNITS)
        rs_done = signal("rs_done", HA)
        o_done = signal("mo_done", HA)
        ot_ps = signal("ot_ps", HA // 2)
        ot_done = signal("ot_done", HA // 2)
        y_ps = signal("y_ps", HA // 2)
        x_done = signal("x_done", HA // 2)
        block = ctx.enter_context(nc.Block())

        def transposed(it, u):
            h, i = UN[u]
            return (pt_done[1].sem, pt_done[1].at(it, h + 1)) if i == T4 - 1 else (pt_done[0].sem, pt_done[0].at(it, (T4 - 1) * h + i + 1))

        LATE = 8
        UN = [(u // T4, u % T4) for u in range(UNITS + LATE)]
        HALF = UNITS // 2
        KQ = [(t, m) for t in range(T4) for m in "kq"]
        EVENTS = [("p", n) for n in range(len(KQ))] + [("v", t) for t in range(T4)] + [("t", n) for n in range(len(KQ))]
        LAST_SUM = len(KQ) - 1


        def units_held(e):
            kind, n = EVENTS[e]
            return 1 if kind == "v" or kind == "t" and KQ[n][1] == "k" else 2

        AT_UNIT = [sum(units_held(b) for b in range(e)) for e in range(len(EVENTS))]
        assert AT_UNIT[-1] < HALF

        def beside(u):
            return [e for e in range(len(EVENTS)) if AT_UNIT[e] == u % HALF]

        @block.gpsimd
        def _(pool):
            nc.gpsimd.memset(qTh[:], 0.0).then_inc(z0, 1)
            nc.gpsimd.memset(qTl[:], 0.0).then_inc(z0, 1)

            def rope(st):
                for n in range(len(KQ)):
                    pool.wait_ge(rot_done.sem, rot_done.at(st, n + 1))
                    nc.gpsimd.tensor_tensor(ra[:, n], ra[:, n], rb[:, n % 2], ALU.add).then_inc(add_done.sem, 1)
                pool.wait_ge(add_done.sem, add_done.at(st))
                pool.wait_ge(inv_done.sem, inv_done.at(st))
                for n in range(len(KQ)):
                    a3 = ra[:, n].rearrange("p (h c) -> p h c", c=DH)
                    nc.gpsimd.tensor_tensor(a3, a3, ss[:, n].unsqueeze(2).broadcast_to([P, HH, DH]), ALU.mult).then_inc(rope_done.sem, 1)

            rope(0)
            with pool.Fori(0, B - 1) as it:
                rope(it * 2 + 1)
                rope(it * 2 + 2)
            rope(2 * B - 1)

        @block.scalar
        def _(act):
            act.wait_ge(z0, 2)

            def load_z(n):
                nc.scalar.activation(zT[:], zT_all[:, bass.ds(n * T4, T4), :].rearrange("p t c -> p (t c)"), ACT.Copy).then_inc(z_in.sem, 1)

            def event(st, g, e):
                kind, n = EVENTS[e]
                if kind == "p":
                    act.wait_ge(proj.sem, proj.at(st, e + 1))
                    if n >= 2:
                        act.wait_ge(ss_done.sem, ss_done.at(st, n - 1))
                    nc.scalar.activation(sqb[:, n % 2], Q_BANK[:], ACT.Square).then_inc(sq_done.sem, 1)
                elif kind == "v":
                    act.wait_ge(proj.sem, proj.at(st, e + 1))
                    nc.scalar.activation(V[:, g, n], Q_BANK[:], ACT.Copy).then_inc(v_done.sem, 1)
                else:
                    act.wait_ge(tr_ps.sem, tr_ps.at(st, n + 1))
                    src = Q_BANK[:].rearrange("p (a t) -> p a t", t=P)
                    t, m = KQ[n]
                    ts = slice(t * P, t * P + P)
                    if m == "k":
                        nc.scalar.activation(kTh[:, g, :, ts], src, ACT.Copy).then_inc(hi_done.sem, 1)
                    else:
                        nc.scalar.activation(qTh[0:DH, g, 0::2, ts], src[0:DH], ACT.Copy)
                        nc.scalar.activation(qTh[DH:P, g, 1::2, ts], src[DH:P], ACT.Copy).then_inc(hi_done.sem, 1)

            def root(st):
                act.wait_ge(ss_done.sem, ss_done.at(st))
                nc.scalar.activation(ss[:], ss[:], ACT.Sqrt, bias=K["eps6"][:, 0:1], scale=1.0 / DH).then_inc(rms_done.sem, 1)

            def ot(it, g):
                act.wait_ge(ot_ps.sem, ot_ps.at(it, g + 1))
                if g >= 2:
                    act.wait_ge(y_ps.sem, y_ps.at(it, g - 1))
                nc.scalar.activation(OT[:, g % 2, :], OT_BANK[:], ACT.Copy).then_inc(ot_done.sem, 1)

            def widest_out(it, h):
                u = T4 * h + T4 - 1
                act.wait_ge(pt_ps.sem, pt_ps.at(it, u + 1))
                act.wait_ge(o_ps.sem, o_ps.at(it, u - 2))
                nc.scalar.activation(PT_[:, u % 4, :], PT_BANK[u % 2][:], ACT.Copy).then_inc(pt_done[1].sem, 1)

            def units(it, us, more=True):
                for u in us:
                    h, i = UN[u]
                    w = P * (i + 1)
                    if u == HALF and more:
                        act.wait_ge(proj.sem, proj.at(it * 2 + 1))
                        load_z(it + 1)
                    if u < HALF or more:
                        st, g = it * 2 + 1 + u // HALF, 1 - u // HALF % 2
                        for e in beside(u):
                            if EVENTS[e] == ("v", 0) and u >= HALF:
                                act.wait_ge(o_ps.sem, o_ps.at(it, HALF))
                            event(st, g, e)
                        if u % HALF == AT_UNIT[LAST_SUM] + 2:
                            root(st)
                    if i == 1 and h and (h - 1 < HA or more):
                        widest_out(it, h - 1)
                    if u < UNITS or more:
                        act.wait_ge(max_done.sem, max_done.at(it, u + 1))
                        if u >= 3:
                            act.wait_ge(pt_ps.sem, pt_ps.at(it, u - 2))
                        if i == 0 and h >= 2:
                            act.wait_ge(o_done.sem, o_done.at(it, h - 1))
                        nc.scalar.activation(Pm[:, u % 4, 0:w], S_BANK[u % UNITS % 3][:, 0:w], ACT.Exp, bias=nmx[:, u % 4:u % 4 + 1],
                                             accum_out=rs[:, h % 2, i:i + 1]).then_inc(p_done.sem, 1)
                    if i == 0 and h % 2 and h >= 3:
                        ot(it, h // 2 - 1)

            load_z(0)
            for e in range(len(EVENTS)):
                event(0, 0, e)
                if e == LAST_SUM + 1:
                    root(0)
            units(0, range(LATE))
            with act.Fori(0, B - 1) as it:
                units(it, range(LATE, UNITS + LATE))
            units(B - 1, range(LATE, UNITS + LATE), False)

        @block.vector
        def _(dve):
            dve.wait_ge(z0, 2)

            def event(st, g, e):
                kind, n = EVENTS[e]
                if kind == "v":
                    return
                t, m = KQ[n]
                if kind == "p":
                    tab = K["rope"][:, 0 if m == "k" else 1, t]
                    b4 = Q_BANK[:].rearrange("p (h w c) -> p h w c", w=2, c=DH // 2)
                    r4 = rb[:, n % 2].rearrange("p (h w c) -> p h w c", w=2, c=DH // 2)
                    dve.wait_ge(sq_done.sem, sq_done.at(st, n + 1))
                    nc.vector.tensor_tensor(ra[:, n].rearrange("p (h c) -> p h c", c=DH), Q_BANK[:].rearrange("p (h c) -> p h c", c=DH),
                                            tab[:, 0:1].broadcast_to([P, HH, DH]), ALU.mult)
                    if n >= 2:
                        dve.wait_ge(add_done.sem, add_done.at(st, n - 1))
                    nc.vector.tensor_tensor(r4[:, :, 0], b4[:, :, 1], tab[:, 1:2, 0:32].broadcast_to([P, HH, 32]), ALU.mult)
                    nc.vector.tensor_tensor(r4[:, :, 1], b4[:, :, 0], tab[:, 1:2, 32:64].broadcast_to([P, HH, 32]), ALU.mult).then_inc(rot_done.sem, 1)
                else:
                    dve.wait_ge(hi_done.sem, hi_done.at(st, n + 1))
                    src = Q_BANK[:].rearrange("p (a t) -> p a t", t=P)
                    ts = slice(t * P, t * P + P)
                    if m == "k":
                        nc.vector.tensor_tensor(kTl[:, g, :, ts], src, kTh[:, g, :, ts], ALU.subtract).then_inc(lo_done.sem, 1)
                    else:
                        nc.vector.tensor_tensor(qTl[0:DH, g, 0::2, ts], src[0:DH], qTh[0:DH, g, 0::2, ts], ALU.subtract)
                        nc.vector.tensor_tensor(qTl[DH:P, g, 1::2, ts], src[DH:P], qTh[DH:P, g, 1::2, ts], ALU.subtract).then_inc(lo_done.sem, 1)

            def sums(st, e):
                kind, n = EVENTS[e]
                if kind == "p":
                    nc.vector.tensor_reduce(ss[:, n], sqb[:, n % 2].rearrange("p (h c) -> p h c", c=DH), AX.X, ALU.add).then_inc(ss_done.sem, 1)

            def inverse_rms(st):
                dve.wait_ge(rms_done.sem, rms_done.at(st))
                nc.vector.reciprocal(ss[:], ss[:]).then_inc(inv_done.sem, 1)

            def pt_out(it, u):
                w = P * (UN[u][1] + 1)
                dve.wait_ge(pt_ps.sem, pt_ps.at(it, u + 1))
                if u >= 3:
                    dve.wait_ge(o_ps.sem, o_ps.at(it, u - 2))
                nc.vector.tensor_copy(PT_[:, u % 4, 0:w], PT_BANK[u % 2][:, 0:w]).then_inc(pt_done[0].sem, 1)

            def inverse_sums(it, h):
                dve.wait_ge(p_done.sem, p_done.at(it, T4 * h + T4))
                nc.vector.reciprocal(rs[:, h % 2], rs[:, h % 2]).then_inc(rs_done.sem, 1)

            def o_out(it, h):
                dve.wait_ge(rs_done.sem, rs_done.at(it, h + 1))
                dve.wait_ge(o_ps.sem, o_ps.at(it, T4 * h + T4))
                if h >= 4:
                    dve.wait_ge(ot_ps.sem, ot_ps.at(it, h // 2 - 1))
                nc.vector.tensor_tensor(O[:, h // 2 % 2, :, DH * (h % 2):DH * (h % 2) + DH], O_BANK[h % 2][:, 0:T4 * DH].rearrange("p (t c) -> p t c", t=T4),
                                        rs[:, h % 2].unsqueeze(2).broadcast_to([P, T4, DH]), ALU.mult).then_inc(o_done.sem, 1)

            def add(it, g):
                dve.wait_ge(y_ps.sem, y_ps.at(it, g + 1))
                if g:
                    dve.wait_ge(x_done.sem, x_done.at(it, g))
                x = x_all[:, bass.ds(it * T4, T4), :]
                nc.vector.tensor_tensor(x, x, OT_BANK[:].rearrange("p (t c) -> p t c", t=T4), ALU.add).then_inc(x_done.sem, 1)

            def units(it, us, more=True):
                for u in us:
                    h, i = UN[u]
                    w = P * (i + 1)
                    if u < UNITS or more:
                        dve.wait_ge(s_ps.sem, s_ps.at(it, u + 1))
                        if u >= 4:
                            dve.wait_ge(p_done.sem, p_done.at(it, u - 3))
                        nc.vector.tensor_reduce(nmx[:, u % 4:u % 4 + 1], S_BANK[u % UNITS % 3][:, 0:w], AX.X, ALU.max, negate=True).then_inc(max_done.sem, 1)
                    if u >= 2 and UN[u - 2][1] < T4 - 1 and (u - 2 < UNITS or more):
                        pt_out(it, u - 2)
                    if i == 2 and h and (h - 1 < HA or more):
                        inverse_sums(it, h - 1)
                    if i == 3 and h and (h - 1 < HA or more):
                        o_out(it, h - 1)
                    if i == 2 and h % 2 and h >= 3:
                        add(it, h // 2 - 1)
                    if u < HALF or more:
                        st, g = it * 2 + 1 + u // HALF, 1 - u // HALF % 2
                        for e in beside(u):
                            event(st, g, e)
                        if u % HALF:
                            for e in beside(u - 1):
                                sums(st, e)
                        if u % HALF == AT_UNIT[LAST_SUM] + 2:
                            inverse_rms(st)

            for e in range(len(EVENTS)):
                event(0, 0, e)
                sums(0, e)
                if e == LAST_SUM + 1:
                    inverse_rms(0)
            units(0, range(LATE))
            with dve.Fori(0, B - 1) as it:
                units(it, range(LATE, UNITS + LATE))
            units(B - 1, range(LATE, UNITS + LATE), False)

        @block.tensor
        def _(pe):
            pe.wait_ge(z0, 2)
            order = {"q": 0, "k": 1, "v": 2}

            def event(st, g, e):
                kind, n = EVENTS[e]
                if e:
                    before, b = EVENTS[e - 1]
                    if before == "p":
                        pe.wait_ge(rot_done.sem, rot_done.at(st, b + 1))
                    elif before == "v":
                        pe.wait_ge(v_done.sem, v_done.at(st, b + 1))
                    else:
                        pe.wait_ge(lo_done.sem, lo_done.at(st, b + 1))
                if kind == "t":
                    pe.wait_ge(rope_done.sem, rope_done.at(st, n + 1))
                    for a in range(HH // 2):
                        last = nc.tensor.transpose(Q_BANK[:, a * P:(a + 1) * P], ra[:, n, a * P:(a + 1) * P], ident[:])
                    last.then_inc(tr_ps.sem, 1)
                else:
                    t, m = KQ[n] if kind == "p" else (n, "v")
                    c0 = order[m] * HA * DH + g * W
                    nc.tensor.matmul(Q_BANK[:], zT[:, t * P:(t + 1) * P], K["wqkvT"][:, c0:c0 + W], start=True, stop=True).then_inc(proj.sem, 1)

            def scores(it, u):
                h, i = UN[u]
                g, hh = h // HH % 2, h % HH
                w = P * (i + 1)
                ts = slice(i * P, i * P + P)
                if u == UNITS:
                    pe.wait_ge(p_done.sem, p_done.at(it, u))
                elif u >= 3:
                    pe.wait_ge(p_done.sem, p_done.at(it, u - 2))
                dst = S_BANK[u % UNITS % 3]
                nc.tensor.matmul(dst[:, 0:w], qTh[:, g, hh, ts], kTh[:, g, hh // 2, 0:w], start=True, stop=False)
                nc.tensor.matmul(dst[:, 0:w], qTl[:, g, hh, ts], kTh[:, g, hh // 2, 0:w], start=False, stop=False)
                nc.tensor.matmul(dst[:, w - P:w], K["identb"][:], K["maskb"][:], start=False, stop=False, skip_group_check=True)
                nc.tensor.matmul(dst[:, 0:w], qTh[:, g, hh, ts], kTl[:, g, hh // 2, 0:w], start=False, stop=True).then_inc(s_ps.sem, 1)

            def turn_p(it, u):
                pe.wait_ge(p_done.sem, p_done.at(it, u + 1))
                if u >= 2:
                    sem, value = transposed(it, u - 2)
                    pe.wait_ge(sem, value)
                for j in range(UN[u][1] + 1):
                    last = nc.tensor.transpose(PT_BANK[u % 2][:, j * P:(j + 1) * P], Pm[:, u % 4, j * P:(j + 1) * P], ident[:])
                last.then_inc(pt_ps.sem, 1)

            def values(it, u):
                h, i = UN[u]
                sem, value = transposed(it, u)
                pe.wait_ge(sem, value)
                if i == 0 and h >= 2:
                    pe.wait_ge(o_done.sem, o_done.at(it, h - 1))
                if i == 0 and h % 2 and h >= 3:
                    pe.wait_ge(x_done.sem, x_done.at(it, h // 2))
                c0 = DH * (h % HH)
                for j in range(i + 1):
                    last = nc.tensor.matmul(O_BANK[h % 2][:, DH * i:DH * i + DH], PT_[:, u % 4, j * P:(j + 1) * P], V[:, h // HH % 2, j, c0:c0 + DH],
                                            start=j == 0, stop=j == i)
                last.then_inc(o_ps.sem, 1)

            def out_pair(it, g):
                pe.wait_ge(o_done.sem, o_done.at(it, 2 * g + 2))
                for t in range(T4):
                    last = nc.tensor.transpose(OT_BANK[:, t * P:(t + 1) * P], O[:, g % 2, t, :], ident[:])
                last.then_inc(ot_ps.sem, 1)

            def out_product(it, g):
                pe.wait_ge(ot_done.sem, ot_done.at(it, g + 1))
                for t in range(T4):
                    last = nc.tensor.matmul(OT_BANK[:, t * P:(t + 1) * P], OT[:, g % 2, t * P:(t + 1) * P], K["woT"][:, g, :], start=True, stop=True)
                last.then_inc(y_ps.sem, 1)

            def units(it, us, more=True):
                for u in us:
                    live = u < UNITS or more
                    if u % HALF == 0 and live:
                        pe.wait_ge(lo_done.sem, lo_done.at(it * 2 + u // HALF))
                        pe.wait_ge(v_done.sem, v_done.at(it * 2 + u // HALF))
                    if live:
                        scores(it, u)
                    if u >= 2 and (u - 2 < UNITS or more):
                        turn_p(it, u - 2)
                    if u < HALF or more:
                        st, g = it * 2 + 1 + u // HALF, 1 - u // HALF % 2
                        for e in beside(u):
                            if e == 0 and HALF <= u < UNITS:
                                pe.wait_ge(z_in.sem, z_in.at(it + 1))
                            event(st, g, e)
                    if u >= 3 and (u - 3 < UNITS or more):
                        values(it, u - 3)
                    h, i = UN[u]
                    if h % 2 and h >= 3:
                        if i == 0:
                            out_pair(it, h // 2 - 1)
                        if i == 1:
                            out_product(it, h // 2 - 1)

            pe.wait_ge(z_in.sem, 1)
            for e in range(len(EVENTS)):
                event(0, 0, e)
            units(0, range(LATE))
            with pe.Fori(0, B - 1) as it:
                units(it, range(LATE, UNITS + LATE))
            units(B - 1, range(LATE, UNITS + LATE), False)

def build_kernel(nc, d, out):
    with ExitStack() as ctx:
        def sb(name, shape, dt=F32):
            return ctx.enter_context(nc.sbuf_tensor(name, shape, dt))

        def load_all(names, sem):
            with nc.Block() as block:
                @block.sync
                def _(sp):
                    for n in names:
                        sp.dma_start(keep[n][:], d[n]).then_inc(sem, 16)
                    sp.wait_ge(sem, 16 * len(names))

        def loaded(names_shapes, stack):
            for n, shape in names_shapes.items():
                keep[n] = stack.enter_context(nc.sbuf_tensor(n, shape, F32))
            return list(names_shapes)

        keep = {}
        loaded(dict(ident=[P, P], anti=[P, 2 * P], eps6=[P, 1], eps5=[P, 1], still=[P, GROUP + 1]), ctx)
        loaded(dict(v_tok=[P, TILES, H], d_tok=[P, TILES, H], fs_tok=[P, TILES, H]), ctx)
        with ExitStack() as own:
            names = loaded(dict(wqkv=[H, 3, H], wb=[H, NH], cw=[H, 3, CONV], fsw=[H, FS], blk=[P, P], causal=[P, P]), own)
            load_all(["ident", "anti", "eps6", "eps5"] + names, own.enter_context(nc.semaphore("first_in")))
            delta_phase(nc, d, keep)
        names = loaded(dict(fl_tok=[P, TILES, H], bias=[P, H], cbT=[H, H], wqkvT=[H, 3 * HA * DH], woT=[P, HA // 2, H], rope=[P, 2, T4, 2, DH]), ctx)[1:]
        for n in ("identb", "maskb"):
            keep[n] = ctx.enter_context(nc.sbuf_tensor(n, [P, P], BF16))
        with ExitStack() as own:
            names += loaded(dict(x_all=[P, TILES, H], b1=[P, 2], b2=[P, 16], w1x=[H, MH], w1s=[32, MH], w2=[P, 2, 16], wo_a=[H, H],
                                 scb=[P, H], onorm=[H, 1], rtemp=[P, 16], mask=[P, P], nw=[P, 2, 2, DH]), own)
            fir_phase(nc, d, keep, names)
            tables(nc, keep, own)
            gate_phase(nc, d, keep)
        attention_phase(nc, keep)
        last_phase(nc, dict(out=out), keep)


def tables(nc, K, ctx):
    g = K["rtemp"]
    t = ctx.enter_context(nc.sbuf_tensor("soft", [P, 3, 16], F32))
    step = ctx.enter_context(nc.semaphore("table_step"))
    expd = ctx.enter_context(nc.semaphore("table_exp"))
    with nc.Block() as block:
        @block.scalar
        def _(act):
            act.wait_ge(step, 2)
            nc.scalar.activation(t[:, 1], t[:, 0], ACT.Exp, scale=-1.0).then_inc(expd, 1)
            act.wait_ge(step, 3)
            nc.scalar.activation(t[:, 2], t[:, 1], ACT.Ln).then_inc(expd, 1)

        @block.vector
        def _(dve):
            n = [0]

            def chain(ins):
                n[0] += 1
                ins.then_inc(step, 1)
                dve.wait_ge(step, n[0])

            chain(nc.vector.tensor_scalar(t[:, 0], g[:], -1.0, None, ALU.mult))
            chain(nc.vector.tensor_tensor(t[:, 0], t[:, 0], g[:], ALU.max))
            dve.wait_ge(expd, 1)
            chain(nc.vector.tensor_scalar(t[:, 1], t[:, 1], 1.0, None, ALU.add))
            dve.wait_ge(expd, 2)
            chain(nc.vector.scalar_tensor_tensor(g[:], g[:], 0.0, t[:, 2], ALU.max, ALU.add))
            chain(nc.vector.tensor_scalar(g[:], g[:], 1e-4, None, ALU.add))
            chain(nc.vector.reciprocal(g[:], g[:]))
            chain(nc.vector.tensor_tensor(K["w2"][:], K["w2"][:], g[:].unsqueeze(1).broadcast_to([P, 2, 16]), ALU.mult))
            chain(nc.vector.tensor_tensor(K["b2"][:], K["b2"][:], g[:], ALU.mult))
            chain(nc.vector.tensor_scalar(K["scb"][:], K["scb"][:], 1.0 / 127.0, None, ALU.mult))
            chain(nc.vector.tensor_tensor(K["cbT"][:], K["cbT"][:], K["scb"][:], ALU.mult))
            chain(nc.vector.tensor_scalar(K["wo_a"][:], K["wo_a"][:], K["onorm"][:, 0:1], None, ALU.mult))
            for w in range(2):
                chain(nc.vector.tensor_tensor(K["rope"][:, w], K["rope"][:, w], K["nw"][:, w].unsqueeze(1).broadcast_to([P, T4, 2, DH]), ALU.mult))
            q_table = K["rope"][:, 1].rearrange("p t w c -> p (t w c)")
            chain(nc.vector.tensor_scalar(q_table, q_table, DH ** -0.5, None, ALU.mult))
            chain(nc.vector.tensor_copy(K["identb"][:], K["ident"][:]))
            chain(nc.vector.tensor_copy(K["maskb"][:], K["mask"][:]))


def layouts(a):
    q, b = "L0_attn_a_", "L0_attn_b_"
    a = {k: np.asarray(v, np.float32) for k, v in a.items()}
    k = np.arange(P)
    same = k[:, None] // CH == k[None, :] // CH
    f = np.float32
    angles = np.arange(L, dtype=f)[:, None] * (f(1.0) / f(10000.0) ** (np.arange(0, DH, 2, dtype=f) / f(DH)))
    cos, sin = np.cos(angles).astype(f), np.sin(angles).astype(f)
    turn = np.stack([np.concatenate([cos, cos], 1), np.concatenate([-sin, sin], 1)], 1)
    turn = turn.reshape(T4, P, 2, DH).transpose(1, 0, 2, 3)
    wide = lambda v, *s: np.ascontiguousarray(np.broadcast_to(v, (P, *s)))
    nws = [a[b + "k_norm_w"], a[b + "q_norm_w"]]
    nw = np.stack([np.stack([w, np.concatenate([w[32:], w[:32]])]) for w in nws])
    z = np.zeros((H, P + P // 2), f)
    z[:, FL:2 * FL] = a[q + "fir_long_w"].reshape(H, FL)[:, ::-1]
    return dict(
        x=a[q + "hidden_states"].reshape(B * L, H),
        wqkv=np.stack([a[q + "Wq"], a[q + "Wk"], a[q + "Wv"]], 1), wb=a[q + "Wb"],
        cw=np.stack([a[q + f"conv_{n}_w"] for n in "qkv"], 1), fsw=a[q + "fir_short_w"].reshape(H, FS),
        ident=np.eye(P, dtype=f), anti=(k[:, None] + np.arange(2 * P)[None, :] == P + P // 2 - 1).astype(f), blk=same.astype(f), causal=(same & (k[:, None] <= k[None, :])).astype(f),
        eps6=np.full((P, 1), 1e-6, f), eps5=np.full((P, 1), 1e-5, f), fir_z=z,
        b1=a[q + "mlp_b1"].reshape(2, P).T.copy(), b2=wide(a[q + "mlp_b2"], 16),
        w1x=a[q + "mlp_w1"][:H],
        w1s=a[q + "mlp_w1"][H:].reshape(4, 2, NH, MH).transpose(1, 0, 2, 3).reshape(32, MH).copy(), w2=a[q + "mlp_w2"].reshape(2, P, 16).transpose(1, 0, 2).copy(),
        wo_a=a[q + "Wo"], cbT=a["L0_ffn_CB"].T.copy(), scb=wide(a["L0_ffn_SCB"], H), bias=wide(a["L0_ffn_bias"], H),
        onorm=np.tile(a[q + "o_norm_w"], NH)[:, None].copy(), rtemp=wide(np.repeat(a[q + "gate_log_temp"], 4), 16),
        wqkvT=a[b + "wqkv"].T.copy(), woT=a[b + "wo"].T.reshape(HA // 2, P, H).transpose(1, 0, 2).copy(),
        rope=np.ascontiguousarray(np.broadcast_to(turn[:, None], (P, 2, T4, 2, DH))), nw=wide(nw, 2, 2, DH),
        mask=np.where(k[:, None] >= k[None, :], f(0), f(-1e30)).astype(f),
    )


def kernel(**inputs):
    import concourse.bacc as bacc
    from concourse.bass_utils import run_bass_kernel_spmd

    nc = bacc.Bacc("TRN2", target_bir_lowering=False, num_devices=1)
    arrays = {f"in_{n}": v for n, v in layouts(inputs).items()}
    d = {n[3:]: nc.dram_tensor(n, v.shape, mybir.dt.from_np(v.dtype), kind="ExternalInput").ap() for n, v in arrays.items()}
    out = nc.dram_tensor("out_x", (B * L, H), F32, kind="ExternalOutput").ap()
    d["x"] = d["x"].rearrange("(n p) c -> p n c", p=P)
    d["x_all"] = d["x"]
    build_kernel(nc, d, out.rearrange("(n p) c -> p n c", p=P))
    r = run_bass_kernel_spmd(nc, [arrays], core_ids=[0])
    return r.results[0]["out_x"].reshape(B, L, H)
```
